# Optimizing a Trainium2 kernel written in Bass

```python
import numpy as np
import jax
import jax.numpy as jnp

def _softmax(x, axis=-1):
    return jax.nn.softmax(x, axis=axis)

def _gelu(x):
    return jax.nn.gelu(x, approximate=True)

def _silu(x):
    return jax.nn.silu(x)

def _sigmoid(x):
    return jax.nn.sigmoid(x)

def _layernorm(x, axis=-1, eps=1e-05):
    m = jnp.mean(x, axis=axis, keepdims=True)
    v = jnp.var(x, axis=axis, keepdims=True)
    return (x - m) / jnp.sqrt(v + eps)

def _scatter_add(tgt, idx, src, axis=0):
    return tgt.at[idx].add(src)

def _segment_sum(src, seg, n):
    return jax.ops.segment_sum(src, seg, n)
kernel_name = 'mk_sandwich_d1_jaxref_r8_dbde1c'

def setup_inputs(seed: int=0):
    np.random.seed(seed)
    _w = jnp.asarray

    def _L0_attn_setup():
        import jax, jax.numpy as jnp
        import numpy as np
        D = 128
        DI = 256
        HS = 16
        PS = DI // HS
        NS = 64
        KC = 4
        CHUNK = 64
        HA = 16
        HKV = 4
        PA = D // HA
        MLP_MULT = 4
        ROPE_BASE = 10000.0
        B_SZ = 2
        L_SEQ = 256

        def rms_norm(x):
            eps = jnp.asarray(jnp.finfo(x.dtype).eps, x.dtype)
            return x * jax.lax.rsqrt(jnp.mean(jnp.square(x), axis=-1, keepdims=True) + eps)

        def silu(x):
            return x * jax.nn.sigmoid(x)

        def apply_rope(x, cos, sin):
            half = x.shape[-1] // 2
            x1, x2 = (x[..., :half], x[..., half:])
            return jnp.concatenate([x1 * cos + x2 * sin, -x1 * sin + x2 * cos], axis=-1)

        def selective_scan(x, A, Bm, Cm, dt, chunk):
            Bb, L, H, P = x.shape
            N = Bm.shape[-1]
            decay = jnp.exp(A * dt)
            nc = L // chunk
            xp = x.reshape(Bb, nc, chunk, H, P).transpose(0, 1, 3, 2, 4)
            Bp = Bm.reshape(Bb, nc, chunk, H, N).transpose(0, 1, 3, 2, 4)
            Cp = Cm.reshape(Bb, nc, chunk, H, N).transpose(0, 1, 3, 2, 4)
            x_dt = xp * dt[None, None, :, None, None]
            idx = jnp.arange(chunk)
            diff = idx[:, None] - idx[None, :]
            Lm = jnp.where(diff >= 0, decay[:, None, None] ** jnp.maximum(diff, 0), 0.0)
            CB = jnp.einsum('bchqn,bchkn->bchqk', Cp, Bp)
            y_diag = jnp.einsum('bchqk,bchkp->bchqp', CB * Lm[None, None], x_dt)
            decay_rev = decay[:, None] ** (chunk - 1 - idx)[None, :]
            states = jnp.einsum('bchtn,bchtp->bchnp', Bp * decay_rev[None, None, :, :, None], x_dt)
            ci = jnp.arange(nc)
            shift = ci[:, None] - ci[None, :] - 1
            cdec = decay ** chunk
            M = jnp.where(shift >= 0, cdec[:, None, None] ** jnp.maximum(shift, 0), 0.0)
            h_carry = jnp.einsum('hij,bjhnp->bihnp', M, states)
            decay_out = decay[:, None] ** (idx + 1)[None, :]
            y_off = jnp.einsum('bchtn,bchnp->bchtp', Cp, h_carry) * decay_out[None, None, :, :, None]
            y = (y_diag + y_off).transpose(0, 1, 3, 2, 4).reshape(Bb, L, H, P)
            return y

        def mlp(n, fc_w, proj_w):
            h = jax.nn.relu(n @ fc_w)
            return jnp.square(h) @ proj_w
        key = jax.random.key(seed)
        ks = jax.random.split(key, 24)
        w = lambda k, shp, s=0.02: jax.random.normal(k, shp, jnp.float32) * s
        dt_init = jax.random.uniform(ks[0], (HS,), jnp.float32, 0.001, 0.1)
        dt_bias = dt_init + jnp.log(-jnp.expm1(-dt_init))
        return {'x': jax.random.normal(ks[1], (B_SZ, L_SEQ, D), jnp.float32), 'in_proj_w': w(ks[2], (D, 2 * DI)), 'conv_w': w(ks[3], (DI, KC), 0.2), 'conv_b': jnp.zeros((DI,), jnp.float32), 'B_proj_w': w(ks[4], (D, HS * NS)), 'C_proj_w': w(ks[5], (D, HS * NS)), 'dt_bias': dt_bias, 'A_log': jnp.log(jnp.arange(1, HS + 1, dtype=jnp.float32)), 'D_param': jnp.ones((HS,), jnp.float32), 'out_proj_w': w(ks[6], (DI, D)), 'resid_mix_m': jnp.stack([jnp.ones(D), jnp.zeros(D)]).astype(jnp.float32), 'mamba_scale': jnp.ones((D,), jnp.float32), 'm_fc_w': w(ks[7], (D, MLP_MULT * D)), 'm_proj_w': w(ks[8], (MLP_MULT * D, D)), 'm_mlp_scale': jnp.ones((D,), jnp.float32), 'resid_mix_a': jnp.stack([jnp.ones(D), jnp.zeros(D)]).astype(jnp.float32), 'q_w': w(ks[9], (D, D)), 'k_w': w(ks[10], (D, HKV * PA)), 'v_w': w(ks[11], (D, HKV * PA)), 'o_w': w(ks[12], (D, D)), 'q_gain': jnp.full((HA,), 1.0, jnp.float32), 'attn_scale': jnp.ones((D,), jnp.float32), 'a_fc_w': w(ks[13], (D, MLP_MULT * D)), 'a_proj_w': w(ks[14], (MLP_MULT * D, D)), 'a_mlp_scale': jnp.ones((D,), jnp.float32)}
    _L0_attn_in = _L0_attn_setup()

    def _L0_ffn_setup():
        import jax, jax.numpy as jnp
        import numpy as np
        D_IN, D_HID = (128, 512)

        def _ternary(key, shape):
            return jax.random.randint(key, shape, -1, 2).astype(jnp.float32)

        def _tlin(x, w, s):
            return jnp.einsum('bsi,oi->bso', x, w) * s
        key = jax.random.key(seed)
        ks = jax.random.split(key, 12)
        inv = lambda fan: 1.0 / np.sqrt(fan).astype(np.float32)
        return {'x': jax.random.normal(ks[0], (4, 256, D_IN), dtype=jnp.float32), 'w1_w': _ternary(ks[1], (D_HID, D_IN)), 'w1_s': jax.random.uniform(ks[2], (D_HID,), dtype=jnp.float32) * inv(D_IN), 'w2_w': _ternary(ks[3], (D_HID, D_IN)), 'w2_s': jax.random.uniform(ks[4], (D_HID,), dtype=jnp.float32) * inv(D_IN), 'h1_w': _ternary(ks[5], (D_HID, D_HID)), 'h1_s': jax.random.uniform(ks[6], (D_HID,), dtype=jnp.float32) * inv(D_HID), 'h2_w': _ternary(ks[7], (D_HID, D_HID)), 'h2_s': jax.random.uniform(ks[8], (D_HID,), dtype=jnp.float32) * inv(D_HID), 'w3_w': _ternary(ks[9], (D_IN, D_HID)), 'w3_s': jax.random.uniform(ks[10], (D_IN,), dtype=jnp.float32) * inv(D_HID)}
    _L0_ffn_in = _L0_ffn_setup()
    _d = {'L0_attn_x': _L0_attn_in['x'], 'L0_attn_in_proj_w': _L0_attn_in['in_proj_w'], 'L0_attn_conv_w': _L0_attn_in['conv_w'], 'L0_attn_conv_b': _L0_attn_in['conv_b'], 'L0_attn_B_proj_w': _L0_attn_in['B_proj_w'], 'L0_attn_C_proj_w': _L0_attn_in['C_proj_w'], 'L0_attn_dt_bias': _L0_attn_in['dt_bias'], 'L0_attn_A_log': _L0_attn_in['A_log'], 'L0_attn_D_param': _L0_attn_in['D_param'], 'L0_attn_out_proj_w': _L0_attn_in['out_proj_w'], 'L0_attn_resid_mix_m': _L0_attn_in['resid_mix_m'], 'L0_attn_mamba_scale': _L0_attn_in['mamba_scale'], 'L0_attn_m_fc_w': _L0_attn_in['m_fc_w'], 'L0_attn_m_proj_w': _L0_attn_in['m_proj_w'], 'L0_attn_m_mlp_scale': _L0_attn_in['m_mlp_scale'], 'L0_attn_resid_mix_a': _L0_attn_in['resid_mix_a'], 'L0_attn_q_w': _L0_attn_in['q_w'], 'L0_attn_k_w': _L0_attn_in['k_w'], 'L0_attn_v_w': _L0_attn_in['v_w'], 'L0_attn_o_w': _L0_attn_in['o_w'], 'L0_attn_q_gain': _L0_attn_in['q_gain'], 'L0_attn_attn_scale': _L0_attn_in['attn_scale'], 'L0_attn_a_fc_w': _L0_attn_in['a_fc_w'], 'L0_attn_a_proj_w': _L0_attn_in['a_proj_w'], 'L0_attn_a_mlp_scale': _L0_attn_in['a_mlp_scale'], 'L0_ffn_w1_w': _L0_ffn_in['w1_w'], 'L0_ffn_w1_s': _L0_ffn_in['w1_s'], 'L0_ffn_w2_w': _L0_ffn_in['w2_w'], 'L0_ffn_w2_s': _L0_ffn_in['w2_s'], 'L0_ffn_h1_w': _L0_ffn_in['h1_w'], 'L0_ffn_h1_s': _L0_ffn_in['h1_s'], 'L0_ffn_h2_w': _L0_ffn_in['h2_w'], 'L0_ffn_h2_s': _L0_ffn_in['h2_s'], 'L0_ffn_w3_w': _L0_ffn_in['w3_w'], 'L0_ffn_w3_s': _L0_ffn_in['w3_s']}
    _x0 = _d['L0_attn_x']
    _d['L0_attn_x'] = jax.random.normal(jax.random.fold_in(jax.random.key(seed), 1), (16, 256, 128), dtype=_x0.dtype)
    del _x0
    return _d

def reference(L0_attn_x, L0_attn_in_proj_w, L0_attn_conv_w, L0_attn_conv_b, L0_attn_B_proj_w, L0_attn_C_proj_w, L0_attn_dt_bias, L0_attn_A_log, L0_attn_D_param, L0_attn_out_proj_w, L0_attn_resid_mix_m, L0_attn_mamba_scale, L0_attn_m_fc_w, L0_attn_m_proj_w, L0_attn_m_mlp_scale, L0_attn_resid_mix_a, L0_attn_q_w, L0_attn_k_w, L0_attn_v_w, L0_attn_o_w, L0_attn_q_gain, L0_attn_attn_scale, L0_attn_a_fc_w, L0_attn_a_proj_w, L0_attn_a_mlp_scale, L0_ffn_w1_w, L0_ffn_w1_s, L0_ffn_w2_w, L0_ffn_w2_s, L0_ffn_h1_w, L0_ffn_h1_s, L0_ffn_h2_w, L0_ffn_h2_s, L0_ffn_w3_w, L0_ffn_w3_s):

    def _L0_attn_ref(x, in_proj_w, conv_w, conv_b, B_proj_w, C_proj_w, dt_bias, A_log, D_param, out_proj_w, resid_mix_m, mamba_scale, m_fc_w, m_proj_w, m_mlp_scale, resid_mix_a, q_w, k_w, v_w, o_w, q_gain, attn_scale, a_fc_w, a_proj_w, a_mlp_scale):
        import jax, jax.numpy as jnp
        import numpy as np
        D = 128
        DI = 256
        HS = 16
        PS = DI // HS
        NS = 64
        KC = 4
        CHUNK = 64
        HA = 16
        HKV = 4
        PA = D // HA
        MLP_MULT = 4
        ROPE_BASE = 10000.0
        B_SZ = 2
        L_SEQ = 256

        def rms_norm(x):
            eps = jnp.asarray(jnp.finfo(x.dtype).eps, x.dtype)
            return x * jax.lax.rsqrt(jnp.mean(jnp.square(x), axis=-1, keepdims=True) + eps)

        def silu(x):
            return x * jax.nn.sigmoid(x)

        def apply_rope(x, cos, sin):
            half = x.shape[-1] // 2
            x1, x2 = (x[..., :half], x[..., half:])
            return jnp.concatenate([x1 * cos + x2 * sin, -x1 * sin + x2 * cos], axis=-1)

        def selective_scan(x, A, Bm, Cm, dt, chunk):
            Bb, L, H, P = x.shape
            N = Bm.shape[-1]
            decay = jnp.exp(A * dt)
            nc = L // chunk
            xp = x.reshape(Bb, nc, chunk, H, P).transpose(0, 1, 3, 2, 4)
            Bp = Bm.reshape(Bb, nc, chunk, H, N).transpose(0, 1, 3, 2, 4)
            Cp = Cm.reshape(Bb, nc, chunk, H, N).transpose(0, 1, 3, 2, 4)
            x_dt = xp * dt[None, None, :, None, None]
            idx = jnp.arange(chunk)
            diff = idx[:, None] - idx[None, :]
            Lm = jnp.where(diff >= 0, decay[:, None, None] ** jnp.maximum(diff, 0), 0.0)
            CB = jnp.einsum('bchqn,bchkn->bchqk', Cp, Bp)
            y_diag = jnp.einsum('bchqk,bchkp->bchqp', CB * Lm[None, None], x_dt)
            decay_rev = decay[:, None] ** (chunk - 1 - idx)[None, :]
            states = jnp.einsum('bchtn,bchtp->bchnp', Bp * decay_rev[None, None, :, :, None], x_dt)
            ci = jnp.arange(nc)
            shift = ci[:, None] - ci[None, :] - 1
            cdec = decay ** chunk
            M = jnp.where(shift >= 0, cdec[:, None, None] ** jnp.maximum(shift, 0), 0.0)
            h_carry = jnp.einsum('hij,bjhnp->bihnp', M, states)
            decay_out = decay[:, None] ** (idx + 1)[None, :]
            y_off = jnp.einsum('bchtn,bchnp->bchtp', Cp, h_carry) * decay_out[None, None, :, :, None]
            y = (y_diag + y_off).transpose(0, 1, 3, 2, 4).reshape(Bb, L, H, P)
            return y

        def mlp(n, fc_w, proj_w):
            h = jax.nn.relu(n @ fc_w)
            return jnp.square(h) @ proj_w
        Bb, L, _ = x.shape
        x0 = x
        xm = resid_mix_m[0][None, None] * x + resid_mix_m[1][None, None] * x0
        n = rms_norm(xm)
        vg = n @ in_proj_w
        value, gate = (vg[..., :DI], vg[..., DI:])
        v_t = value.transpose(0, 2, 1)
        v_conv = jax.lax.conv_general_dilated(v_t, conv_w[:, None, :], (1,), [(KC - 1, 0)], feature_group_count=DI, dimension_numbers=('NCH', 'OIH', 'NCH')) + conv_b[None, :, None]
        value = silu(v_conv).transpose(0, 2, 1).reshape(Bb, L, HS, PS)
        Bm = (xm @ B_proj_w).reshape(Bb, L, HS, NS)
        Cm = (xm @ C_proj_w).reshape(Bb, L, HS, NS)
        dt = jax.nn.softplus(dt_bias)
        A = -jnp.exp(A_log)
        y = selective_scan(value, A, Bm, Cm, dt, CHUNK)
        y = y + D_param[None, None, :, None] * value
        y = y.reshape(Bb, L, DI) * silu(gate) @ out_proj_w
        xm = xm + mamba_scale[None, None] * y
        xm = xm + m_mlp_scale[None, None] * mlp(rms_norm(xm), m_fc_w, m_proj_w)
        xa = resid_mix_a[0][None, None] * xm + resid_mix_a[1][None, None] * x0
        n = rms_norm(xa)
        q = (n @ q_w).reshape(Bb, L, HA, PA).transpose(0, 2, 1, 3)
        k = (n @ k_w).reshape(Bb, L, HKV, PA).transpose(0, 2, 1, 3)
        v = (n @ v_w).reshape(Bb, L, HKV, PA).transpose(0, 2, 1, 3)
        q = rms_norm(q)
        k = rms_norm(k)
        inv_freq = 1.0 / ROPE_BASE ** (jnp.arange(0, PA, 2, dtype=jnp.float32) / PA)
        f = jnp.outer(jnp.arange(L, dtype=jnp.float32), inv_freq)
        cos, sin = (jnp.cos(f)[None, None], jnp.sin(f)[None, None])
        q = apply_rope(q, cos, sin) * q_gain[None, :, None, None]
        k = apply_rope(k, cos, sin)
        G = HA // HKV
        k = jnp.repeat(k, G, axis=1)
        v = jnp.repeat(v, G, axis=1)
        s = jnp.einsum('bhqd,bhkd->bhqk', q, k) / np.float32(np.sqrt(PA))
        mask = jnp.tril(jnp.ones((L, L), bool))
        s = jnp.where(mask[None, None], s, jnp.asarray(-jnp.inf, s.dtype))
        att = jax.nn.softmax(s, axis=-1)
        y = jnp.einsum('bhqk,bhkd->bhqd', att, v).transpose(0, 2, 1, 3).reshape(Bb, L, D)
        xa = xa + attn_scale[None, None] * (y @ o_w)
        xa = xa + a_mlp_scale[None, None] * mlp(rms_norm(xa), a_fc_w, a_proj_w)
        return xa

    def _L0_ffn_ref(x, w1_w, w1_s, w2_w, w2_s, h1_w, h1_s, h2_w, h2_s, w3_w, w3_s):
        import jax, jax.numpy as jnp
        import numpy as np
        D_IN, D_HID = (128, 512)

        def _ternary(key, shape):
            return jax.random.randint(key, shape, -1, 2).astype(jnp.float32)

        def _tlin(x, w, s):
            return jnp.einsum('bsi,oi->bso', x, w) * s
        h = jax.nn.silu(_tlin(x, w1_w, w1_s)) * _tlin(x, w2_w, w2_s)
        h = jax.nn.gelu(_tlin(h, h1_w, h1_s), approximate=False)
        h = jax.nn.gelu(_tlin(h, h2_w, h2_s), approximate=False)
        return _tlin(h, w3_w, w3_s)
    x = L0_attn_x
    x = x + _layernorm(_L0_attn_ref(_layernorm(x, axis=-1), L0_attn_in_proj_w, L0_attn_conv_w, L0_attn_conv_b, L0_attn_B_proj_w, L0_attn_C_proj_w, L0_attn_dt_bias, L0_attn_A_log, L0_attn_D_param, L0_attn_out_proj_w, L0_attn_resid_mix_m, L0_attn_mamba_scale, L0_attn_m_fc_w, L0_attn_m_proj_w, L0_attn_m_mlp_scale, L0_attn_resid_mix_a, L0_attn_q_w, L0_attn_k_w, L0_attn_v_w, L0_attn_o_w, L0_attn_q_gain, L0_attn_attn_scale, L0_attn_a_fc_w, L0_attn_a_proj_w, L0_attn_a_mlp_scale), axis=-1)
    x = x + _layernorm(_L0_ffn_ref(_layernorm(x, axis=-1), L0_ffn_w1_w, L0_ffn_w1_s, L0_ffn_w2_w, L0_ffn_w2_s, L0_ffn_h1_w, L0_ffn_h1_s, L0_ffn_h2_w, L0_ffn_h2_s, L0_ffn_w3_w, L0_ffn_w3_s), axis=-1)
    return x

_drawn_inputs = setup_inputs


def setup_inputs(seed=0):
    import zlib

    import numpy as np

    out = dict(_drawn_inputs(seed))
    spreads = {'L0_attn_conv_b': (0.0, 0.8),
     'L0_attn_D_param': (1.0, 0.6),
     'L0_attn_mamba_scale': (1.0, 0.6),
     'L0_attn_m_mlp_scale': (1.0, 0.6),
     'L0_attn_q_gain': (1.0, 0.6),
     'L0_attn_attn_scale': (1.0, 0.6),
     'L0_attn_a_mlp_scale': (1.0, 0.6)}
    factors = {'L0_attn_in_proj_w': 8.0,
     'L0_attn_conv_w': 8.0,
     'L0_attn_B_proj_w': 8.0,
     'L0_attn_C_proj_w': 8.0,
     'L0_attn_dt_bias': 8.0,
     'L0_attn_A_log': 8.0,
     'L0_attn_out_proj_w': 8.0,
     'L0_attn_m_fc_w': 4.085,
     'L0_attn_m_proj_w': 3.658,
     'L0_attn_resid_mix_a': 6.298,
     'L0_attn_q_w': 8.0,
     'L0_attn_k_w': 8.0,
     'L0_attn_v_w': 8.0,
     'L0_attn_o_w': 8.0,
     'L0_attn_a_fc_w': 3.895,
     'L0_attn_a_proj_w': 3.614}
    for name, (base, spread) in spreads.items():
        noise = np.random.default_rng([zlib.crc32(name.encode()), seed]).standard_normal(out[name].shape)
        drawn = base * np.exp(spread * noise) if base else spread * noise
        out[name] = jnp.asarray(drawn.astype(out[name].dtype))
    for name, factor in factors.items():
        out[name] = (out[name] * factor).astype(out[name].dtype)
    return out
```

```python
from contextlib import ExitStack

import numpy as np
import concourse.bass as bass
from concourse import mybir

F32, F32R, BF16, I32 = mybir.dt.float32, mybir.dt.float32r, mybir.dt.bfloat16, mybir.dt.int32
ACT = mybir.ActivationFunctionType
ALU = mybir.AluOpType
AX = mybir.AxisListType

P = 128
BATCH, L, D = 16, 256, 128
DI, HS, NS, KC = 256, 16, 64, 4
PS = DI // HS
HA, HKV, PA = 16, 4, 8
G = HA // HKV
HID = 512
PAIRS = BATCH // 2
TOK = 2 * L
TILES = TOK // P
NBLK = HID // P
UNITS = 2 * HS
TRI = L + P
QK = HA + HKV
QKV = (HA + 2 * HKV) * PA
EPS_LN = 1e-5
EPS_RMS = float(np.finfo(np.float32).eps)

PER = dict(
    x_in=16, bn_f=1, aggr_f=4, rs_f_eps=3, rs_f=3, nrm_f=3, xm=1, ssq_f=8, conv=8, val=2, cb_full=32, masked=32,
    y_mm=32, yacc_free=3, yg=2, hid_f=4, mlp_f=1, mix=2, fr_full=30, fr_evac0=15, fr_evac1=15,
    xa=1, x_res=16, rs_b_eps=5, rs_b=5, nrm_b=5, ssq_b=8, sq=2, newton=14, rope=2, split=2, mrow=4, pv=32, rden=2,
    b6_full=1, b6_free=2, b7_full=3, b7_free=3, hid_b=4, bn_b=3, aggr_b=12, x1=1, bk_full=98, bk_evac0=49,
    bk_evac1=49, out_ready=1, stored=16)

PROJECT = [("norm_in", 0), ("in_turn", 0), ("gates", 0), ("val_turn", 0)]
MIXER = [("scan", u) for u in range(UNITS + 1)] + [("m_out", 0), ("n2_turn", 0), ("up", 0), ("down", 0)]


def _body():
    at, out = [0], []

    def scans(n):
        out.extend(("scan", 1, u) for u in range(at[0], at[0] + n))
        at[0] += n

    def step(name, ahead=0, k=0):
        out.append((name, ahead, k))

    step("norm_a")
    scans(2)
    step("qkv")
    scans(2)
    step("rope")
    scans(4)
    step("qk_turn")
    for u in range(UNITS):
        step("score", 0, u)
        if u % 4 == 3:
            scans(1)
    for u in range(UNITS + 1):
        step("attend", 0, u)
        if u % 4 == 3:
            scans(1)
    scans(1)
    step("y_turn")
    scans(1)
    step("o_proj")
    scans(2)
    step("n4_turn")
    step("up_b")
    scans(1)
    step("down_b")
    scans(4)
    step("x2_turn")
    step("gated", 0, 0)
    step("gated", 0, 1)
    step("m_out", 1)
    step("gated", 0, 2)
    step("gated", 0, 3)
    step("n2_turn", 1)
    step("hidden1", 0, 0)
    step("up", 1)
    step("hidden1", 0, 1)
    step("hidden1", 0, 2)
    step("down", 1)
    step("hidden1", 0, 3)
    step("norm_in", 2)
    step("hidden2", 0, 0)
    step("in_turn", 2)
    step("hidden2", 0, 1)
    step("gates", 2)
    step("hidden2", 0, 2)
    step("hidden2", 0, 3)
    step("val_turn", 2)
    step("ffn_out")
    assert at[0] == UNITS + 1
    return out


BODY = _body()


def program(nc, t, out):
    ctx = ExitStack()

    def sb(name, shape, dt=F32):
        return ctx.enter_context(nc.sbuf_tensor(name, shape, dt))

    def sem(name):
        return ctx.enter_context(nc.semaphore(name))

    S = {name: sem(name) for name in PER}

    def at(i, name, c):
        return i * PER[name] + c + 1

    ident = sb("ident", [P, P])
    ident_bf = sb("ident_bf", [P, P], BF16)
    sl = sb("sl", [P, 2, TOK])
    diff, causal = sl[:, 0, 0:TRI], sl[:, 1, 0:TRI]
    sq = sb("sq", [P, TILES, QK, PA])
    mask_f = sq[:].rearrange("p t h c -> p (t h c)")[:, 0:4 * P].rearrange("p (a b c) -> p a b c", a=2, b=2)
    mask_bf = sb("mask_bf", [P, 2, 2, P], BF16)
    cosT = sb("cosT", [P, 2, QK, PA])
    sinT = sb("sinT", [P, 2, QK, PA])
    w_in = sb("w_in", [P, 2 * DI])
    w_B = sb("w_B", [P, HS * NS])
    w_C = sb("w_C", [P, HS * NS])
    w_out = sb("w_out", [P, 2, D])
    w_mfc = sb("w_mfc", [P, HID])
    w_mpj = sb("w_mpj", [P, NBLK, D])
    w_qkv = sb("w_qkv", [P, QKV])
    w_o = sb("w_o", [P, D])
    w_afc = sb("w_afc", [P, HID])
    w_apj = sb("w_apj", [P, NBLK, D])
    w_1 = sb("w_1", [P, HID])
    w_2 = sb("w_2", [P, HID])
    w_h1 = sb("w_h1", [P, NBLK, HID])
    w_h2 = sb("w_h2", [P, NBLK, HID])
    w_3 = sb("w_3", [P, NBLK, D])
    rows = sb("rows", [P, 9, D])
    R_M0, R_M1, R_A0, R_A1, R_MS, R_MM, R_AS, R_AM, R_W3 = range(9)
    cols = sb("cols", [P, 40])
    C_CW, C_CB, C_D, C_W1, C_W2, C_H1, C_H2 = 0, 8, 10, 12, 16, 20, 24
    heads = sb("heads", [P, 3, HS])
    gain = sb("gain", [P, TILES * QK])
    LM = sb("LM", [P, HS, TRI])
    half = sb("half", [P, TILES])
    eps_ln = sb("eps_ln", [P, TILES])
    eps_rms = sb("eps_rms", [P, TILES])
    waited = sb("waited", [P, 1])
    sc = sb("sc", [P, 12, HS])

    x_in = sb("x_in", [P, TILES, D])
    stat = sb("stat", [P, TILES, 6])
    mv = sb("mv", [P, TILES, 2])
    ms = sb("ms", [P, TILES])
    rs = sb("rs", [P, TILES])
    ss_f = sb("ss_f", [P, TILES])
    junk_a = sb("junk_a", [P, D])
    xh = sb("xh", [P, TILES, D])
    xm = sb("xm", [P, TILES, D])
    nrm = sb("nrm", [P, TILES, D])
    xmT = sb("xmT", [P, TOK])
    nT = sb("nT", [P, TOK])
    vpad = sb("vpad", [P, 2, 2, L + KC - 1])
    cv = sb("cv", [P, 2, 2, L])
    val = sb("val", [P, 2, TOK])
    gate = sb("gate", [P, 2, TOK])
    xpad = sb("xpad", [P, TILES, HS, 2 * PS])
    BT = sb("BT", [P, 2, TOK])
    CT = sb("CT", [P, 2, TOK])
    M = sb("M", [P, 2, TRI])
    yg = sb("yg", [P, 2, TOK])
    relu = sb("relu", [P, NBLK, TOK])
    hid = relu
    mix = cv[:, 0, :, :].rearrange("p s (t d) -> p (s t) d", d=D)

    xa = sb("xa", [P, TILES, D])
    x_res = sb("x_res", [P, TILES, D])
    bstat = sb("bstat", [P, TILES, 6])
    bmv = sb("bmv", [P, TILES, 2])
    bms = sb("bms", [P, TILES])
    brs = sb("brs", [P, TILES])
    ss_b = sb("ss_b", [P, TILES])
    x1 = sb("x1", [P, TILES, D])
    junk_b = sb("junk_b", [P, D])
    bn = sb("bn", [P, TILES, D])
    bnT = sb("bnT", [P, TOK])
    qs = sb("qs", [P, 6, TILES * QK])
    qi = sb("qi", [P, TILES * QK], I32)
    yi = sb("yi", [P, TILES * QK], I32)
    qn = sb("qn", [P, TILES, QK, PA])
    ro = sb("ro", [P, TILES, QK, PA])
    r2 = sq
    Qs = sb("Qs", [P, TILES, G, HKV, 32])
    Ks = sb("Ks", [P, TILES, HKV, 32])
    QT = sb("QT", [P, G, TOK], F32R)
    KT = sb("KT", [P, TOK], F32R)
    Va = sb("Va", [P, TILES, HKV, PA + 1])
    mneg = sb("mneg", [P, TILES, HA])
    PT = sb("PT", [P, 2, TRI])
    rden = sb("rden", [P, TILES, HA])
    ytm = sb("ytm", [P, TILES, HA, PA])
    ya = sb("ya", [P, TOK])
    bhid = sb("bhid", [P, NBLK, TOK])
    brelu = bhid
    hC = sb("hC", [P, NBLK, TOK])
    hD = brelu
    out_sb = sb("out_sb", [P, TILES, D])

    bank = [ctx.enter_context(nc.psum_tensor(f"bank{k}", [P, 512], F32)) for k in range(8)]
    FRONT = dict(banks=(0, 1), full="fr_full", evac=("fr_evac0", "fr_evac1"))
    BACK = dict(banks=(4, 5), full="bk_full", evac=("bk_evac0", "bk_evac1"))
    CB, YACC = bank[2], bank[3]
    B6, B7 = bank[6], bank[7]
    PV = [b[:, 0:2 * HA * (PA + 1)].rearrange("p (t h c) -> p t h c", t=2, c=PA + 1) for b in (B6, B7)]
    Q4 = Qs[:].rearrange("p t g j c -> p t (g j) c")

    def ring(r, n):
        return bank[r["banks"][n % 2]]

    def evac(r, n):
        return S[r["evac"][n % 2]]

    def free_at(i, r, n):
        return at(i, r["evac"][n % 2], n // 2)

    def evac_at(i, r, n):
        return at(i, r["evac"][n % 2], n // 2 + 1)

    def full_at(i, r, n):
        return at(i, r["full"], n + 1)

    def K_TURN(k):
        return K_Q2 + (k // 2) * (2 + HA) + k % 2

    def K_EXP(u):
        return K_Q2 + (u // HA) * (2 + HA) + 2 + u % HA

    F_XM, F_N, F_V, F_G, F_XT, F_BC, F_O, F_N2, F_FC = 0, 1, 2, 4, 6, 8, 24, 25, 26
    K_N3, K_QKV, K_Q1, K_K, K_S, K_Q2, K_Y, K_N4, K_FC, K_W, K_H1, K_H2 = (
        0, 1, 3, 7, 8, 40, 76, 77, 78, 82, 90, 94)

    def diag(x, k, b):
        H8 = HS // 2
        whole = x[:, k, b * H8:(b + 1) * H8, :].rearrange("p h c -> p (h c)")
        return bass.AP(whole.tensor, whole.offset, [list(whole.ap[0]), [4 * PS, H8 // 2], [3 * PS, 2], [1, PS]])

    def tri(ap):
        return ap.rearrange("p (a b) -> p a b", b=P)[:, 0:3:2, :]

    weights = [
        (ident, "c_ident"), (w_in, "w_in"), (rows, "rows"), (cols, "cols"), (heads, "heads"),
        (diff, "c_diff"), (causal, "c_causal"), (w_B, "w_B"), (w_C, "w_C"),
        (mask_f, "c_mask"), (w_out, "w_out"), (w_mfc, "w_mfc"), (w_mpj, "w_mpj"), (gain, "gain"), (cosT, "c_cos"),
        (sinT, "c_sin"), (w_qkv, "w_qkv"), (w_o, "w_o"), (w_afc, "w_afc"), (w_apj, "w_apj"),
        (w_1, "w_1"), (w_2, "w_2"), (w_h1, "w_h1"), (w_h2, "w_h2"), (w_3, "w_3")]
    weights_in = sem("weights_in")
    prep_pool, prep_act, prep, prep_dve = sem("prep_pool"), sem("prep_act"), sem("prep"), sem("prep_dve")
    xt_v = t["x"].rearrange("(n p) d -> p n d", p=P)
    ot_v = out.rearrange("(n p) d -> p n d", p=P)
    block = ctx.enter_context(nc.Block())

    @block.sync
    def _(sp):
        def load_x(i):
            sp.wait_ge(S["xm"], at(i, "xm", 0))
            sp.dma_start(x_in[:], xt_v[:, bass.ds(i * TILES, TILES), :]).then_inc(S["x_in"], 16)

        def load_res(i):
            sp.wait_ge(S["x1"], at(i, "x1", 0))
            sp.dma_start(x_res[:], xt_v[:, bass.ds(i * TILES, TILES), :]).then_inc(S["x_res"], 16)

        def store(i):
            sp.wait_ge(S["out_ready"], at(i, "out_ready", 1))
            sp.dma_start(ot_v[:, bass.ds(i * TILES, TILES), :], out_sb[:]).then_inc(S["stored"], 16)

        for name in PER:
            sp.sem_inc(S[name], 1)
        for dst, name in weights:
            if name == "w_in":
                load_x(0)
            sp.dma_start(dst if isinstance(dst, bass.AP) else dst[:], t[name]).then_inc(weights_in, 16)
        load_res(0)
        load_x(1)
        with sp.Fori(0, PAIRS - 2) as i:
            load_x(i + 2)
            load_res(i + 1)
            store(i)
        load_res(PAIRS - 1)
        store(PAIRS - 2)
        store(PAIRS - 1)
        sp.wait_ge(S["stored"], at(PAIRS, "stored", 0))

    def run(parts, order, i):
        for name, ahead, k in order:
            if name in parts:
                parts[name](i + ahead, k)

    def pipeline(eng, parts):
        run(parts, [(n, 1 - 1, k) for n, k in PROJECT], 0)
        run(parts, [(n, 0, k) for n, k in MIXER], 0)
        run(parts, [(n, 0, k) for n, k in PROJECT], 1)
        with eng.Fori(0, PAIRS - 2) as i:
            run(parts, BODY, i)
        run(parts, [x for x in BODY if x[1] < 2], PAIRS - 2)
        run(parts, [x for x in BODY if x[1] < 1], PAIRS - 1)

    @block.gpsimd
    def _(pool):
        g = nc.gpsimd
        g.memset(half[:], -0.5)
        g.memset(eps_ln[:], EPS_LN)
        g.memset(eps_rms[:], D * EPS_RMS)
        g.memset(vpad[:], 0.0)
        g.memset(xpad[:], 0.0)
        g.memset(Qs[:], 0.0)
        g.memset(Ks[:, :, :, 0:24], 0.0)
        g.memset(Ks[:, :, :, 24:26], 1.0)
        g.memset(Ks[:, :, :, 26:32], 0.0)
        g.memset(Va[:], 1.0).then_inc(prep_pool, 1)
        pool.wait_ge(prep_pool, 1)

        def rsqrt(i, c, name, src, dst, tmp, eps, ready, ready_c, used):
            pool.wait_ge(S[ready], at(i, ready, ready_c))
            pool.wait_ge(S[used], at(i, used, c))
            g.tensor_tensor(tmp[:], src, eps[:], ALU.add).then_inc(S[name + "_eps"], 1)
            pool.wait_ge(S[name + "_eps"], at(i, name + "_eps", c + 1))
            g.tensor_tensor(dst[:], tmp[:], half[:], ALU.pow).then_inc(S[name], 1)

        def square_hidden(i, r, n0, h, done):
            for j in range(NBLK):
                pool.wait_ge(evac(r, n0 + j), evac_at(i, r, n0 + j))
                g.tensor_tensor(h[:, j, :], h[:, j, :], h[:, j, :], ALU.mult).then_inc(S[done], 1)

        def norm_in(i, _):
            rsqrt(i, 0, "rs_f", mv[:, :, 1], rs, ms, eps_ln, "aggr_f", TILES, "nrm_f")
            rsqrt(i, 1, "rs_f", ss_f[:], rs, ms, eps_rms, "ssq_f", TILES, "nrm_f")

        def m_out(i, _):
            rsqrt(i, 2, "rs_f", ss_f[:], rs, ms, eps_rms, "ssq_f", 2 * TILES, "nrm_f")

        def up(i, _):
            square_hidden(i, FRONT, F_FC, hid, "hid_f")

        def norm_a(i, _):
            rsqrt(i, 0, "rs_b", ss_b[:], brs, bms, eps_rms, "ssq_b", TILES, "nrm_b")

        def o_proj(i, _):
            rsqrt(i, 1, "rs_b", ss_b[:], brs, bms, eps_rms, "ssq_b", 2 * TILES, "nrm_b")

        def up_b(i, _):
            square_hidden(i, BACK, K_FC, bhid, "hid_b")

        def down_b(i, _):
            rsqrt(i, 2, "rs_b", bmv[:, :, 1], brs, bms, eps_ln, "aggr_b", TILES, "nrm_b")
            rsqrt(i, 3, "rs_b", bmv[:, :, 1], brs, bms, eps_ln, "aggr_b", 2 * TILES, "nrm_b")

        def ffn_out(i, _):
            rsqrt(i, 4, "rs_b", bmv[:, :, 1], brs, bms, eps_ln, "aggr_b", 3 * TILES, "nrm_b")

        pipeline(pool, dict(norm_in=norm_in, m_out=m_out, up=up, norm_a=norm_a, o_proj=o_proj, up_b=up_b,
                            down_b=down_b, ffn_out=ffn_out))

    @block.scalar
    def _(act):
        a = nc.scalar
        act.wait_ge(weights_in, 16 * len(weights))
        act.wait_ge(prep, 1)
        a.activation(sc[:, 1, :], sc[:, 0, :], ACT.Exp).then_inc(prep_act, 1)
        a.activation(sc[:, 2, :], sc[:, 11, :], ACT.Exp).then_inc(prep_act, 1)
        act.wait_ge(prep, 2)
        for h in range(HS):
            a.activation(LM[:, h, :], diff, ACT.Exp, scale=sc[:, 3, h:h + 1]).then_inc(prep_act, 1)

        def squares(i, c, src, dst, junk, done):
            for k in range(TILES):
                a.activation(junk[:], src[:, k, :], ACT.Square, accum_out=dst[:, k:k + 1]).then_inc(S[done], 1)
                act.wait_ge(S[done], at(i, done, TILES * c + k + 1))

        def copy(i, r, n, dst, src=None):
            act.wait_ge(S[r["full"]], full_at(i, r, n))
            a.activation(dst, ring(r, n)[:] if src is None else src, ACT.Copy).then_inc(evac(r, n), 1)

        def norm_in(i, _):
            act.wait_ge(S["xm"], at(i, "xm", 1))
            squares(i, 0, xm, ss_f, junk_a, "ssq_f")

        def in_turn(i, _):
            copy(i, FRONT, F_XM, xmT[:])
            copy(i, FRONT, F_N, nT[:])

        def gates(i, _):
            for b in range(2):
                n = F_V + b
                copy(i, FRONT, n, vpad[:, b, :, KC - 1:], ring(FRONT, n)[:].rearrange("p (s l) -> p s l", s=2))
            for b in range(2):
                n = F_G + b
                act.wait_ge(S["fr_full"], full_at(i, FRONT, n))
                a.activation(gate[:, b, :], ring(FRONT, n)[:], ACT.Silu).then_inc(evac(FRONT, n), 1)
            for b in range(2):
                act.wait_ge(S["conv"], at(i, "conv", KC * (b + 1)))
                a.activation(val[:, b, :], cv[:, b, :, :].rearrange("p s l -> p (s l)"), ACT.Silu).then_inc(S["val"], 1)

        def val_turn(i, _):
            for b in range(2):
                n = F_XT + b
                act.wait_ge(S["fr_full"], full_at(i, FRONT, n))
                for k in range(TILES):
                    src = ring(FRONT, n)[:, k * P:(k + 1) * P].rearrange("p (a b c) -> p a b c", b=2, c=PS)
                    last = a.activation(diag(xpad, k, b), src, ACT.Copy)
                last.then_inc(evac(FRONT, n), 1)

        def scan(i, u):
            if u % 4 == 2 and u // 4 + 1 < HS // 2:
                project_BC(i, u // 4 + 1)
            if u == 0:
                project_BC(i, 0)

        def project_BC(i, hp):
            for k, dst in enumerate((BT, CT)):
                if hp >= 2:
                    act.wait_ge(S["cb_full"], at(i, "cb_full", 4 * (hp - 1)))
                copy(i, FRONT, F_BC + 2 * hp + k, dst[:, hp % 2, :])

        def m_out(i, _):
            act.wait_ge(evac(FRONT, F_O), evac_at(i, FRONT, F_O))
            squares(i, 1, xm, ss_f, junk_a, "ssq_f")

        def n2_turn(i, _):
            copy(i, FRONT, F_N2, nT[:])

        def up(i, _):
            for j in range(NBLK):
                act.wait_ge(S["fr_full"], full_at(i, FRONT, F_FC + j))
                a.activation(relu[:, j, :], ring(FRONT, F_FC + j)[:], ACT.Relu).then_inc(evac(FRONT, F_FC + j), 1)

        def norm_a(i, _):
            act.wait_ge(S["xa"], at(i, "xa", 1))
            squares(i, 0, xa, ss_b, junk_b, "ssq_b")

        def qkv(i, _):
            copy(i, BACK, K_N3, bnT[:])
            for tp in range(2):
                n = K_QKV + tp
                act.wait_ge(S["bk_full"], full_at(i, BACK, n))
                q3 = ring(BACK, n)[:, 0:2 * QKV].rearrange("p (t c) -> p t c", t=2)
                a.activation(sq[:, 2 * tp:2 * tp + 2, :, :].rearrange("p t h c -> p t (h c)"), q3[:, :, 0:QK * PA], ACT.Square)
                vv = q3[:, :, QK * PA:].rearrange("p t (h c) -> p t h c", c=PA)
                for k in range(2):
                    last = a.activation(Va[:, 2 * tp + k, :, 0:PA], vv[:, k, :, :], ACT.Copy)
                last.then_inc(S["sq"], 1)

        def q_evac(i, n, k):
            copy(i, BACK, n, QT[:, :, k * P:(k + 1) * P], ring(BACK, n)[:].rearrange("p (g c) -> p g c", g=G))

        def qk_turn(i, _):
            for k in range(TILES):
                q_evac(i, K_Q1 + k, k)
            copy(i, BACK, K_K, KT[:])

        def attend(i, u):
            if u == UNITS:
                return
            if u % HA == 0:
                for k in (2 * (u // HA), 2 * (u // HA) + 1):
                    q_evac(i, K_TURN(k), k)
            n = K_EXP(u)
            act.wait_ge(S["bk_full"], full_at(i, BACK, n))
            act.wait_ge(S["pv"], at(i, "pv", u - 1 if u >= 2 else 0))
            a.activation(PT[:, u % 2, :], ring(BACK, n)[:, 0:TRI], ACT.Exp).then_inc(evac(BACK, n), 1)

        def y_turn(i, _):
            copy(i, BACK, K_Y, ya[:])

        def o_proj(i, _):
            act.wait_ge(S["b7_free"], at(i, "b7_free", 2))
            squares(i, 1, xa, ss_b, junk_b, "ssq_b")

        def n4_turn(i, _):
            copy(i, BACK, K_N4, bnT[:])

        def up_b(i, _):
            for j in range(NBLK):
                act.wait_ge(S["bk_full"], full_at(i, BACK, K_FC + j))
                a.activation(bhid[:, j, :], ring(BACK, K_FC + j)[:], ACT.Relu).then_inc(evac(BACK, K_FC + j), 1)

        def x2_turn(i, _):
            act.wait_ge(S["b6_full"], at(i, "b6_full", 1))
            a.activation(bnT[:], B6[:], ACT.Copy).then_inc(S["b6_free"], 1)

        def gated(i, j):
            n = K_W + 2 * j
            act.wait_ge(S["bk_full"], full_at(i, BACK, n))
            if j >= 2:
                act.wait_ge(evac(BACK, n - 3), evac_at(i, BACK, n - 3))
            a.activation(sl[:, j % 2, :], ring(BACK, n)[:], ACT.Silu,
                         scale=cols[:, C_W1 + j:C_W1 + j + 1]).then_inc(evac(BACK, n), 1)

        def gelu(i, n, dst, c):
            act.wait_ge(S["bk_full"], full_at(i, BACK, n))
            a.activation(dst, ring(BACK, n)[:], ACT.Gelu, scale=cols[:, c:c + 1]).then_inc(evac(BACK, n), 1)

        def hidden1(i, j):
            gelu(i, K_H1 + j, hC[:, j, :], C_H1 + j)

        def hidden2(i, j):
            gelu(i, K_H2 + j, bhid[:, j, :], C_H2 + j)

        pipeline(act, dict(norm_in=norm_in, in_turn=in_turn, gates=gates, val_turn=val_turn, scan=scan, m_out=m_out,
                           n2_turn=n2_turn, up=up, norm_a=norm_a, qkv=qkv, qk_turn=qk_turn, attend=attend,
                           y_turn=y_turn, o_proj=o_proj, n4_turn=n4_turn, up_b=up_b, x2_turn=x2_turn, gated=gated,
                           hidden1=hidden1, hidden2=hidden2))

    @block.vector
    def _(dve):
        v = nc.vector
        step = [0]

        def prep_link(ins):
            step[0] += 1
            ins.then_inc(prep_dve, 1)
            dve.wait_ge(prep_dve, step[0])

        dve.wait_ge(weights_in, 16 * len(weights))
        prep_link(v.tensor_scalar(sc[:, 4, :], heads[:, 0, :], -1.0, None, ALU.mult))
        prep_link(v.tensor_tensor(sc[:, 0, :], heads[:, 0, :], sc[:, 4, :], ALU.min))
        v.tensor_scalar(sc[:, 11, :], heads[:, 1, :], 80.0, None, ALU.min).then_inc(prep, 1)
        dve.wait_ge(prep_act, 2)
        prep_link(v.tensor_scalar(sc[:, 4, :], sc[:, 1, :], 2.0, None, ALU.add))
        prep_link(v.reciprocal(sc[:, 5, :], sc[:, 4, :]))
        prep_link(v.tensor_tensor(sc[:, 6, :], sc[:, 1, :], sc[:, 5, :], ALU.mult))
        prep_link(v.tensor_tensor(sc[:, 7, :], sc[:, 6, :], sc[:, 6, :], ALU.mult))
        prep_link(v.tensor_scalar(sc[:, 8, :], sc[:, 7, :], 2.0 / 17, 2.0 / 15, ALU.mult, ALU.add))
        for odd in (13, 11, 9, 7, 5, 3, 1):
            prep_link(v.tensor_tensor(sc[:, 9, :], sc[:, 8, :], sc[:, 7, :], ALU.mult))
            prep_link(v.tensor_scalar(sc[:, 8, :], sc[:, 9, :], 2.0 / odd, None, ALU.add))
        prep_link(v.tensor_tensor(sc[:, 9, :], sc[:, 8, :], sc[:, 6, :], ALU.mult))
        prep_link(v.tensor_scalar(sc[:, 4, :], heads[:, 0, :], 0.0, None, ALU.max))
        prep_link(v.tensor_tensor(sc[:, 10, :], sc[:, 4, :], sc[:, 9, :], ALU.add))
        prep_link(v.tensor_tensor(sc[:, 5, :], sc[:, 10, :], sc[:, 2, :], ALU.mult))
        v.tensor_scalar(sc[:, 3, :], sc[:, 5, :], -1.0, -1e4, ALU.mult, ALU.max).then_inc(prep, 1)
        for w, r, nk in ((w_out, R_MS, 2), (w_mpj, R_MM, NBLK), (w_apj, R_AM, NBLK), (w_3, R_W3, NBLK)):
            for k in range(nk):
                v.tensor_tensor(w[:, k, :], w[:, k, :], rows[:, r, :], ALU.mult)
        v.tensor_tensor(w_o[:], w_o[:], rows[:, R_AS, :], ALU.mult)
        v.tensor_tensor(rows[:, R_M0, :], rows[:, R_M0, :], rows[:, R_M1, :], ALU.add)
        v.tensor_scalar(gain[:].rearrange("p (t h) -> p t h", t=TILES)[:, :, 0:HA],
                        gain[:].rearrange("p (t h) -> p t h", t=TILES)[:, :, 0:HA], 1.0 / float(np.sqrt(PA)), None, ALU.mult)
        v.tensor_copy(ident_bf[:], ident[:])
        v.tensor_copy(mask_bf[:], mask_f)
        dve.wait_ge(prep_act, 2 + HS)
        for h in range(HS):
            last = v.scalar_tensor_tensor(LM[:, h, :], LM[:, h, :], sc[:, 10, h:h + 1], causal, ALU.mult, ALU.mult)
        last.then_inc(prep, 1)
        dve.wait_ge(prep, 3)
        dve.wait_ge(prep_pool, 1)

        def token_stats(i, c, src, st, m, side):
            for k in range(TILES):
                last = v.bn_stats(st[:, k, :], src[:, k, :])
            last.then_inc(S["bn_" + side], 1)
            dve.wait_ge(S["bn_" + side], at(i, "bn_" + side, c + 1))
            v.memset(waited[:], 0.0)
            for k in range(TILES):
                last = v.bn_aggr(m[:, k, :], st[:, k, :])
            last.then_inc(S["aggr_" + side], TILES)

        def layer_norm(i, c, src, dst, m, r, name):
            dve.wait_ge(S[name], at(i, name, c))
            for k in range(TILES):
                last = v.tensor_scalar(dst[:, k, :], src[:, k, :], m[:, k, 0:1], r[:, k:k + 1], ALU.subtract, ALU.mult)
            return last

        def rms_norm(i, c, src, dst, r, name):
            dve.wait_ge(S[name], at(i, name, c))
            for k in range(TILES):
                last = v.tensor_scalar(dst[:, k, :], src[:, k, :], r[:, k:k + 1], float(np.sqrt(D)), ALU.mult, ALU.mult)
            return last

        def flat(x3):
            return x3[:].rearrange("p t d -> p (t d)")

        def by_channel(r):
            return rows[:, r, :].unsqueeze(1).to_broadcast([P, TILES, D])

        def norm_in(i, _):
            dve.wait_ge(S["x_in"], at(i, "x_in", 16))
            token_stats(i, 0, x_in, stat, mv, "f")
            layer_norm(i, 1, x_in, xh, mv, rs, "rs_f").then_inc(S["nrm_f"], 1)
            dve.wait_ge(S["nrm_f"], at(i, "nrm_f", 1))
            v.tensor_tensor(xm[:], xh[:], by_channel(R_M0), ALU.mult).then_inc(S["xm"], 1)
            dve.wait_ge(S["xm"], at(i, "xm", 1))
            rms_norm(i, 2, xm, nrm, rs, "rs_f").then_inc(S["nrm_f"], 1)

        def gates(i, _):
            for b in range(2):
                w = lambda j: cols[:, C_CW + b * KC + j:C_CW + b * KC + j + 1]
                dve.wait_ge(evac(FRONT, F_V + b), evac_at(i, FRONT, F_V + b))
                v.tensor_scalar(cv[:, b, :, :], vpad[:, b, :, 0:L], w(0), cols[:, C_CB + b:C_CB + b + 1],
                                ALU.mult, ALU.add).then_inc(S["conv"], 1)
                for j in range(1, KC):
                    dve.wait_ge(S["conv"], at(i, "conv", KC * b + j))
                    v.scalar_tensor_tensor(cv[:, b, :, :], vpad[:, b, :, j:j + L], w(j), cv[:, b, :, :],
                                           ALU.mult, ALU.add).then_inc(S["conv"], 1)

        def scan(i, u):
            if u < UNITS:
                dve.wait_ge(S["cb_full"], at(i, "cb_full", u + 1))
                dve.wait_ge(S["y_mm"], at(i, "y_mm", u - 1 if u >= 2 else 0))
                v.tensor_tensor(M[:, u % 2, :], CB[:, 0:TRI], LM[:, u // 2, :], ALU.mult).then_inc(S["masked"], 1)
            if u in (HS + 1, UNITS):
                b = 0 if u == HS + 1 else 1
                dve.wait_ge(S["y_mm"], at(i, "y_mm", HS * (b + 1)))
                v.scalar_tensor_tensor(yg[:, b, :], val[:, b, :], cols[:, C_D + b:C_D + b + 1], YACC[:],
                                       ALU.mult, ALU.add).then_inc(S["yacc_free"], 1)
                dve.wait_ge(S["yacc_free"], at(i, "yacc_free", b + 1))
                v.tensor_tensor(yg[:, b, :], yg[:, b, :], gate[:, b, :], ALU.mult).then_inc(S["yg"], 1)

        def m_out(i, _):
            dve.wait_ge(S["fr_full"], full_at(i, FRONT, F_O))
            v.tensor_tensor(flat(xm), flat(xm), ring(FRONT, F_O)[:], ALU.add).then_inc(evac(FRONT, F_O), 1)
            dve.wait_ge(evac(FRONT, F_O), evac_at(i, FRONT, F_O))
            rms_norm(i, 3, xm, nrm, rs, "rs_f").then_inc(S["nrm_f"], 1)
            dve.wait_ge(S["val"], at(i, "val", 2))
            v.tensor_tensor(mix, xh[:], by_channel(R_A1), ALU.mult).then_inc(S["mix"], 1)

        def down(i, _):
            dve.wait_ge(S["mlp_f"], at(i, "mlp_f", 1))
            v.tensor_tensor(flat(xm), flat(xm), YACC[:], ALU.add).then_inc(S["yacc_free"], 1)
            dve.wait_ge(S["yacc_free"], at(i, "yacc_free", 3))
            v.tensor_tensor(xm[:], xm[:], by_channel(R_A0), ALU.mult).then_inc(S["mix"], 1)
            dve.wait_ge(S["mix"], at(i, "mix", 2))
            dve.wait_ge(S["x1"], at(i, "x1", 0))
            v.tensor_tensor(xa[:], xm[:], mix, ALU.add).then_inc(S["xa"], 1)

        def norm_a(i, _):
            dve.wait_ge(S["xa"], at(i, "xa", 1))
            rms_norm(i, 1, xa, bn, brs, "rs_b").then_inc(S["nrm_b"], 1)

        def rope(i, _):
            n_link = [0]

            def link(ins):
                n_link[0] += 1
                ins.then_inc(S["newton"], 1)
                dve.wait_ge(S["newton"], at(i, "newton", n_link[0]))

            W = lambda k: qs[:, k, :]
            dve.wait_ge(S["sq"], at(i, "sq", 2))
            link(v.reduce_sum(W(5), sq[:].rearrange("p t h c -> p (t h) c"), axis=AX.X))
            link(v.tensor_scalar(W(0), W(5), 1.0 / PA, EPS_RMS, ALU.mult, ALU.add))
            link(v.tensor_scalar(qi[:], W(0).bitcast(I32), 1, None, ALU.logical_shift_right))
            link(v.tensor_scalar(yi[:], qi[:], -1.0, float(0x5F3759DF), ALU.mult, ALU.add))
            y = yi[:].bitcast(F32)
            for k in range(3):
                link(v.tensor_tensor(W(1), y, y, ALU.mult))
                link(v.scalar_tensor_tensor(W(2), W(1), -0.5, W(0), ALU.mult, ALU.mult))
                link(v.scalar_tensor_tensor(W(3 + k % 2), W(2), 1.5, y, ALU.add, ALU.mult))
                y = W(3 + k % 2)
            link(v.tensor_tensor(W(1), y, gain[:], ALU.mult))
            for tp in range(2):
                n = K_QKV + tp
                T = slice(2 * tp * QK, 2 * (tp + 1) * QK)
                q3 = ring(BACK, n)[:, 0:2 * QKV].rearrange("p (t h c) -> p t h c", t=2, c=PA)[:, :, 0:QK, :]
                scale = qs[:, 1, T].rearrange("p (t h) -> p t h", t=2).unsqueeze(3).to_broadcast([P, 2, QK, PA])
                v.tensor_tensor(qn[:, 2 * tp:2 * tp + 2, :, :], q3, scale, ALU.mult).then_inc(evac(BACK, n), 1)
            dve.wait_ge(evac(BACK, K_QKV), evac_at(i, BACK, K_QKV))
            dve.wait_ge(evac(BACK, K_QKV + 1), evac_at(i, BACK, K_QKV + 1))
            H2 = PA // 2
            for s in range(2):
                T = slice(2 * s, 2 * s + 2)
                fold = lambda z: z.rearrange("p t h c -> p (t h) c")
                v.tensor_tensor(ro[:, T], qn[:, T], cosT[:], ALU.mult)
                v.tensor_tensor(fold(r2[:, T])[:, :, 0:H2], fold(qn[:, T])[:, :, H2:], fold(sinT[:])[:, :, 0:H2], ALU.mult)
                last = v.tensor_tensor(fold(r2[:, T])[:, :, H2:], fold(qn[:, T])[:, :, 0:H2], fold(sinT[:])[:, :, H2:], ALU.mult)
            last.then_inc(S["rope"], 1)
            dve.wait_ge(S["rope"], at(i, "rope", 1))
            v.tensor_tensor(ro[:], ro[:], r2[:], ALU.add).then_inc(S["rope"], 1)
            dve.wait_ge(S["rope"], at(i, "rope", 2))
            qr, kr = ro[:, :, 0:HA, :], ro[:, :, HA:QK, :]
            v.tensor_copy(Q4[:, :, :, 0:8].bitcast(F32R), qr)
            v.tensor_copy(Q4[:, :, :, 8:16].bitcast(F32R), qr)
            v.tensor_copy(Ks[:, :, :, 0:8].bitcast(F32R), kr)
            v.tensor_copy(Ks[:, :, :, 16:24].bitcast(F32R), kr).then_inc(S["split"], 1)
            dve.wait_ge(S["split"], at(i, "split", 1))
            v.tensor_tensor(Q4[:, :, :, 16:24], qr, Q4[:, :, :, 0:8], ALU.subtract)
            v.tensor_tensor(Ks[:, :, :, 8:16], kr, Ks[:, :, :, 0:8], ALU.subtract).then_inc(S["split"], 1)

        def score(i, u):
            s, h = u // HA, u % HA
            n = K_S + u
            hq = (h % G) * HKV + h // G
            dve.wait_ge(S["bk_full"], full_at(i, BACK, n))
            v.reduce_max(mneg[:, 2 * s, hq:hq + 1], ring(BACK, n)[:, 0:P], axis=AX.X, negate=True)
            v.reduce_max(mneg[:, 2 * s + 1, hq:hq + 1], ring(BACK, n)[:, P:TRI], axis=AX.X, negate=True).then_inc(evac(BACK, n), 1)
            if h == HA - 1:
                T = slice(2 * s, 2 * s + 2)
                dve.wait_ge(evac(BACK, n), evac_at(i, BACK, n))
                v.tensor_copy(Q4[:, T, :, 24].bitcast(F32R), mneg[:, T, :]).then_inc(S["mrow"], 1)
                dve.wait_ge(S["mrow"], at(i, "mrow", 2 * s + 1))
                v.tensor_tensor(Q4[:, T, :, 25].bitcast(F32R), mneg[:, T, :], Q4[:, T, :, 24], ALU.subtract).then_inc(S["mrow"], 1)

        def y_turn(i, _):
            for s in range(2):
                T = slice(2 * s, 2 * s + 2)
                dve.wait_ge(S["pv"], at(i, "pv", HA * (s + 1)))
                v.reciprocal(rden[:, T, :], PV[s][:, :, :, PA]).then_inc(S["rden"], 1)
                dve.wait_ge(S["rden"], at(i, "rden", s + 1))
                v.tensor_tensor(ytm[:, T, :, :], PV[s][:, :, :, 0:PA], rden[:, T, :].unsqueeze(3).to_broadcast([P, 2, HA, PA]),
                                ALU.mult).then_inc(S["b6_free" if s == 0 else "b7_free"], 1)

        def o_proj(i, _):
            dve.wait_ge(S["b7_full"], at(i, "b7_full", 1))
            v.tensor_tensor(flat(xa), flat(xa), B7[:], ALU.add).then_inc(S["b7_free"], 1)
            dve.wait_ge(S["b7_free"], at(i, "b7_free", 2))
            rms_norm(i, 2, xa, bn, brs, "rs_b").then_inc(S["nrm_b"], 1)

        def down_b(i, _):
            dve.wait_ge(S["b7_full"], at(i, "b7_full", 2))
            v.tensor_tensor(flat(xa), flat(xa), B7[:], ALU.add).then_inc(S["b7_free"], 1)
            dve.wait_ge(S["b7_free"], at(i, "b7_free", 3))
            token_stats(i, 0, xa, bstat, bmv, "b")
            layer_norm(i, 3, xa, bn, bmv, brs, "rs_b").then_inc(S["nrm_b"], 1)
            dve.wait_ge(S["nrm_b"], at(i, "nrm_b", 3))
            dve.wait_ge(S["x_res"], at(i, "x_res", 16))
            v.tensor_tensor(x1[:], bn[:], x_res[:], ALU.add).then_inc(S["x1"], 1)
            dve.wait_ge(S["x1"], at(i, "x1", 1))
            token_stats(i, 1, x1, bstat, bmv, "b")
            layer_norm(i, 4, x1, bn, bmv, brs, "rs_b").then_inc(S["nrm_b"], 1)

        def gated(i, j):
            n = K_W + 2 * j + 1
            dve.wait_ge(S["bk_full"], full_at(i, BACK, n))
            dve.wait_ge(evac(BACK, n - 1), evac_at(i, BACK, n - 1))
            v.scalar_tensor_tensor(bhid[:, j, :], ring(BACK, n)[:], cols[:, C_W2 + j:C_W2 + j + 1], sl[:, j % 2, :],
                                   ALU.mult, ALU.mult).then_inc(evac(BACK, n), 1)

        def ffn_out(i, _):
            dve.wait_ge(S["b7_full"], at(i, "b7_full", 3))
            B7t = B7[:].rearrange("p (t d) -> p t d", t=TILES)
            token_stats(i, 2, B7t, bstat, bmv, "b")
            dve.wait_ge(S["stored"], at(i, "stored", 0))
            layer_norm(i, 5, B7t, out_sb, bmv, brs, "rs_b").then_inc(S["nrm_b"], 1)
            dve.wait_ge(S["nrm_b"], at(i, "nrm_b", 5))
            v.tensor_tensor(out_sb[:], out_sb[:], x1[:], ALU.add).then_inc(S["out_ready"], 1)

        pipeline(dve, dict(norm_in=norm_in, gates=gates, scan=scan, m_out=m_out, down=down, norm_a=norm_a, rope=rope,
                           score=score, y_turn=y_turn, o_proj=o_proj, down_b=down_b, gated=gated, ffn_out=ffn_out))

    @block.tensor
    def _(pe):
        p = nc.tensor
        pe.wait_ge(weights_in, 16 * len(weights))
        pe.wait_ge(prep, 3)
        pe.wait_ge(prep_pool, 1)

        def mm(o, lhsT, rhs, start):
            return p.matmul(o, lhsT, rhs, start=start, stop=True, skip_group_check=True)

        def turn(o, src):
            for k in range(TILES):
                last = p.transpose(o[:, k * P:(k + 1) * P], src[:, k, :], ident[:])
            return last

        def to_tokens(o, hidden, w, j):
            for k in range(TILES):
                last = mm(o[:, k * P:(k + 1) * P], hidden[:, k * P:(k + 1) * P], w[:, j, :], start=(j == 0 and k == 0))
            return last

        def project(i, r, n, w, src):
            pe.wait_ge(evac(r, n), free_at(i, r, n))
            mm(ring(r, n)[:], w, src, True).then_inc(S[r["full"]], 1)

        def in_turn(i, _):
            pe.wait_ge(S["xm"], at(i, "xm", 1))
            pe.wait_ge(evac(FRONT, F_XM), free_at(i, FRONT, F_XM))
            turn(ring(FRONT, F_XM), xm).then_inc(S["fr_full"], 1)
            pe.wait_ge(S["nrm_f"], at(i, "nrm_f", 2))
            pe.wait_ge(evac(FRONT, F_N), free_at(i, FRONT, F_N))
            turn(ring(FRONT, F_N), nrm).then_inc(S["fr_full"], 1)

        def gates(i, _):
            pe.wait_ge(evac(FRONT, F_N), evac_at(i, FRONT, F_N))
            for j in range(4):
                project(i, FRONT, F_V + j, w_in[:, j * P:(j + 1) * P], nT[:])

        def val_turn(i, _):
            for b in range(2):
                n = F_XT + b
                pe.wait_ge(S["val"], at(i, "val", b + 1))
                pe.wait_ge(evac(FRONT, n), free_at(i, FRONT, n))
                for k in range(TILES):
                    last = p.transpose(ring(FRONT, n)[:, k * P:(k + 1) * P], val[:, b, k * P:(k + 1) * P], ident[:])
                last.then_inc(S["fr_full"], 1)

        def project_BC(i, hp):
            for k, w in enumerate((w_B, w_C)):
                project(i, FRONT, F_BC + 2 * hp + k, w[:, hp * P:(hp + 1) * P], xmT[:])

        def scores(i, u):
            h, s = u // 2, u % 2
            hp, r, q0 = h // 2, (h % 2) * NS, s * L
            if u % 4 == 0:
                for n in (F_BC + 2 * hp, F_BC + 2 * hp + 1):
                    pe.wait_ge(evac(FRONT, n), evac_at(i, FRONT, n))
            pe.wait_ge(S["masked"], at(i, "masked", u))
            B_, C_ = BT[r:r + NS, hp % 2, :], CT[r:r + NS, hp % 2, :]
            mm(CB[:, 0:L], B_[:, q0:q0 + P], C_[:, q0:q0 + L], True)
            mm(CB[:, L:TRI], B_[:, q0 + P:q0 + L], C_[:, q0 + P:q0 + L], False).then_inc(S["cb_full"], 1)

        def values(i, u):
            h, s = u // 2, u % 2
            q0 = s * L
            if u % HS == 0:
                pe.wait_ge(S["yacc_free"], at(i, "yacc_free", u // HS))
            if u == 0:
                for n in (F_XT, F_XT + 1):
                    pe.wait_ge(evac(FRONT, n), evac_at(i, FRONT, n))
            pe.wait_ge(S["masked"], at(i, "masked", u + 1))
            quad = slice(32 * (h // 2 % 4), 32 * (h // 2 % 4) + 32)
            mm(YACC[quad, q0:q0 + L], xpad[:, 2 * s, h, :], M[:, u % 2, 0:L], start=(u % 4 == 0))
            mm(YACC[quad, q0 + P:q0 + L], xpad[:, 2 * s + 1, h, :], M[:, u % 2, L:TRI], False).then_inc(S["y_mm"], 1)

        def scan(i, u):
            if u == 0:
                project_BC(i, 0)
            if u % 4 == 2 and u // 4 + 1 < HS // 2:
                project_BC(i, u // 4 + 1)
            if u < UNITS:
                scores(i, u)
            if u >= 1:
                values(i, u - 1)

        def m_out(i, _):
            pe.wait_ge(evac(FRONT, F_O), free_at(i, FRONT, F_O))
            for j in range(2):
                pe.wait_ge(S["yg"], at(i, "yg", j + 1))
                last = to_tokens(ring(FRONT, F_O), yg[:, j, :], w_out, j)
            last.then_inc(S["fr_full"], 1)

        def n2_turn(i, _):
            pe.wait_ge(S["nrm_f"], at(i, "nrm_f", 3))
            pe.wait_ge(evac(FRONT, F_N2), free_at(i, FRONT, F_N2))
            turn(ring(FRONT, F_N2), nrm).then_inc(S["fr_full"], 1)

        def up(i, _):
            pe.wait_ge(evac(FRONT, F_N2), evac_at(i, FRONT, F_N2))
            for j in range(NBLK):
                project(i, FRONT, F_FC + j, w_mfc[:, j * P:(j + 1) * P], nT[:])

        def down(i, _):
            pe.wait_ge(S["yacc_free"], at(i, "yacc_free", 2))
            for j in range(NBLK):
                pe.wait_ge(S["hid_f"], at(i, "hid_f", j + 1))
                last = to_tokens(YACC, hid[:, j, :], w_mpj, j)
            last.then_inc(S["mlp_f"], 1)

        def qkv(i, _):
            pe.wait_ge(S["nrm_b"], at(i, "nrm_b", 1))
            pe.wait_ge(evac(BACK, K_N3), free_at(i, BACK, K_N3))
            turn(ring(BACK, K_N3), bn).then_inc(S["bk_full"], 1)
            pe.wait_ge(evac(BACK, K_N3), evac_at(i, BACK, K_N3))
            for tp in range(2):
                n = K_QKV + tp
                pe.wait_ge(evac(BACK, n), free_at(i, BACK, n))
                for k in range(2):
                    T = (2 * tp + k) * P
                    last = mm(ring(BACK, n)[:, k * QKV:(k + 1) * QKV], bnT[:, T:T + P], w_qkv[:], True)
                last.then_inc(S["bk_full"], 1)

        def q_turn(i, n, k):
            pe.wait_ge(evac(BACK, n), free_at(i, BACK, n))
            for g in range(G):
                last = p.transpose(ring(BACK, n)[:, g * P:(g + 1) * P], Qs[:, k, g, :, :].rearrange("p j c -> p (j c)"), ident[:])
            last.then_inc(S["bk_full"], 1)

        def qk_turn(i, _):
            pe.wait_ge(S["split"], at(i, "split", 2))
            for k in range(TILES):
                q_turn(i, K_Q1 + k, k)
            pe.wait_ge(evac(BACK, K_K), free_at(i, BACK, K_K))
            turn(ring(BACK, K_K), Ks[:].rearrange("p t j c -> p t (j c)")).then_inc(S["bk_full"], 1)

        def score(i, u):
            s, h = u // HA, u % HA
            n, j, g, q0 = K_S + u, h // G, h % G, s * L
            rows_ = slice(32 * j, 32 * j + 24)
            o = ring(BACK, n)
            if u == 0:
                for m in range(K_Q1, K_K + 1):
                    pe.wait_ge(evac(BACK, m), evac_at(i, BACK, m))
            pe.wait_ge(evac(BACK, n), free_at(i, BACK, n))
            mm(o[:, 0:P], QT[rows_, g, q0:q0 + P], KT[rows_, q0:q0 + P], True)
            mm(o[:, P:TRI], QT[rows_, g, q0 + P:q0 + L], KT[rows_, q0:q0 + L], False)
            mm(tri(o[:, 0:TRI]), ident_bf[:], mask_bf[:, 0, :, :], False).then_inc(S["bk_full"], 1)

        def weights_T(i, u):
            s, h = u // HA, u % HA
            n, j, g, q0 = K_EXP(u), h // G, h % G, s * L
            rows_ = slice(32 * j, 32 * j + 26)
            o = ring(BACK, n)
            if h == 0:
                for k in (2 * s, 2 * s + 1):
                    pe.wait_ge(evac(BACK, K_TURN(k)), evac_at(i, BACK, K_TURN(k)))
            pe.wait_ge(evac(BACK, n), free_at(i, BACK, n))
            mm(o[:, 0:L], KT[rows_, q0:q0 + P], QT[rows_, g, q0:q0 + L], True)
            mm(o[:, L:TRI], KT[rows_, q0 + P:q0 + L], QT[rows_, g, q0 + P:q0 + L], False)
            mm(tri(o[:, 0:TRI]), ident_bf[:], mask_bf[:, 1, :, :], False).then_inc(S["bk_full"], 1)

        def weighted(i, u):
            s, h = u // HA, u % HA
            hq, j = (h % G) * HKV + h // G, h // G
            if u == 0:
                pe.wait_ge(S["b6_free"], at(i, "b6_free", 0))
            if u == HA:
                pe.wait_ge(S["nrm_b"], at(i, "nrm_b", 0))
            pe.wait_ge(evac(BACK, K_EXP(u)), evac_at(i, BACK, K_EXP(u)))
            w = PT[:, u % 2, :]
            mm(PV[s][:, 0, hq, :], w[:, 0:P], Va[:, 2 * s, j, :], True)
            mm(PV[s][:, 1, hq, :], w[:, P:L], Va[:, 2 * s, j, :], True)
            mm(PV[s][:, 1, hq, :], w[:, L:TRI], Va[:, 2 * s + 1, j, :], False).then_inc(S["pv"], 1)

        def attend(i, u):
            if u < UNITS:
                if u % HA == 0:
                    pe.wait_ge(S["mrow"], at(i, "mrow", 2 * (u // HA) + 2))
                    for k in (2 * (u // HA), 2 * (u // HA) + 1):
                        q_turn(i, K_TURN(k), k)
                weights_T(i, u)
            if u >= 1:
                weighted(i, u - 1)

        def y_turn(i, _):
            pe.wait_ge(S["b6_free"], at(i, "b6_free", 1))
            pe.wait_ge(S["b7_free"], at(i, "b7_free", 1))
            pe.wait_ge(evac(BACK, K_Y), free_at(i, BACK, K_Y))
            turn(ring(BACK, K_Y), ytm[:].rearrange("p t h c -> p t (h c)")).then_inc(S["bk_full"], 1)

        def o_proj(i, _):
            pe.wait_ge(evac(BACK, K_Y), evac_at(i, BACK, K_Y))
            for k in range(TILES):
                last = mm(B7[:, k * P:(k + 1) * P], ya[:, k * P:(k + 1) * P], w_o[:], start=(k == 0))
            last.then_inc(S["b7_full"], 1)

        def n4_turn(i, _):
            pe.wait_ge(S["nrm_b"], at(i, "nrm_b", 2))
            pe.wait_ge(evac(BACK, K_N4), free_at(i, BACK, K_N4))
            turn(ring(BACK, K_N4), bn).then_inc(S["bk_full"], 1)

        def up_b(i, _):
            pe.wait_ge(evac(BACK, K_N4), evac_at(i, BACK, K_N4))
            for j in range(NBLK):
                project(i, BACK, K_FC + j, w_afc[:, j * P:(j + 1) * P], bnT[:])

        def down_b(i, _):
            pe.wait_ge(S["b7_free"], at(i, "b7_free", 2))
            for j in range(NBLK):
                pe.wait_ge(S["hid_b"], at(i, "hid_b", j + 1))
                last = to_tokens(B7, bhid[:, j, :], w_apj, j)
            last.then_inc(S["b7_full"], 1)

        def x2_turn(i, _):
            pe.wait_ge(S["nrm_b"], at(i, "nrm_b", 4))
            turn(B6, bn).then_inc(S["b6_full"], 1)

        def gated(i, j):
            if j == 0:
                pe.wait_ge(S["b6_free"], at(i, "b6_free", 2))
            project(i, BACK, K_W + 2 * j, w_1[:, j * P:(j + 1) * P], bnT[:])
            project(i, BACK, K_W + 2 * j + 1, w_2[:, j * P:(j + 1) * P], bnT[:])

        def hidden(i, n, j, w, src, ready):
            pe.wait_ge(evac(BACK, n), free_at(i, BACK, n))
            for k in range(NBLK):
                if j == 0:
                    pe.wait_ge(evac(BACK, ready(k)), evac_at(i, BACK, ready(k)))
                last = mm(ring(BACK, n)[:], w[:, k, j * P:(j + 1) * P], src[:, k, :], start=(k == 0))
            last.then_inc(S["bk_full"], 1)

        def hidden1(i, j):
            hidden(i, K_H1 + j, j, w_h1, bhid, lambda k: K_W + 2 * k + 1)

        def hidden2(i, j):
            hidden(i, K_H2 + j, j, w_h2, hC, lambda k: K_H1 + k)

        def ffn_out(i, _):
            pe.wait_ge(S["b7_free"], at(i, "b7_free", 3))
            for j in range(NBLK):
                pe.wait_ge(evac(BACK, K_H2 + j), evac_at(i, BACK, K_H2 + j))
                last = to_tokens(B7, bhid[:, j, :], w_3, j)
            last.then_inc(S["b7_full"], 1)

        pipeline(pe, dict(in_turn=in_turn, gates=gates, val_turn=val_turn, scan=scan, m_out=m_out, n2_turn=n2_turn,
                          up=up, down=down, qkv=qkv, qk_turn=qk_turn, score=score, attend=attend, y_turn=y_turn,
                          o_proj=o_proj, n4_turn=n4_turn, up_b=up_b, down_b=down_b, x2_turn=x2_turn, gated=gated,
                          hidden1=hidden1, hidden2=hidden2, ffn_out=ffn_out))

    ctx.close()



def kernel(**inputs):
    import numpy as _np
    import concourse.bacc as _bacc
    from concourse import mybir as _mybir
    from concourse.bass_utils import run_bass_kernel_spmd as _run

    A = {k.replace("L0_attn_", "").replace("L0_ffn_", ""): _np.asarray(v) for k, v in inputs.items()}
    rep = lambda v: _np.broadcast_to(v, (P,) + v.shape)
    blocks = lambda w: w.reshape(-1, P, w.shape[-1]).transpose(1, 0, 2)
    col = lambda v: v.reshape(-1, P).T
    order = _np.arange(HA).reshape(HKV, G).T.reshape(-1)
    q_w = A["q_w"].reshape(D, HA, PA)[:, order, :].reshape(D, D)
    o_w = A["o_w"].reshape(HA, PA, D)[order].reshape(D, D)
    conv = A["conv_w"].reshape(2, P, KC).transpose(1, 0, 2).reshape(P, 2 * KC)
    tens = {
        "x": A["x"].reshape(BATCH * L, D),
        "w_in": A["in_proj_w"], "w_B": A["B_proj_w"], "w_C": A["C_proj_w"], "w_out": blocks(A["out_proj_w"]),
        "w_mfc": A["m_fc_w"], "w_mpj": blocks(A["m_proj_w"]),
        "w_qkv": _np.concatenate([q_w, A["k_w"], A["v_w"]], axis=1), "w_o": o_w,
        "w_afc": A["a_fc_w"], "w_apj": blocks(A["a_proj_w"]),
        "w_1": A["w1_w"].T, "w_2": A["w2_w"].T, "w_h1": blocks(A["h1_w"].T), "w_h2": blocks(A["h2_w"].T),
        "w_3": blocks(A["w3_w"].T),
        "rows": rep(_np.stack([A["resid_mix_m"][0], A["resid_mix_m"][1], A["resid_mix_a"][0], A["resid_mix_a"][1],
                               A["mamba_scale"], A["m_mlp_scale"], A["attn_scale"], A["a_mlp_scale"], A["w3_s"]])),
        "cols": _np.concatenate([conv, col(A["conv_b"]), col(_np.repeat(A["D_param"], PS)), col(A["w1_s"]),
                                 col(A["w2_s"]), col(A["h1_s"]), col(A["h2_s"]), _np.zeros((P, 12), _np.float32)], axis=1),
        "heads": rep(_np.stack([A["dt_bias"], A["A_log"], A["A_log"]])),
        "gain": rep(_np.tile(_np.concatenate([A["q_gain"][order], _np.ones(HKV, _np.float32)]), TILES)),
    }
    r, c = _np.arange(P)[:, None], _np.arange(P)[None, :]
    later = _np.where(c >= r, c - r, 0)
    tens["c_ident"] = _np.eye(P)
    tens["c_diff"] = _np.concatenate([later, c - r + P, later], axis=1)
    tens["c_causal"] = _np.concatenate([c >= r, _np.ones((P, P)), c >= r], axis=1)
    tens["c_mask"] = _np.stack([_np.stack([_np.where(c > r, -1e30, 0.0)] * 2, 1), _np.stack([_np.where(r > c, -1e30, 0.0)] * 2, 1)], 1)
    inv = 1.0 / _np.float32(10000.0) ** (_np.arange(0, PA, 2, dtype=_np.float32) / PA)
    ang = _np.outer(_np.arange(L, dtype=_np.float32), inv).reshape(2, P, PA // 2).transpose(1, 0, 2)[:, :, None, :]
    ang = _np.broadcast_to(ang, (P, 2, QK, PA // 2))
    tens["c_cos"] = _np.concatenate([_np.cos(ang), _np.cos(ang)], axis=3)
    tens["c_sin"] = _np.concatenate([_np.sin(ang), -_np.sin(ang)], axis=3)

    nc = _bacc.Bacc("TRN2", target_bir_lowering=False, num_devices=1)
    t, arrays = {}, {}
    for name, a in tens.items():
        a = _np.ascontiguousarray(a, dtype=_np.float32)
        arrays["in_" + name] = a
        t[name] = nc.dram_tensor("in_" + name, a.shape, _mybir.dt.float32, kind="ExternalInput").ap()
    out = nc.dram_tensor("out_0", (BATCH * L, D), _mybir.dt.float32, kind="ExternalOutput").ap()
    program(nc, t, out)
    r = _run(nc, [arrays], core_ids=[0])
    return r.results[0]["out_0"].reshape(BATCH, L, D)
```

```python
from contextlib import ExitStack

import numpy as np
import concourse.bass as bass
from concourse import mybir

F32, F32R, BF16, I32 = mybir.dt.float32, mybir.dt.float32r, mybir.dt.bfloat16, mybir.dt.int32
ACT = mybir.ActivationFunctionType
ALU = mybir.AluOpType
AX = mybir.AxisListType

P = 128
BATCH, L, D = 16, 256, 128
DI, HS, NS, KC = 256, 16, 64, 4
PS = DI // HS
HA, HKV, PA = 16, 4, 8
G = HA // HKV
HID = 512
PAIRS = BATCH // 2
TOK = 2 * L
TILES = TOK // P
NBLK = HID // P
UNITS = 2 * HS
TRI = L + P
QK = HA + HKV
QKV = (HA + 2 * HKV) * PA
EPS_LN = 1e-5
EPS_RMS = float(np.finfo(np.float32).eps)

EXPS = 3 * HKV

PER = dict(
    x_in=16, bn_f=1, aggr_f=4, rs_f_eps=3, rs_f=3, nrm_f=3, xm=1, ssq_f=8, conv=8, val=2, cb_full=32, masked=32,
    y_mm=32, yacc_free=3, yg=2, hid_f=4, mlp_f=1, mix=2, fr_full=30, fr_evac0=15, fr_evac1=15,
    xa=1, x_res=16, rs_b_eps=4, rs_b=4, nrm_b=4, ssq_b=8, sq=2, newton=14, rope=2, split=2, mrow=4, pv=24, pv_evac=4,
    rden=4, b7_full=3, b7_free=2, hid_b=4, bn_b=2, aggr_b=8, x1=1, bk_full=94, bk_evac0=47, bk_evac1=47,
    out_ready=1, stored=16, split_b=2,
    bn_o=1, aggr_o=4, rs_o_eps=1, rs_o=1, nrm_o=1)


def _body():
    at, out = [0], []

    def scans(n=1):
        out.extend(("scan", 2, u) for u in range(at[0], at[0] + n))
        at[0] += n

    def step(name, ahead, k=0):
        out.append((name, ahead, k))

    step("load_x", 2)
    step("x2_turn", 0)
    step("gated", 0, 0)
    step("gated", 0, 1)
    step("m_out", 1)
    step("gated", 0, 2)
    step("m_norm", 1)
    step("gated", 0, 3)
    step("n2_turn", 1)
    step("hidden1", 0, 0)
    step("up", 1)
    step("hidden1", 0, 1)
    step("hidden1", 0, 2)
    step("down", 1)
    step("norm_in", 2)
    step("hidden1", 0, 3)
    step("norm_in2", 2)
    step("hidden2", 0, 0)
    step("in_turn", 2)
    step("norm_a", 1)
    step("hidden2", 0, 1)
    step("gates", 2)
    step("hidden2", 0, 2)
    step("hidden2", 0, 3)
    step("val_turn", 2)
    step("ffn_out", 0)
    step("load_res", 1)
    scans(1)
    step("ffn_norm", 0)
    step("store", 0)
    step("qkv", 1)
    scans(3)
    step("rope1", 1)
    scans(1)
    step("rope2", 1)
    scans(1)
    step("rope3", 1)
    scans(1)
    step("qk_turn", 1)
    step("split32", 1)
    scans(1)
    for u in range(UNITS):
        step("score", 1, u)
        if u % 4 == 3:
            scans(1)
    for s in range(2):
        step("q2_turn", 1, s)
        for e in range(EXPS):
            step("attend", 1, s * EXPS + e)
            if s == 1 and e == 1:
                step("y_rows", 1, 0)
            if e % 4 == 3:
                scans(1)
    step("attend", 1, 2 * EXPS)
    scans(1)
    step("y_rows", 1, 1)
    scans(1)
    step("y_turn", 1)
    scans(1)
    step("o_proj", 1)
    scans(1)
    step("n4_norm", 1)
    scans(1)
    step("n4_turn", 1)
    step("up_b", 1)
    scans(1)
    step("down_b", 1)
    scans(1)
    step("ln_a", 1)
    scans(1)
    step("ln_b", 1)
    scans(UNITS + 1 - at[0])
    return out


BODY = _body()


def program(nc, t, out):
    ctx = ExitStack()

    def sb(name, shape, dt=F32):
        return ctx.enter_context(nc.sbuf_tensor(name, shape, dt))

    def sem(name):
        return ctx.enter_context(nc.semaphore(name))

    S = {name: sem(name) for name in PER}

    def at(i, name, c):
        return i * PER[name] + c + 1

    ident = sb("ident", [P, P])
    ident_bf = sb("ident_bf", [P, P], BF16)
    sl = sb("sl", [P, 2, TOK])
    diff, causal = sl[:, 0, 0:TRI], sl[:, 1, 0:TRI]
    sq = sb("sq", [P, TILES, QK, PA])
    mask_f = sq[:].rearrange("p t h c -> p (t h c)")[:, 0:2 * P].rearrange("p (a c) -> p a c", a=2)
    mask_bf = sb("mask_bf", [P, 2, G, P], BF16)
    cosT = sb("cosT", [P, 2, QK, PA])
    sinT = sb("sinT", [P, 2, QK, PA])
    w_in = sb("w_in", [P, 2 * DI])
    w_B = sb("w_B", [P, HS * NS])
    w_C = sb("w_C", [P, HS * NS])
    w_out = sb("w_out", [P, 2, D])
    w_mfc = sb("w_mfc", [P, HID])
    w_mpj = sb("w_mpj", [P, NBLK, D])
    w_qkv = sb("w_qkv", [P, QKV])
    w_o = sb("w_o", [P, D])
    w_afc = sb("w_afc", [P, HID])
    w_apj = sb("w_apj", [P, NBLK, D])
    w_1 = sb("w_1", [P, HID])
    w_2 = sb("w_2", [P, HID])
    w_h1 = sb("w_h1", [P, NBLK, HID])
    w_h2 = sb("w_h2", [P, NBLK, HID])
    w_3 = sb("w_3", [P, NBLK, D])
    rows = sb("rows", [P, 9, D])
    R_M0, R_M1, R_A0, R_A1, R_MS, R_MM, R_AS, R_AM, R_W3 = range(9)
    cols = sb("cols", [P, 40])
    C_CW, C_CB, C_D, C_W1, C_W2, C_H1, C_H2 = 0, 8, 10, 12, 16, 20, 24
    heads = sb("heads", [P, 3, HS])
    gain = sb("gain", [P, TILES * QK])
    LM = sb("LM", [P, HS, TRI])
    half = sb("half", [P, TILES])
    eps_ln = sb("eps_ln", [P, TILES])
    eps_rms = sb("eps_rms", [P, TILES])
    waited = sb("waited", [P, 1])
    sc = sb("sc", [P, 12, HS])

    x_in = sb("x_in", [P, TILES, D])
    stat = sb("stat", [P, TILES, 6])
    mv = sb("mv", [P, TILES, 2])
    ms = sb("ms", [P, TILES])
    rs = sb("rs", [P, TILES])
    ss_f = sb("ss_f", [P, TILES])
    junk_a = sb("junk_a", [P, TILES, D])
    xh = sb("xh", [P, TILES, D])
    xm = sb("xm", [P, TILES, D])
    nrm = sb("nrm", [P, TILES, D])
    xmT = sb("xmT", [P, TOK])
    nT = sb("nT", [P, TOK])
    vpad = sb("vpad", [P, 2, 2, L + KC - 1])
    cv = sb("cv", [P, 2, 2, L])
    val = sb("val", [P, 2, TOK])
    gate = sb("gate", [P, 2, TOK])
    xpad = sb("xpad", [P, TILES, HS, 2 * PS])
    BT = sb("BT", [P, 2, TOK])
    CT = sb("CT", [P, 2, TOK])
    M = sb("M", [P, 2, TRI])
    yg = val
    relu = sb("relu", [P, NBLK, TOK])
    hid = relu
    mix = cv[:, 0, :, :].rearrange("p s (t d) -> p (s t) d", d=D)

    xa = sb("xa", [P, TILES, D])
    x_res = sb("x_res", [P, TILES, D])
    bstat = sb("bstat", [P, TILES, 6])
    bmv = sb("bmv", [P, TILES, 2])
    bms = sb("bms", [P, TILES])
    brs = sb("brs", [P, TILES])
    ss_b = sb("ss_b", [P, TILES])
    ostat = sb("ostat", [P, TILES, 6])
    omv = sb("omv", [P, TILES, 2])
    oms = sb("oms", [P, TILES])
    ors = sb("ors", [P, TILES])
    x1 = sb("x1", [P, TILES, D])
    junk_b = junk_a
    bn = sb("bn", [P, TILES, D])
    bnT = sb("bnT", [P, TOK])
    qs = sb("qs", [P, 6, TILES * QK])
    qi = sb("qi", [P, TILES * QK], I32)
    yi = sb("yi", [P, TILES * QK], I32)
    qn = sb("qn", [P, TILES, QK, PA])
    ro = sb("ro", [P, TILES, QK, PA])
    r2 = sq
    Qs = sb("Qs", [P, TILES, G, HKV, 32])
    Ks = sb("Ks", [P, TILES, HKV, 32])
    QT = sb("QT", [P, G, TOK], F32R)
    KT = sb("KT", [P, TOK], F32R)
    Qb = sb("Qb", [P, TILES, G, HKV, 32], BF16)
    Kb = sb("Kb", [P, TILES, HKV, 32], BF16)
    QTb = sb("QTb", [P, G, TOK], BF16)
    KTb = sb("KTb", [P, TOK], BF16)
    Va = sb("Va", [P, TILES, HKV, 32])
    mneg = sb("mneg", [P, TILES, HA])
    PT = sb("PT", [P, 2, 512])
    yv = sl
    rden = sb("rden", [P, 2, 2, 4 * HKV])
    ytm = qn[:].rearrange("p t h c -> p (t h c)")[:, 0:TILES * D].rearrange("p (t h c) -> p t h c", t=TILES, c=PA)
    ya = bnT
    bhid = sb("bhid", [P, NBLK, TOK])
    brelu = bhid
    hC = Qs[:].rearrange("p t g j c -> p t (g j c)")
    hD = brelu
    out_sb = sb("out_sb", [P, TILES, D])

    bank = [ctx.enter_context(nc.psum_tensor(f"bank{k}", [P, 512], F32)) for k in range(8)]
    FRONT = dict(banks=(0, 1), full="fr_full", evac=("fr_evac0", "fr_evac1"))
    BACK = dict(banks=(4, 5), full="bk_full", evac=("bk_evac0", "bk_evac1"))
    CB, YACC = bank[2], bank[3]
    B6, B7 = bank[6], bank[7]
    PV = (B6, B7)
    Q4 = Qs[:].rearrange("p t g j c -> p t (g j) c")
    Qb4 = Qb[:].rearrange("p t g j c -> p t (g j) c")

    def ring(r, n):
        return bank[r["banks"][n % 2]]

    def ring_bf(r, n):
        return ring(r, n)[:].bitcast(BF16)

    def evac(r, n):
        return S[r["evac"][n % 2]]

    def free_at(i, r, n):
        return at(i, r["evac"][n % 2], n // 2)

    def evac_at(i, r, n):
        return at(i, r["evac"][n % 2], n // 2 + 1)

    def full_at(i, r, n):
        return at(i, r["full"], n + 1)

    F_XM, F_N, F_V, F_G, F_XT, F_BC, F_O, F_N2, F_FC = 0, 1, 2, 4, 6, 8, 24, 25, 26
    K_N3, K_QKV, K_QB, K_KB, K_K, K_S, K_SOFT = 0, 1, 3, 5, 6, 7, 39
    K_Y, K_N4, K_FC, K_X2, K_W, K_H1, K_H2 = 71, 72, 73, 77, 78, 86, 90

    def K_TURN(k):
        return K_SOFT + (k // 2) * (2 + EXPS) + k % 2

    def K_EXP(e):
        return K_SOFT + 2 + e if e < EXPS else K_SOFT + 4 + e if e < EXPS + 2 else K_SOFT + 6 + e

    def K_YT(s, c):
        return K_SOFT + (6 + EXPS if s == 0 else 6 + 2 * EXPS) + c

    def diag(x, k, b):
        H8 = HS // 2
        whole = x[:, k, b * H8:(b + 1) * H8, :].rearrange("p h c -> p (h c)")
        return bass.AP(whole.tensor, whole.offset, [list(whole.ap[0]), [4 * PS, H8 // 2], [3 * PS, 2], [1, PS]])

    def tri(ap):
        return ap.rearrange("p (a b) -> p a b", b=P)[:, 0:3:2, :]

    weights = [
        (ident, "c_ident"), (w_in, "w_in"), (rows, "rows"), (cols, "cols"), (heads, "heads"),
        (diff, "c_diff"), (causal, "c_causal"), (w_B, "w_B"), (w_C, "w_C"),
        (mask_f, "c_mask"), (w_out, "w_out"), (w_mfc, "w_mfc"), (w_mpj, "w_mpj"), (gain, "gain"), (cosT, "c_cos"),
        (sinT, "c_sin"), (w_qkv, "w_qkv"), (w_o, "w_o"), (w_afc, "w_afc"), (w_apj, "w_apj"),
        (w_1, "w_1"), (w_2, "w_2"), (w_h1, "w_h1"), (w_h2, "w_h2"), (w_3, "w_3")]
    weights_in = sem("weights_in")
    prep_pool, prep_act, prep, prep_dve = sem("prep_pool"), sem("prep_act"), sem("prep"), sem("prep_dve")
    xt_v = t["x"].rearrange("(n p) d -> p n d", p=P)
    ot_v = out.rearrange("(n p) d -> p n d", p=P)
    block = ctx.enter_context(nc.Block())

    def run(parts, i, whole):
        for name, ahead, k in BODY:
            if name in parts and (whole or 0 <= i + ahead < PAIRS):
                parts[name](i + ahead, k)

    def pipeline(eng, parts):
        run(parts, -2, False)
        run(parts, -1, False)
        with eng.Fori(0, PAIRS - 2) as i:
            run(parts, i, True)
        run(parts, PAIRS - 2, False)
        run(parts, PAIRS - 1, False)

    @block.sync
    def _(sp):
        def load_x(i):
            sp.wait_ge(S["xm"], at(i, "xm", 0))
            sp.dma_start(x_in[:], xt_v[:, bass.ds(i * TILES, TILES), :]).then_inc(S["x_in"], 16)

        def load_res(i, _):
            sp.wait_ge(S["x1"], at(i, "x1", 0))
            sp.dma_start(x_res[:], xt_v[:, bass.ds(i * TILES, TILES), :]).then_inc(S["x_res"], 16)

        def store(i, _):
            sp.wait_ge(S["out_ready"], at(i, "out_ready", 1))
            sp.dma_start(ot_v[:, bass.ds(i * TILES, TILES), :], out_sb[:]).then_inc(S["stored"], 16)

        for name in PER:
            sp.sem_inc(S[name], 1)
        for dst, name in weights:
            if name == "w_in":
                load_x(0)
            sp.dma_start(dst if isinstance(dst, bass.AP) else dst[:], t[name]).then_inc(weights_in, 16)
        pipeline(sp, dict(load_x=lambda i, _: load_x(i) if not (isinstance(i, int) and i == 0) else None,
                          load_res=load_res, store=store))
        sp.wait_ge(S["stored"], at(PAIRS, "stored", 0))

    @block.gpsimd
    def _(pool):
        g = nc.gpsimd
        g.memset(half[:], -0.5)
        g.memset(eps_ln[:], EPS_LN)
        g.memset(eps_rms[:], D * EPS_RMS)
        g.memset(vpad[:], 0.0)
        g.memset(xpad[:], 0.0)
        g.memset(Qs[:], 0.0)
        g.memset(Ks[:, :, :, 0:24], 0.0)
        g.memset(Ks[:, :, :, 24:26], 1.0)
        g.memset(Ks[:, :, :, 26:32], 0.0)
        g.memset(Qb[:], 0.0)
        g.memset(Kb[:], 0.0)
        g.memset(Va[:, :, :, 0:PA], 0.0)
        g.memset(Va[:, :, :, PA + 1:32], 0.0)
        g.memset(Va[:, :, :, PA:PA + 1], 1.0).then_inc(prep_pool, 1)
        pool.wait_ge(prep_pool, 1)

        def rsqrt(i, c, name, src, dst, tmp, eps, ready, ready_c, used):
            pool.wait_ge(S[ready], at(i, ready, ready_c))
            pool.wait_ge(S[used], at(i, used, c))
            g.tensor_tensor(tmp[:], src, eps[:], ALU.add).then_inc(S[name + "_eps"], 1)
            pool.wait_ge(S[name + "_eps"], at(i, name + "_eps", c + 1))
            g.tensor_tensor(dst[:], tmp[:], half[:], ALU.pow).then_inc(S[name], 1)

        def square_hidden(i, r, n0, h, done):
            for j in range(NBLK):
                pool.wait_ge(evac(r, n0 + j), evac_at(i, r, n0 + j))
                g.tensor_tensor(h[:, j, :], h[:, j, :], h[:, j, :], ALU.mult).then_inc(S[done], 1)

        def norm_in(i, _):
            rsqrt(i, 0, "rs_f", mv[:, :, 1], rs, ms, eps_ln, "aggr_f", TILES, "nrm_f")

        def norm_in2(i, _):
            rsqrt(i, 1, "rs_f", ss_f[:], rs, ms, eps_rms, "ssq_f", TILES, "nrm_f")

        def m_out(i, _):
            rsqrt(i, 2, "rs_f", ss_f[:], rs, ms, eps_rms, "ssq_f", 2 * TILES, "nrm_f")

        def up(i, _):
            square_hidden(i, FRONT, F_FC, hid, "hid_f")

        def norm_a(i, _):
            rsqrt(i, 0, "rs_b", ss_b[:], brs, bms, eps_rms, "ssq_b", TILES, "nrm_b")

        def o_proj(i, _):
            rsqrt(i, 1, "rs_b", ss_b[:], brs, bms, eps_rms, "ssq_b", 2 * TILES, "nrm_b")

        def up_b(i, _):
            square_hidden(i, BACK, K_FC, bhid, "hid_b")

        def down_b(i, _):
            rsqrt(i, 2, "rs_b", bmv[:, :, 1], brs, bms, eps_ln, "aggr_b", TILES, "nrm_b")

        def ln_a(i, _):
            rsqrt(i, 3, "rs_b", bmv[:, :, 1], brs, bms, eps_ln, "aggr_b", 2 * TILES, "nrm_b")

        def ffn_out(i, _):
            rsqrt(i, 0, "rs_o", omv[:, :, 1], ors, oms, eps_ln, "aggr_o", TILES, "nrm_o")

        pipeline(pool, dict(norm_in=norm_in, norm_in2=norm_in2, ln_a=ln_a, m_out=m_out, up=up, norm_a=norm_a, o_proj=o_proj, up_b=up_b,
                            down_b=down_b, ffn_out=ffn_out))

    @block.scalar
    def _(act):
        a = nc.scalar
        act.wait_ge(weights_in, 16 * len(weights))
        act.wait_ge(prep, 1)
        a.activation(sc[:, 1, :], sc[:, 0, :], ACT.Exp).then_inc(prep_act, 1)
        a.activation(sc[:, 2, :], sc[:, 11, :], ACT.Exp).then_inc(prep_act, 1)
        act.wait_ge(prep, 2)
        for h in range(HS):
            a.activation(LM[:, h, :], diff, ACT.Exp, scale=sc[:, 3, h:h + 1]).then_inc(prep_act, 1)

        def squares(i, c, src, dst, junk, done):
            for k in range(TILES):
                last = a.activation(junk[:, k, :], src[:, k, :], ACT.Square, accum_out=dst[:, k:k + 1])
            last.then_inc(S[done], TILES)
            act.wait_ge(S[done], at(i, done, TILES * (c + 1)))

        def copy(i, r, n, dst, src=None):
            act.wait_ge(S[r["full"]], full_at(i, r, n))
            a.activation(dst, ring(r, n)[:] if src is None else src, ACT.Copy).then_inc(evac(r, n), 1)

        def norm_in2(i, _):
            act.wait_ge(S["xm"], at(i, "xm", 1))
            squares(i, 0, xm, ss_f, junk_a, "ssq_f")

        def in_turn(i, _):
            copy(i, FRONT, F_XM, xmT[:])
            copy(i, FRONT, F_N, nT[:])

        def gates(i, _):
            for b in range(2):
                n = F_V + b
                copy(i, FRONT, n, vpad[:, b, :, KC - 1:], ring(FRONT, n)[:].rearrange("p (s l) -> p s l", s=2))
            for b in range(2):
                n = F_G + b
                act.wait_ge(S["fr_full"], full_at(i, FRONT, n))
                a.activation(gate[:, b, :], ring(FRONT, n)[:], ACT.Silu).then_inc(evac(FRONT, n), 1)
            for b in range(2):
                act.wait_ge(S["conv"], at(i, "conv", KC * (b + 1)))
                a.activation(val[:, b, :], cv[:, b, :, :].rearrange("p s l -> p (s l)"), ACT.Silu).then_inc(S["val"], 1)

        def val_turn(i, _):
            for b in range(2):
                n = F_XT + b
                act.wait_ge(S["fr_full"], full_at(i, FRONT, n))
                for k in range(TILES):
                    src = ring(FRONT, n)[:, k * P:(k + 1) * P].rearrange("p (a b c) -> p a b c", b=2, c=PS)
                    last = a.activation(diag(xpad, k, b), src, ACT.Copy)
                last.then_inc(evac(FRONT, n), 1)

        def scan(i, u):
            if u % 4 == 2 and u // 4 + 1 < HS // 2:
                project_BC(i, u // 4 + 1)
            if u == 0:
                project_BC(i, 0)

        def project_BC(i, hp):
            for k, dst in enumerate((BT, CT)):
                if hp >= 2:
                    act.wait_ge(S["cb_full"], at(i, "cb_full", 4 * (hp - 1)))
                copy(i, FRONT, F_BC + 2 * hp + k, dst[:, hp % 2, :])

        def m_out(i, _):
            act.wait_ge(evac(FRONT, F_O), evac_at(i, FRONT, F_O))
            squares(i, 1, xm, ss_f, junk_a, "ssq_f")

        def n2_turn(i, _):
            copy(i, FRONT, F_N2, nT[:])

        def up(i, _):
            for j in range(NBLK):
                act.wait_ge(S["fr_full"], full_at(i, FRONT, F_FC + j))
                a.activation(relu[:, j, :], ring(FRONT, F_FC + j)[:], ACT.Relu).then_inc(evac(FRONT, F_FC + j), 1)

        def norm_a(i, _):
            act.wait_ge(S["xa"], at(i, "xa", 1))
            squares(i, 0, xa, ss_b, junk_b, "ssq_b")

        def qkv(i, _):
            copy(i, BACK, K_N3, bnT[:])
            for tp in range(2):
                n = K_QKV + tp
                act.wait_ge(S["bk_full"], full_at(i, BACK, n))
                q3 = ring(BACK, n)[:, 0:2 * QKV].rearrange("p (t c) -> p t c", t=2)
                a.activation(sq[:, 2 * tp:2 * tp + 2, :, :].rearrange("p t h c -> p t (h c)"), q3[:, :, 0:QK * PA], ACT.Square)
                vv = q3[:, :, QK * PA:].rearrange("p t (h c) -> p t h c", c=PA)
                for k in range(2):
                    last = a.activation(Va[:, 2 * tp + k, :, 0:PA], vv[:, k, :, :], ACT.Copy)
                last.then_inc(S["sq"], 1)

        def q_evac(i, n, k):
            copy(i, BACK, n, QT[:, :, k * P:(k + 1) * P], ring(BACK, n)[:].rearrange("p (g c) -> p g c", g=G))

        def qk_turn(i, _):
            for c in range(2):
                n = K_QB + c
                act.wait_ge(S["bk_full"], full_at(i, BACK, n))
                for k in range(2):
                    src = ring_bf(BACK, n)[:, k * 4 * P:(k + 1) * 4 * P].rearrange("p (g c) -> p g c", g=G)
                    last = a.activation(QTb[:, :, (2 * c + k) * P:(2 * c + k + 1) * P], src, ACT.Copy)
                last.then_inc(evac(BACK, n), 1)
            copy(i, BACK, K_KB, KTb[:], ring_bf(BACK, K_KB)[:, 0:TOK])

        def split32(i, _):
            copy(i, BACK, K_K, KT[:])

        def q2_turn(i, s):
            for k in (2 * s, 2 * s + 1):
                q_evac(i, K_TURN(k), k)

        def attend(i, e):
            if e == EXPS or e == 2 * EXPS:
                s = e // EXPS - 1
                act.wait_ge(S["pv"], at(i, "pv", e))
                if s == 1:
                    act.wait_ge(S["bk_full"], full_at(i, BACK, K_YT(0, 1)))
                else:
                    act.wait_ge(S["bk_full"], at(i, "bk_full", 0))
                for c in range(2):
                    a.activation(yv[:, c, :], PV[c][:], ACT.Copy).then_inc(S["pv_evac"], 1)
            if e == 2 * EXPS:
                return
            n = K_EXP(e)
            act.wait_ge(S["bk_full"], full_at(i, BACK, n))
            act.wait_ge(S["pv"], at(i, "pv", e - 1 if e >= 2 else 0))
            a.activation(PT[:, e % 2, :], ring(BACK, n)[:], ACT.Exp).then_inc(evac(BACK, n), 1)

        def y_turn(i, _):
            copy(i, BACK, K_Y, ya[:])

        def o_proj(i, _):
            act.wait_ge(S["b7_free"], at(i, "b7_free", 1))
            squares(i, 1, xa, ss_b, junk_b, "ssq_b")

        def n4_turn(i, _):
            copy(i, BACK, K_N4, bnT[:])

        def up_b(i, _):
            for j in range(NBLK):
                act.wait_ge(S["bk_full"], full_at(i, BACK, K_FC + j))
                a.activation(bhid[:, j, :], ring(BACK, K_FC + j)[:], ACT.Relu).then_inc(evac(BACK, K_FC + j), 1)

        def x2_turn(i, _):
            copy(i, BACK, K_X2, bnT[:])

        def gated(i, j):
            n = K_W + 2 * j
            act.wait_ge(S["bk_full"], full_at(i, BACK, n))
            if j >= 2:
                act.wait_ge(evac(BACK, n - 3), evac_at(i, BACK, n - 3))
            a.activation(sl[:, j % 2, :], ring(BACK, n)[:], ACT.Silu,
                         scale=cols[:, C_W1 + j:C_W1 + j + 1]).then_inc(evac(BACK, n), 1)

        def gelu(i, n, dst, c):
            act.wait_ge(S["bk_full"], full_at(i, BACK, n))
            a.activation(dst, ring(BACK, n)[:], ACT.Gelu, scale=cols[:, c:c + 1]).then_inc(evac(BACK, n), 1)

        def hidden1(i, j):
            gelu(i, K_H1 + j, hC[:, j, :], C_H1 + j)

        def hidden2(i, j):
            gelu(i, K_H2 + j, bhid[:, j, :], C_H2 + j)

        pipeline(act, dict(norm_in2=norm_in2, in_turn=in_turn, gates=gates, val_turn=val_turn, scan=scan, m_out=m_out,
                           n2_turn=n2_turn, up=up, norm_a=norm_a, qkv=qkv, qk_turn=qk_turn, split32=split32, q2_turn=q2_turn, attend=attend,
                           y_turn=y_turn, o_proj=o_proj, n4_turn=n4_turn, up_b=up_b, x2_turn=x2_turn, gated=gated,
                           hidden1=hidden1, hidden2=hidden2))

    @block.vector
    def _(dve):
        v = nc.vector
        step = [0]

        def prep_link(ins):
            step[0] += 1
            ins.then_inc(prep_dve, 1)
            dve.wait_ge(prep_dve, step[0])

        dve.wait_ge(weights_in, 16 * len(weights))
        prep_link(v.tensor_scalar(sc[:, 4, :], heads[:, 0, :], -1.0, None, ALU.mult))
        prep_link(v.tensor_tensor(sc[:, 0, :], heads[:, 0, :], sc[:, 4, :], ALU.min))
        v.tensor_scalar(sc[:, 11, :], heads[:, 1, :], 80.0, None, ALU.min).then_inc(prep, 1)
        dve.wait_ge(prep_act, 2)
        prep_link(v.tensor_scalar(sc[:, 4, :], sc[:, 1, :], 2.0, None, ALU.add))
        prep_link(v.reciprocal(sc[:, 5, :], sc[:, 4, :]))
        prep_link(v.tensor_tensor(sc[:, 6, :], sc[:, 1, :], sc[:, 5, :], ALU.mult))
        prep_link(v.tensor_tensor(sc[:, 7, :], sc[:, 6, :], sc[:, 6, :], ALU.mult))
        prep_link(v.tensor_scalar(sc[:, 8, :], sc[:, 7, :], 2.0 / 17, 2.0 / 15, ALU.mult, ALU.add))
        for odd in (13, 11, 9, 7, 5, 3, 1):
            prep_link(v.tensor_tensor(sc[:, 9, :], sc[:, 8, :], sc[:, 7, :], ALU.mult))
            prep_link(v.tensor_scalar(sc[:, 8, :], sc[:, 9, :], 2.0 / odd, None, ALU.add))
        prep_link(v.tensor_tensor(sc[:, 9, :], sc[:, 8, :], sc[:, 6, :], ALU.mult))
        prep_link(v.tensor_scalar(sc[:, 4, :], heads[:, 0, :], 0.0, None, ALU.max))
        prep_link(v.tensor_tensor(sc[:, 10, :], sc[:, 4, :], sc[:, 9, :], ALU.add))
        prep_link(v.tensor_tensor(sc[:, 5, :], sc[:, 10, :], sc[:, 2, :], ALU.mult))
        v.tensor_scalar(sc[:, 3, :], sc[:, 5, :], -1.0, -1e4, ALU.mult, ALU.max).then_inc(prep, 1)
        for w, r, nk in ((w_out, R_MS, 2), (w_mpj, R_MM, NBLK), (w_apj, R_AM, NBLK), (w_3, R_W3, NBLK)):
            for k in range(nk):
                v.tensor_tensor(w[:, k, :], w[:, k, :], rows[:, r, :], ALU.mult)
        v.tensor_tensor(w_o[:], w_o[:], rows[:, R_AS, :], ALU.mult)
        v.tensor_tensor(rows[:, R_M0, :], rows[:, R_M0, :], rows[:, R_M1, :], ALU.add)
        v.tensor_scalar(gain[:].rearrange("p (t h) -> p t h", t=TILES)[:, :, 0:HA],
                        gain[:].rearrange("p (t h) -> p t h", t=TILES)[:, :, 0:HA], 1.0 / float(np.sqrt(PA)), None, ALU.mult)
        v.tensor_copy(ident_bf[:], ident[:])
        v.tensor_copy(mask_bf[:], mask_f.unsqueeze(2).to_broadcast([P, 2, G, P]))
        dve.wait_ge(prep_act, 2 + HS)
        for h in range(HS):
            last = v.scalar_tensor_tensor(LM[:, h, :], LM[:, h, :], sc[:, 10, h:h + 1], causal, ALU.mult, ALU.mult)
        last.then_inc(prep, 1)
        dve.wait_ge(prep, 3)
        dve.wait_ge(prep_pool, 1)

        def token_stats(i, c, src, st, m, side):
            for k in range(TILES):
                last = v.bn_stats(st[:, k, :], src[:, k, :])
            last.then_inc(S["bn_" + side], 1)
            dve.wait_ge(S["bn_" + side], at(i, "bn_" + side, c + 1))
            v.memset(waited[:], 0.0)
            for k in range(TILES):
                last = v.bn_aggr(m[:, k, :], st[:, k, :])
            last.then_inc(S["aggr_" + side], TILES)

        def layer_norm(i, c, src, dst, m, r, name):
            dve.wait_ge(S[name], at(i, name, c))
            for k in range(TILES):
                last = v.tensor_scalar(dst[:, k, :], src[:, k, :], m[:, k, 0:1], r[:, k:k + 1], ALU.subtract, ALU.mult)
            return last

        def rms_norm(i, c, src, dst, r, name):
            dve.wait_ge(S[name], at(i, name, c))
            for k in range(TILES):
                last = v.tensor_scalar(dst[:, k, :], src[:, k, :], r[:, k:k + 1], float(np.sqrt(D)), ALU.mult, ALU.mult)
            return last

        def flat(x3):
            return x3[:].rearrange("p t d -> p (t d)")

        def by_channel(r):
            return rows[:, r, :].unsqueeze(1).to_broadcast([P, TILES, D])

        def norm_in(i, _):
            dve.wait_ge(S["x_in"], at(i, "x_in", 16))
            token_stats(i, 0, x_in, stat, mv, "f")

        def norm_in2(i, _):
            layer_norm(i, 1, x_in, xh, mv, rs, "rs_f").then_inc(S["nrm_f"], 1)
            dve.wait_ge(S["nrm_f"], at(i, "nrm_f", 1))
            v.tensor_tensor(xm[:], xh[:], by_channel(R_M0), ALU.mult).then_inc(S["xm"], 1)

        def in_turn(i, _):
            rms_norm(i, 2, xm, nrm, rs, "rs_f").then_inc(S["nrm_f"], 1)

        def gates(i, _):
            for b in range(2):
                w = lambda j: cols[:, C_CW + b * KC + j:C_CW + b * KC + j + 1]
                dve.wait_ge(evac(FRONT, F_V + b), evac_at(i, FRONT, F_V + b))
                v.tensor_scalar(cv[:, b, :, :], vpad[:, b, :, 0:L], w(0), cols[:, C_CB + b:C_CB + b + 1],
                                ALU.mult, ALU.add).then_inc(S["conv"], 1)
                for j in range(1, KC):
                    dve.wait_ge(S["conv"], at(i, "conv", KC * b + j))
                    v.scalar_tensor_tensor(cv[:, b, :, :], vpad[:, b, :, j:j + L], w(j), cv[:, b, :, :],
                                           ALU.mult, ALU.add).then_inc(S["conv"], 1)

        def scan(i, u):
            if u < UNITS:
                dve.wait_ge(S["cb_full"], at(i, "cb_full", u + 1))
                dve.wait_ge(S["y_mm"], at(i, "y_mm", u - 1 if u >= 2 else 0))
                v.tensor_tensor(M[:, u % 2, :], CB[:, 0:TRI], LM[:, u // 2, :], ALU.mult).then_inc(S["masked"], 1)
            if u in (HS + 1, UNITS):
                b = 0 if u == HS + 1 else 1
                dve.wait_ge(S["y_mm"], at(i, "y_mm", HS * (b + 1)))
                v.scalar_tensor_tensor(yg[:, b, :], val[:, b, :], cols[:, C_D + b:C_D + b + 1], YACC[:],
                                       ALU.mult, ALU.add).then_inc(S["yacc_free"], 1)
                dve.wait_ge(S["yacc_free"], at(i, "yacc_free", b + 1))
                v.tensor_tensor(yg[:, b, :], yg[:, b, :], gate[:, b, :], ALU.mult).then_inc(S["yg"], 1)

        def m_out(i, _):
            dve.wait_ge(S["fr_full"], full_at(i, FRONT, F_O))
            v.tensor_tensor(flat(xm), flat(xm), ring(FRONT, F_O)[:], ALU.add).then_inc(evac(FRONT, F_O), 1)

        def m_norm(i, _):
            rms_norm(i, 3, xm, nrm, rs, "rs_f").then_inc(S["nrm_f"], 1)
            dve.wait_ge(S["val"], at(i, "val", 2))
            v.tensor_tensor(mix, xh[:], by_channel(R_A1), ALU.mult).then_inc(S["mix"], 1)

        def down(i, _):
            dve.wait_ge(S["mlp_f"], at(i, "mlp_f", 1))
            v.tensor_tensor(flat(xm), flat(xm), YACC[:], ALU.add).then_inc(S["yacc_free"], 1)
            dve.wait_ge(S["yacc_free"], at(i, "yacc_free", 3))
            v.tensor_tensor(xm[:], xm[:], by_channel(R_A0), ALU.mult).then_inc(S["mix"], 1)
            dve.wait_ge(S["mix"], at(i, "mix", 2))
            dve.wait_ge(S["x1"], at(i, "x1", 0))
            v.tensor_tensor(xa[:], xm[:], mix, ALU.add).then_inc(S["xa"], 1)

        def qkv(i, _):
            rms_norm(i, 1, xa, bn, brs, "rs_b").then_inc(S["nrm_b"], 1)

        n_link = [0]

        def rope1(i, _):
            n_link[0] = 0
            rope_links(i, 0)

        def rope2(i, _):
            rope_links(i, 1)

        def rope3(i, _):
            rope_links(i, 2)

        def rope_links(i, part):

            def link(ins):
                n_link[0] += 1
                ins.then_inc(S["newton"], 1)
                dve.wait_ge(S["newton"], at(i, "newton", n_link[0]))

            W = lambda k: qs[:, k, :]
            if part == 0:
                dve.wait_ge(S["sq"], at(i, "sq", 2))
                link(v.reduce_sum(W(5), sq[:].rearrange("p t h c -> p (t h) c"), axis=AX.X))
                link(v.tensor_scalar(W(0), W(5), 1.0 / PA, EPS_RMS, ALU.mult, ALU.add))
                link(v.tensor_scalar(qi[:], W(0).bitcast(I32), 1, None, ALU.logical_shift_right))
                link(v.tensor_scalar(yi[:], qi[:], -1.0, float(0x5F3759DF), ALU.mult, ALU.add))
                link(v.tensor_tensor(W(1), yi[:].bitcast(F32), yi[:].bitcast(F32), ALU.mult))
                link(v.scalar_tensor_tensor(W(2), W(1), -0.5, W(0), ALU.mult, ALU.mult))
                link(v.scalar_tensor_tensor(W(3), W(2), 1.5, yi[:].bitcast(F32), ALU.add, ALU.mult))
                return
            if part == 1:
                for k in (3, 4):
                    link(v.tensor_tensor(W(1), W(k), W(k), ALU.mult))
                    link(v.scalar_tensor_tensor(W(2), W(1), -0.5, W(0), ALU.mult, ALU.mult))
                    link(v.scalar_tensor_tensor(W(7 - k), W(2), 1.5, W(k), ALU.add, ALU.mult))
                link(v.tensor_tensor(W(1), W(3), gain[:], ALU.mult))
                for tp in range(2):
                    n = K_QKV + tp
                    T = slice(2 * tp * QK, 2 * (tp + 1) * QK)
                    q3 = ring(BACK, n)[:, 0:2 * QKV].rearrange("p (t h c) -> p t h c", t=2, c=PA)[:, :, 0:QK, :]
                    scale = qs[:, 1, T].rearrange("p (t h) -> p t h", t=2).unsqueeze(3).to_broadcast([P, 2, QK, PA])
                    v.tensor_tensor(qn[:, 2 * tp:2 * tp + 2, :, :], q3, scale, ALU.mult).then_inc(evac(BACK, n), 1)
                return
            dve.wait_ge(evac(BACK, K_QKV), evac_at(i, BACK, K_QKV))
            dve.wait_ge(evac(BACK, K_QKV + 1), evac_at(i, BACK, K_QKV + 1))
            H2 = PA // 2
            for s in range(2):
                T = slice(2 * s, 2 * s + 2)
                fold = lambda z: z.rearrange("p t h c -> p (t h) c")
                v.tensor_tensor(ro[:, T], qn[:, T], cosT[:], ALU.mult)
                v.tensor_tensor(fold(r2[:, T])[:, :, 0:H2], fold(qn[:, T])[:, :, H2:], fold(sinT[:])[:, :, 0:H2], ALU.mult)
                last = v.tensor_tensor(fold(r2[:, T])[:, :, H2:], fold(qn[:, T])[:, :, 0:H2], fold(sinT[:])[:, :, H2:], ALU.mult)
            last.then_inc(S["rope"], 1)
            dve.wait_ge(S["rope"], at(i, "rope", 1))
            v.tensor_tensor(ro[:], ro[:], r2[:], ALU.add).then_inc(S["rope"], 1)
            dve.wait_ge(S["rope"], at(i, "rope", 2))
            qr, kr = ro[:, :, 0:HA, :], ro[:, :, HA:QK, :]
            v.tensor_copy(Qb4[:, :, :, 0:8], qr)
            v.tensor_copy(Kb[:, :, :, 0:8], kr)
            v.tensor_copy(Qb4[:, :, :, 8:16], qr)
            v.tensor_copy(Kb[:, :, :, 16:24], kr).then_inc(S["split_b"], 1)
            dve.wait_ge(S["split_b"], at(i, "split_b", 1))
            v.tensor_tensor(Qb4[:, :, :, 16:24], qr, Qb4[:, :, :, 0:8], ALU.subtract)
            v.tensor_tensor(Kb[:, :, :, 8:16], kr, Kb[:, :, :, 0:8], ALU.subtract).then_inc(S["split_b"], 1)

        def split32(i, _):
            qr, kr = ro[:, :, 0:HA, :], ro[:, :, HA:QK, :]
            v.tensor_copy(Ks[:, :, :, 0:8].bitcast(F32R), kr)
            v.tensor_copy(Ks[:, :, :, 16:24].bitcast(F32R), kr)
            v.tensor_copy(Q4[:, :, :, 0:8].bitcast(F32R), qr)
            v.tensor_copy(Q4[:, :, :, 8:16].bitcast(F32R), qr).then_inc(S["split"], 1)
            dve.wait_ge(S["split"], at(i, "split", 1))
            v.tensor_tensor(Ks[:, :, :, 8:16], kr, Ks[:, :, :, 0:8], ALU.subtract).then_inc(S["split"], 1)
            v.tensor_tensor(Q4[:, :, :, 16:24], qr, Q4[:, :, :, 0:8], ALU.subtract)

        def score(i, u):
            s, h = u // HA, u % HA
            n = K_S + u
            hq = (h % G) * HKV + h // G
            dve.wait_ge(S["bk_full"], full_at(i, BACK, n))
            v.reduce_max(mneg[:, 2 * s, hq:hq + 1], ring(BACK, n)[:, 0:P], axis=AX.X, negate=True)
            v.reduce_max(mneg[:, 2 * s + 1, hq:hq + 1], ring(BACK, n)[:, P:TRI], axis=AX.X, negate=True).then_inc(evac(BACK, n), 1)
            if h == HA - 1:
                T = slice(2 * s, 2 * s + 2)
                dve.wait_ge(evac(BACK, n), evac_at(i, BACK, n))
                v.tensor_copy(Q4[:, T, :, 24].bitcast(F32R), mneg[:, T, :]).then_inc(S["mrow"], 1)
                dve.wait_ge(S["mrow"], at(i, "mrow", 2 * s + 1))
                v.tensor_tensor(Q4[:, T, :, 25].bitcast(F32R), mneg[:, T, :], Q4[:, T, :, 24], ALU.subtract).then_inc(S["mrow"], 1)

        def y_rows(i, s):
            for c in range(2):
                n = K_YT(s, c)
                dve.wait_ge(S["bk_full"], full_at(i, BACK, n))
                rows_ = ring(BACK, n)[:].rearrange("p (g t j c) -> p g t j c", g=2, t=2, j=HKV)
                rd = rden[:, s, c, :].rearrange("p (g t j) -> p g t j", g=2, t=2)
                for g in range(2):
                    last = v.reciprocal(rd[:, g], rows_[:, g, :, :, PA])
                last.then_inc(S["rden"], 1)
                dve.wait_ge(S["rden"], at(i, "rden", 2 * s + c + 1))
                for g in range(2):
                    last = v.tensor_tensor(ytm[:, 2 * s:2 * s + 2, 2 * c + g:HA:G, :], rows_[:, g, :, :, 0:PA],
                                           rd[:, g].unsqueeze(3).to_broadcast([P, 2, HKV, PA]), ALU.mult)
                last.then_inc(evac(BACK, n), 1)

        def o_proj(i, _):
            dve.wait_ge(S["b7_full"], at(i, "b7_full", 1))
            v.tensor_tensor(flat(xa), flat(xa), B7[:], ALU.add).then_inc(S["b7_free"], 1)

        def n4_norm(i, _):
            rms_norm(i, 2, xa, bn, brs, "rs_b").then_inc(S["nrm_b"], 1)

        def down_b(i, _):
            dve.wait_ge(S["b7_full"], at(i, "b7_full", 2))
            v.tensor_tensor(flat(xa), flat(xa), B7[:], ALU.add).then_inc(S["b7_free"], 1)
            dve.wait_ge(S["b7_free"], at(i, "b7_free", 2))
            token_stats(i, 0, xa, bstat, bmv, "b")

        def ln_a(i, _):
            layer_norm(i, 3, xa, bn, bmv, brs, "rs_b").then_inc(S["nrm_b"], 1)
            dve.wait_ge(S["nrm_b"], at(i, "nrm_b", 3))
            dve.wait_ge(S["x_res"], at(i, "x_res", 16))
            dve.wait_ge(S["out_ready"], at(i, "out_ready", 0))
            v.tensor_tensor(x1[:], bn[:], x_res[:], ALU.add).then_inc(S["x1"], 1)
            dve.wait_ge(S["x1"], at(i, "x1", 1))
            token_stats(i, 1, x1, bstat, bmv, "b")

        def ln_b(i, _):
            layer_norm(i, 4, x1, bn, bmv, brs, "rs_b").then_inc(S["nrm_b"], 1)

        def gated(i, j):
            n = K_W + 2 * j + 1
            dve.wait_ge(S["bk_full"], full_at(i, BACK, n))
            dve.wait_ge(evac(BACK, n - 1), evac_at(i, BACK, n - 1))
            v.scalar_tensor_tensor(bhid[:, j, :], ring(BACK, n)[:], cols[:, C_W2 + j:C_W2 + j + 1], sl[:, j % 2, :],
                                   ALU.mult, ALU.mult).then_inc(evac(BACK, n), 1)

        def ffn_out(i, _):
            dve.wait_ge(S["b7_full"], at(i, "b7_full", 3))
            token_stats(i, 0, B7[:].rearrange("p (t d) -> p t d", t=TILES), ostat, omv, "o")

        def ffn_norm(i, _):
            dve.wait_ge(S["stored"], at(i, "stored", 0))
            layer_norm(i, 1, B7[:].rearrange("p (t d) -> p t d", t=TILES), out_sb, omv, ors, "rs_o").then_inc(S["nrm_o"], 1)
            dve.wait_ge(S["nrm_o"], at(i, "nrm_o", 1))
            v.tensor_tensor(out_sb[:], out_sb[:], x1[:], ALU.add).then_inc(S["out_ready"], 1)

        pipeline(dve, dict(norm_in=norm_in, norm_in2=norm_in2, in_turn=in_turn, gates=gates, scan=scan, m_out=m_out,
                           m_norm=m_norm, down=down, qkv=qkv, rope1=rope1, rope2=rope2, rope3=rope3, split32=split32,
                           score=score, y_rows=y_rows, o_proj=o_proj, n4_norm=n4_norm, down_b=down_b, ln_a=ln_a,
                           ln_b=ln_b, gated=gated, ffn_out=ffn_out, ffn_norm=ffn_norm))

    @block.tensor
    def _(pe):
        p = nc.tensor
        pe.wait_ge(weights_in, 16 * len(weights))
        pe.wait_ge(prep, 3)
        pe.wait_ge(prep_pool, 1)

        def mm(o, lhsT, rhs, start):
            return p.matmul(o, lhsT, rhs, start=start, stop=True, skip_group_check=True)

        def turn(o, src):
            for k in range(TILES):
                last = p.transpose(o[:, k * P:(k + 1) * P], src[:, k, :], ident[:])
            return last

        def to_tokens(o, hidden, w, j):
            for k in range(TILES):
                last = mm(o[:, k * P:(k + 1) * P], hidden[:, k * P:(k + 1) * P], w[:, j, :], start=(j == 0 and k == 0))
            return last

        def project(i, r, n, w, src):
            pe.wait_ge(evac(r, n), free_at(i, r, n))
            mm(ring(r, n)[:], w, src, True).then_inc(S[r["full"]], 1)

        def in_turn(i, _):
            pe.wait_ge(S["xm"], at(i, "xm", 1))
            pe.wait_ge(evac(FRONT, F_XM), free_at(i, FRONT, F_XM))
            turn(ring(FRONT, F_XM), xm).then_inc(S["fr_full"], 1)
            pe.wait_ge(S["nrm_f"], at(i, "nrm_f", 2))
            pe.wait_ge(evac(FRONT, F_N), free_at(i, FRONT, F_N))
            turn(ring(FRONT, F_N), nrm).then_inc(S["fr_full"], 1)

        def gates(i, _):
            pe.wait_ge(evac(FRONT, F_N), evac_at(i, FRONT, F_N))
            for j in range(4):
                project(i, FRONT, F_V + j, w_in[:, j * P:(j + 1) * P], nT[:])

        def val_turn(i, _):
            for b in range(2):
                n = F_XT + b
                pe.wait_ge(S["val"], at(i, "val", b + 1))
                pe.wait_ge(evac(FRONT, n), free_at(i, FRONT, n))
                for k in range(TILES):
                    last = p.transpose(ring(FRONT, n)[:, k * P:(k + 1) * P], val[:, b, k * P:(k + 1) * P], ident[:])
                last.then_inc(S["fr_full"], 1)

        def project_BC(i, hp):
            for k, w in enumerate((w_B, w_C)):
                project(i, FRONT, F_BC + 2 * hp + k, w[:, hp * P:(hp + 1) * P], xmT[:])

        def scores(i, u):
            h, s = u // 2, u % 2
            hp, r, q0 = h // 2, (h % 2) * NS, s * L
            if u % 4 == 0:
                for n in (F_BC + 2 * hp, F_BC + 2 * hp + 1):
                    pe.wait_ge(evac(FRONT, n), evac_at(i, FRONT, n))
            pe.wait_ge(S["masked"], at(i, "masked", u))
            B_, C_ = BT[r:r + NS, hp % 2, :], CT[r:r + NS, hp % 2, :]
            mm(CB[:, 0:L], B_[:, q0:q0 + P], C_[:, q0:q0 + L], True)
            mm(CB[:, L:TRI], B_[:, q0 + P:q0 + L], C_[:, q0 + P:q0 + L], False).then_inc(S["cb_full"], 1)

        def values(i, u):
            h, s = u // 2, u % 2
            q0 = s * L
            if u % HS == 0:
                pe.wait_ge(S["yacc_free"], at(i, "yacc_free", u // HS))
            if u == 0:
                for n in (F_XT, F_XT + 1):
                    pe.wait_ge(evac(FRONT, n), evac_at(i, FRONT, n))
            pe.wait_ge(S["masked"], at(i, "masked", u + 1))
            quad = slice(32 * (h // 2 % 4), 32 * (h // 2 % 4) + 32)
            mm(YACC[quad, q0:q0 + L], xpad[:, 2 * s, h, :], M[:, u % 2, 0:L], start=(u % 4 == 0))
            mm(YACC[quad, q0 + P:q0 + L], xpad[:, 2 * s + 1, h, :], M[:, u % 2, L:TRI], False).then_inc(S["y_mm"], 1)

        def scan(i, u):
            if u == 0:
                project_BC(i, 0)
            if u % 4 == 2 and u // 4 + 1 < HS // 2:
                project_BC(i, u // 4 + 1)
            if u < UNITS:
                scores(i, u)
            if u >= 1:
                values(i, u - 1)

        def m_out(i, _):
            pe.wait_ge(evac(FRONT, F_O), free_at(i, FRONT, F_O))
            for j in range(2):
                pe.wait_ge(S["yg"], at(i, "yg", j + 1))
                last = to_tokens(ring(FRONT, F_O), yg[:, j, :], w_out, j)
            last.then_inc(S["fr_full"], 1)

        def n2_turn(i, _):
            pe.wait_ge(S["nrm_f"], at(i, "nrm_f", 3))
            pe.wait_ge(evac(FRONT, F_N2), free_at(i, FRONT, F_N2))
            turn(ring(FRONT, F_N2), nrm).then_inc(S["fr_full"], 1)

        def up(i, _):
            pe.wait_ge(evac(FRONT, F_N2), evac_at(i, FRONT, F_N2))
            for j in range(NBLK):
                project(i, FRONT, F_FC + j, w_mfc[:, j * P:(j + 1) * P], nT[:])

        def down(i, _):
            pe.wait_ge(S["yacc_free"], at(i, "yacc_free", 2))
            for j in range(NBLK):
                pe.wait_ge(S["hid_f"], at(i, "hid_f", j + 1))
                last = to_tokens(YACC, hid[:, j, :], w_mpj, j)
            last.then_inc(S["mlp_f"], 1)

        def qkv(i, _):
            pe.wait_ge(S["nrm_b"], at(i, "nrm_b", 1))
            pe.wait_ge(evac(BACK, K_N3), free_at(i, BACK, K_N3))
            turn(ring(BACK, K_N3), bn).then_inc(S["bk_full"], 1)
            pe.wait_ge(evac(BACK, K_N3), evac_at(i, BACK, K_N3))
            for tp in range(2):
                n = K_QKV + tp
                pe.wait_ge(evac(BACK, n), free_at(i, BACK, n))
                for k in range(2):
                    T = (2 * tp + k) * P
                    last = mm(ring(BACK, n)[:, k * QKV:(k + 1) * QKV], bnT[:, T:T + P], w_qkv[:], True)
                last.then_inc(S["bk_full"], 1)

        def q_turn(i, n, k):
            pe.wait_ge(evac(BACK, n), free_at(i, BACK, n))
            for g in range(G):
                last = p.transpose(ring(BACK, n)[:, g * P:(g + 1) * P], Qs[:, k, g, :, :].rearrange("p j c -> p (j c)"), ident[:])
            last.then_inc(S["bk_full"], 1)

        def qk_turn(i, _):
            pe.wait_ge(S["split_b"], at(i, "split_b", 2))
            for c in range(2):
                n = K_QB + c
                pe.wait_ge(evac(BACK, n), free_at(i, BACK, n))
                for k in range(2):
                    for g in range(G):
                        m = (k * G + g) * P
                        last = p.transpose(ring_bf(BACK, n)[:, m:m + P],
                                           Qb[:, 2 * c + k, g, :, :].rearrange("p j c -> p (j c)"), ident_bf[:])
                last.then_inc(S["bk_full"], 1)
            pe.wait_ge(evac(BACK, K_KB), free_at(i, BACK, K_KB))
            for k in range(TILES):
                last = p.transpose(ring_bf(BACK, K_KB)[:, k * P:(k + 1) * P],
                                   Kb[:, k, :, :].rearrange("p j c -> p (j c)"), ident_bf[:])
            last.then_inc(S["bk_full"], 1)

        def split32(i, _):
            pe.wait_ge(S["split"], at(i, "split", 2))
            pe.wait_ge(evac(BACK, K_K), free_at(i, BACK, K_K))
            turn(ring(BACK, K_K), Ks[:].rearrange("p t j c -> p t (j c)")).then_inc(S["bk_full"], 1)

        def score(i, u):
            s, h = u // HA, u % HA
            n, j, g, q0 = K_S + u, h // G, h % G, s * L
            rows_ = slice(32 * j, 32 * j + 24)
            o = ring(BACK, n)
            if u == 0:
                for m in (K_QB, K_QB + 1, K_KB):
                    pe.wait_ge(evac(BACK, m), evac_at(i, BACK, m))
            pe.wait_ge(evac(BACK, n), free_at(i, BACK, n))
            mm(o[:, 0:P], QTb[rows_, g, q0:q0 + P], KTb[rows_, q0:q0 + P], True)
            mm(o[:, P:TRI], QTb[rows_, g, q0 + P:q0 + L], KTb[rows_, q0:q0 + L], False)
            mm(tri(o[:, 0:TRI]), ident_bf[:], mask_bf[:, 0, 0:2, :], False).then_inc(S["bk_full"], 1)

        def q2_turn(i, s):
            pe.wait_ge(S["mrow"], at(i, "mrow", 2 * s + 2))
            for k in (2 * s, 2 * s + 1):
                n = K_TURN(k)
                pe.wait_ge(evac(BACK, n), free_at(i, BACK, n))
                for g in range(G):
                    last = p.transpose(ring(BACK, n)[:, g * P:(g + 1) * P], Qs[:, k, g, :, :].rearrange("p j c -> p (j c)"), ident[:])
                last.then_inc(S["bk_full"], 1)

        def weights_T(i, e):
            s, j, c = e // EXPS, e % EXPS // 3, e % 3
            n, q0, rows_ = K_EXP(e), s * L, slice(32 * j, 32 * j + 26)
            o = ring(BACK, n)[:]
            if e % EXPS == 0:
                for k in (2 * s, 2 * s + 1):
                    pe.wait_ge(evac(BACK, K_TURN(k)), evac_at(i, BACK, K_TURN(k)))
            if e == 0:
                pe.wait_ge(evac(BACK, K_K), evac_at(i, BACK, K_K))
            pe.wait_ge(evac(BACK, n), free_at(i, BACK, n))
            if c < 2:
                o3 = o.rearrange("p (g q) -> p g q", g=2)
                mm(o3, KT[rows_, q0:q0 + P], QT[rows_, 2 * c:2 * c + 2, q0:q0 + L], True)
                mm(o3[:, :, 0:P], ident_bf[:], mask_bf[:, 1, 0:2, :], False).then_inc(S["bk_full"], 1)
            else:
                o3 = o.rearrange("p (g q) -> p g q", g=G)
                mm(o3, KT[rows_, q0 + P:q0 + L], QT[rows_, :, q0 + P:q0 + L], True)
                mm(o3, ident_bf[:], mask_bf[:, 1, :, :], False).then_inc(S["bk_full"], 1)

        def weighted(i, e):
            s, j, c = e // EXPS, e % EXPS // 3, e % 3
            quad = slice(32 * j, 32 * j + 32)
            if e % EXPS == 0:
                pe.wait_ge(S["pv_evac"], at(i, "pv_evac", 2 * s))
                if s == 0:
                    pe.wait_ge(S["nrm_o"], at(i, "nrm_o", 0))
            pe.wait_ge(evac(BACK, K_EXP(e)), evac_at(i, BACK, K_EXP(e)))
            w = PT[:, e % 2, :]
            if c < 2:
                last = mm(PV[c][quad, :], Va[:, 2 * s, j, :], w, True)
            else:
                for b in range(2):
                    o3 = PV[b][quad, :].rearrange("p (g q) -> p g q", g=2)[:, :, P:L]
                    last = mm(o3, Va[:, 2 * s + 1, j, :], w[:, b * L:(b + 1) * L].rearrange("p (g q) -> p g q", g=2), False)
            last.then_inc(S["pv"], 1)

        def attend(i, e):
            if e < 2 * EXPS:
                weights_T(i, e)
            if e >= 1:
                weighted(i, e - 1)

        def y_rows(i, s):
            for c in range(2):
                n = K_YT(s, c)
                pe.wait_ge(S["pv_evac"], at(i, "pv_evac", 2 * s + c + 1))
                pe.wait_ge(evac(BACK, n), free_at(i, BACK, n))
                for m in range(4):
                    last = p.transpose(ring(BACK, n)[:, m * P:(m + 1) * P], yv[:, c, m * P:(m + 1) * P], ident[:])
                last.then_inc(S["bk_full"], 1)

        def y_turn(i, _):
            for c in range(2):
                pe.wait_ge(evac(BACK, K_YT(1, c)), evac_at(i, BACK, K_YT(1, c)))
            pe.wait_ge(evac(BACK, K_Y), free_at(i, BACK, K_Y))
            turn(ring(BACK, K_Y), ytm.rearrange("p t h c -> p t (h c)")).then_inc(S["bk_full"], 1)

        def o_proj(i, _):
            pe.wait_ge(evac(BACK, K_Y), evac_at(i, BACK, K_Y))
            for k in range(TILES):
                last = mm(B7[:, k * P:(k + 1) * P], ya[:, k * P:(k + 1) * P], w_o[:], start=(k == 0))
            last.then_inc(S["b7_full"], 1)

        def n4_turn(i, _):
            pe.wait_ge(S["nrm_b"], at(i, "nrm_b", 2))
            pe.wait_ge(evac(BACK, K_N4), free_at(i, BACK, K_N4))
            turn(ring(BACK, K_N4), bn).then_inc(S["bk_full"], 1)

        def up_b(i, _):
            pe.wait_ge(evac(BACK, K_N4), evac_at(i, BACK, K_N4))
            for j in range(NBLK):
                project(i, BACK, K_FC + j, w_afc[:, j * P:(j + 1) * P], bnT[:])

        def down_b(i, _):
            pe.wait_ge(S["b7_free"], at(i, "b7_free", 1))
            for j in range(NBLK):
                pe.wait_ge(S["hid_b"], at(i, "hid_b", j + 1))
                last = to_tokens(B7, bhid[:, j, :], w_apj, j)
            last.then_inc(S["b7_full"], 1)

        def x2_turn(i, _):
            pe.wait_ge(S["nrm_b"], at(i, "nrm_b", 4))
            pe.wait_ge(evac(BACK, K_X2), free_at(i, BACK, K_X2))
            turn(ring(BACK, K_X2), bn).then_inc(S["bk_full"], 1)

        def gated(i, j):
            if j == 0:
                pe.wait_ge(evac(BACK, K_X2), evac_at(i, BACK, K_X2))
            project(i, BACK, K_W + 2 * j, w_1[:, j * P:(j + 1) * P], bnT[:])
            project(i, BACK, K_W + 2 * j + 1, w_2[:, j * P:(j + 1) * P], bnT[:])

        def hidden(i, n, j, w, src, ready):
            pe.wait_ge(evac(BACK, n), free_at(i, BACK, n))
            for k in range(NBLK):
                if j == 0:
                    pe.wait_ge(evac(BACK, ready(k)), evac_at(i, BACK, ready(k)))
                last = mm(ring(BACK, n)[:], w[:, k, j * P:(j + 1) * P], src[:, k, :], start=(k == 0))
            last.then_inc(S["bk_full"], 1)

        def hidden1(i, j):
            hidden(i, K_H1 + j, j, w_h1, bhid, lambda k: K_W + 2 * k + 1)

        def hidden2(i, j):
            hidden(i, K_H2 + j, j, w_h2, hC, lambda k: K_H1 + k)

        def ffn_out(i, _):
            pe.wait_ge(S["b7_free"], at(i, "b7_free", 2))
            for j in range(NBLK):
                pe.wait_ge(evac(BACK, K_H2 + j), evac_at(i, BACK, K_H2 + j))
                last = to_tokens(B7, bhid[:, j, :], w_3, j)
            last.then_inc(S["b7_full"], 1)

        pipeline(pe, dict(in_turn=in_turn, gates=gates, val_turn=val_turn, scan=scan, m_out=m_out, n2_turn=n2_turn,
                          up=up, down=down, qkv=qkv, qk_turn=qk_turn, split32=split32, score=score, q2_turn=q2_turn, attend=attend, y_rows=y_rows,
                          y_turn=y_turn,
                          o_proj=o_proj, n4_turn=n4_turn, up_b=up_b, down_b=down_b, x2_turn=x2_turn, gated=gated,
                          hidden1=hidden1, hidden2=hidden2, ffn_out=ffn_out))

    ctx.close()



def kernel(**inputs):
    import numpy as _np
    import concourse.bacc as _bacc
    from concourse import mybir as _mybir
    from concourse.bass_utils import run_bass_kernel_spmd as _run

    A = {k.replace("L0_attn_", "").replace("L0_ffn_", ""): _np.asarray(v) for k, v in inputs.items()}
    rep = lambda v: _np.broadcast_to(v, (P,) + v.shape)
    blocks = lambda w: w.reshape(-1, P, w.shape[-1]).transpose(1, 0, 2)
    col = lambda v: v.reshape(-1, P).T
    order = _np.arange(HA).reshape(HKV, G).T.reshape(-1)
    q_w = A["q_w"].reshape(D, HA, PA)[:, order, :].reshape(D, D)
    conv = A["conv_w"].reshape(2, P, KC).transpose(1, 0, 2).reshape(P, 2 * KC)
    tens = {
        "x": A["x"].reshape(BATCH * L, D),
        "w_in": A["in_proj_w"], "w_B": A["B_proj_w"], "w_C": A["C_proj_w"], "w_out": blocks(A["out_proj_w"]),
        "w_mfc": A["m_fc_w"], "w_mpj": blocks(A["m_proj_w"]),
        "w_qkv": _np.concatenate([q_w, A["k_w"], A["v_w"]], axis=1), "w_o": A["o_w"],
        "w_afc": A["a_fc_w"], "w_apj": blocks(A["a_proj_w"]),
        "w_1": A["w1_w"].T, "w_2": A["w2_w"].T, "w_h1": blocks(A["h1_w"].T), "w_h2": blocks(A["h2_w"].T),
        "w_3": blocks(A["w3_w"].T),
        "rows": rep(_np.stack([A["resid_mix_m"][0], A["resid_mix_m"][1], A["resid_mix_a"][0], A["resid_mix_a"][1],
                               A["mamba_scale"], A["m_mlp_scale"], A["attn_scale"], A["a_mlp_scale"], A["w3_s"]])),
        "cols": _np.concatenate([conv, col(A["conv_b"]), col(_np.repeat(A["D_param"], PS)), col(A["w1_s"]),
                                 col(A["w2_s"]), col(A["h1_s"]), col(A["h2_s"]), _np.zeros((P, 12), _np.float32)], axis=1),
        "heads": rep(_np.stack([A["dt_bias"], A["A_log"], A["A_log"]])),
        "gain": rep(_np.tile(_np.concatenate([A["q_gain"][order], _np.ones(HKV, _np.float32)]), TILES)),
    }
    r, c = _np.arange(P)[:, None], _np.arange(P)[None, :]
    later = _np.where(c >= r, c - r, 0)
    tens["c_ident"] = _np.eye(P)
    tens["c_diff"] = _np.concatenate([later, c - r + P, later], axis=1)
    tens["c_causal"] = _np.concatenate([c >= r, _np.ones((P, P)), c >= r], axis=1)
    tens["c_mask"] = _np.stack([_np.where(c > r, -1e30, 0.0), _np.where(r > c, -1e30, 0.0)], 1)
    inv = 1.0 / _np.float32(10000.0) ** (_np.arange(0, PA, 2, dtype=_np.float32) / PA)
    ang = _np.outer(_np.arange(L, dtype=_np.float32), inv).reshape(2, P, PA // 2).transpose(1, 0, 2)[:, :, None, :]
    ang = _np.broadcast_to(ang, (P, 2, QK, PA // 2))
    tens["c_cos"] = _np.concatenate([_np.cos(ang), _np.cos(ang)], axis=3)
    tens["c_sin"] = _np.concatenate([_np.sin(ang), -_np.sin(ang)], axis=3)

    nc = _bacc.Bacc("TRN2", target_bir_lowering=False, num_devices=1)
    t, arrays = {}, {}
    for name, a in tens.items():
        a = _np.ascontiguousarray(a, dtype=_np.float32)
        arrays["in_" + name] = a
        t[name] = nc.dram_tensor("in_" + name, a.shape, _mybir.dt.float32, kind="ExternalInput").ap()
    out = nc.dram_tensor("out_0", (BATCH * L, D), _mybir.dt.float32, kind="ExternalOutput").ap()
    program(nc, t, out)
    r = _run(nc, [arrays], core_ids=[0])
    return r.results[0]["out_0"].reshape(BATCH, L, D)
```

```python
from contextlib import ExitStack

import numpy as np
import concourse.bass as bass
from concourse import mybir

F32, F32R, BF16, I32 = mybir.dt.float32, mybir.dt.float32r, mybir.dt.bfloat16, mybir.dt.int32
ACT = mybir.ActivationFunctionType
ALU = mybir.AluOpType
AX = mybir.AxisListType

P = 128
BATCH, L, D = 16, 256, 128
DI, HS, NS, KC = 256, 16, 64, 4
PS = DI // HS
HA, HKV, PA = 16, 4, 8
G = HA // HKV
HID = 512
PAIRS = BATCH // 2
TOK = 2 * L
TILES = TOK // P
NBLK = HID // P
UNITS = 2 * HS
TRI = L + P
QK = HA + HKV
QKV = (HA + 2 * HKV) * PA
EPS_LN = 1e-5
EPS_RMS = float(np.finfo(np.float32).eps)
EXPS = 3 * HKV

PER = dict(
    x_in=16, bn_f=1, aggr_f=4, rs_f_eps=3, rs_f=3, nrm_f=3, xm=1, ssq_f=8, conv=8, val=2, cb_full=32, masked=32,
    y_mm=32, yacc_free=3, yg=2, hid_f=4, mlp_f=1, mix=2, fr_full=30, fr_evac0=15, fr_evac1=15,
    xa=1, x_res=16, rs_b_eps=4, rs_b=4, nrm_b=4, ssq_b=8, sq=2, newton=14, rope=2, split=2, mrow=4, pv=24, pv_evac=4,
    rden=4, b7_full=3, b7_free=2, hid_b=4, bn_b=2, aggr_b=8, x1=1, bk_full=94, bk_evac0=47, bk_evac1=47,
    out_ready=1, stored=16, split_b=2, xm_hi=1,
    bn_o=1, aggr_o=4, rs_o_eps=1, rs_o=1, nrm_o=1)


def _chains():
    mixer = [("m_out", 1, 0), ("m_norm", 1, 0), ("n2_turn", 1, 0), ("up", 1, 0), ("down", 1, 0), ("norm_a", 1, 0),
             ("norm_in", 2, 0), ("norm_in2", 2, 0), ("in_turn", 2, 0), ("gates", 2, 0), ("val_turn", 2, 0)]
    mixer += [("scan", 2, u) for u in range(UNITS + 1)]
    rest = [("x2_turn", 0, 0)] + [("gated", 0, j) for j in range(NBLK)]
    rest += [("hidden1", 0, j) for j in range(NBLK)] + [("hidden2", 0, j) for j in range(NBLK)]
    rest += [("ffn_out", 0, 0), ("ffn_norm", 0, 0)]
    rest += [(name, 1, 0) for name in ("n3_turn", "qkv", "rope1", "rope2", "rope3", "qk_turn", "split32")]
    rest += [("score", 1, u) for u in range(UNITS)] + [("q2_turn", 1, 0)]
    rest += [("attend", 1, e) for e in range(EXPS)] + [("q2_turn", 1, 1)]
    rest += [("attend", 1, EXPS), ("attend", 1, EXPS + 1), ("y_rows", 1, 0)]
    rest += [("attend", 1, e) for e in range(EXPS + 2, 2 * EXPS + 1)] + [("y_rows", 1, 1)]
    rest += [(name, 1, 0) for name in ("y_turn", "o_proj", "n4_norm", "n4_turn", "up_b", "down_b", "ln_a", "ln_b")]
    return mixer, rest


MERGE = dict(
    PE=("MRMRMRMMRRRRRMMMRRMRMRRRMRRRMRMRRMRMRRMRRRRRMRRRRMRRMRRMRRMRRMRRMRRRRMRRRRRRRRRMRMRRRRRRRRRR"
        "RRMRMRRMRRRMRRRMRMRRRMRMRMRMRMMRMRMRMRRRMMM"),
    DVE=("MRRRRRRRMRRRMRMMMRMMRRRRRRMRMRRMRMRMRRRRRRRRMRMRRMRRMRRRMRMRRRRMRRRRRRRRRRMMMRRRRRRRRRRRRRMM"
        "RRRRMRMMRRRRRRMRMMRRRRMMRRMMRRMMMRRMMRMRMMM"),
    Activation=("MMMRMMRMMMRRMRMRRMRRMMRRMRRRMRRRRRMRMRMRRMRRRRMRRRRRRMRMRMRRRRRRRRRRRMRRRRMRMRRRMMRMRRRMMMRR"
        "RRRRRRRRRRMRRRMRRRMRRRMRRRMRMRRRMMMMMMRRRRR"),
    Pool=("MMMMMMMMRMMMMMMMMMMRMRRRMRRRMMMRMMMRRMRRRRRRRRRRMRRRMRMRRRMRMRRMMRMMRMRMRRRRRRRRRRRRMRRRRRRR"
        "RRMRRRRRRRRRRRRRMRRRMRRRRRRRRRRRRRRRRRRRMMR"))
LEAD = dict(PE=0, DVE=3, Activation=-4, Pool=-18)


def _body(merge, lead):
    mixer, rest = _chains()
    if lead >= 0:
        mixer = mixer[lead:] + [(name, ahead + 1, k) for name, ahead, k in mixer[:lead]]
    else:
        mixer = [(name, ahead - 1, k) for name, ahead, k in mixer[lead:]] + mixer[:lead]
    m, r = iter(mixer), iter(rest)
    return [next(m) if c == "M" else next(r) for c in merge]


BODY = {engine: _body(merge, LEAD[engine]) for engine, merge in MERGE.items()}
BODY["SP"] = [("load_x", 2, 0), ("load_res", 1, 0), ("store", 0, 0)]


def program(nc, t, out):
    ctx = ExitStack()

    def sb(name, shape, dt=F32):
        return ctx.enter_context(nc.sbuf_tensor(name, shape, dt))

    def sem(name):
        return ctx.enter_context(nc.semaphore(name))

    S = {name: sem(name) for name in PER}

    def at(i, name, c):
        return i * PER[name] + c + 1

    ident = sb("ident", [P, P])
    ident_bf = sb("ident_bf", [P, P], BF16)
    sl = sb("sl", [P, 2, TOK])
    diff, causal = sl[:, 0, 0:TRI], sl[:, 1, 0:TRI]
    sq = sb("sq", [P, TILES, QK, PA])
    mask_f = sq[:].rearrange("p t h c -> p (t h c)")[:, 0:2 * P].rearrange("p (a c) -> p a c", a=2)
    mask_bf = sb("mask_bf", [P, 2, G, P], BF16)
    cosT = sb("cosT", [P, 2, QK, PA])
    sinT = sb("sinT", [P, 2, QK, PA])
    w_in = sb("w_in", [P, 2 * DI])
    w_B_hi, w_B_lo = sb("w_B_hi", [P, HS * NS], F32R), sb("w_B_lo", [P, HS * NS], F32R)
    w_C_hi, w_C_lo = sb("w_C_hi", [P, HS * NS], F32R), sb("w_C_lo", [P, HS * NS], F32R)
    w_out = sb("w_out", [P, 2, D])
    w_mfc = sb("w_mfc", [P, HID])
    w_mpj = sb("w_mpj", [P, NBLK, D])
    w_qkv = sb("w_qkv", [P, QKV])
    w_o = sb("w_o", [P, D])
    w_afc = sb("w_afc", [P, HID])
    w_apj = sb("w_apj", [P, NBLK, D])
    w_1 = sb("w_1", [P, HID])
    w_2 = sb("w_2", [P, HID])
    w_h1 = sb("w_h1", [P, NBLK, HID])
    w_h2 = sb("w_h2", [P, NBLK, HID])
    w_3 = sb("w_3", [P, NBLK, D])
    rows = sb("rows", [P, 9, D])
    R_M0, R_M1, R_A0, R_A1, R_MS, R_MM, R_AS, R_AM, R_W3 = range(9)
    cols = sb("cols", [P, 40])
    C_CW, C_CB, C_D, C_W1, C_W2, C_H1, C_H2 = 0, 8, 10, 12, 16, 20, 24
    heads = sb("heads", [P, 3, HS])
    gain = sb("gain", [P, TILES * QK])
    LM = sb("LM", [P, HS, TRI])
    half = sb("half", [P, TILES])
    eps_ln = sb("eps_ln", [P, TILES])
    eps_rms = sb("eps_rms", [P, TILES])
    waited = sb("waited", [P, 1])
    sc = sb("sc", [P, 12, HS])

    x_in = sb("x_in", [P, TILES, D])
    stat = sb("stat", [P, TILES, 6])
    mv = sb("mv", [P, TILES, 2])
    ms = sb("ms", [P, TILES])
    rs = sb("rs", [P, TILES])
    ss_f = sb("ss_f", [P, TILES])
    junk_a = sb("junk_a", [P, TILES, D])
    xh = sb("xh", [P, TILES, D])
    xm = sb("xm", [P, TILES, D])
    nrm = sb("nrm", [P, TILES, D])
    xmT_hi = sb("xmT_hi", [P, TOK], F32R)
    xmT_lo = sb("xmT_lo", [P, TOK], F32R)
    nT = sb("nT", [P, TOK])
    vpad = sb("vpad", [P, 2, 2, L + KC - 1])
    cv = sb("cv", [P, 2, 2, L])
    val = sb("val", [P, 2, TOK])
    gate = sb("gate", [P, 2, TOK])
    xpad = sb("xpad", [P, TILES, HS, 2 * PS])
    relu = sb("relu", [P, NBLK, TOK])
    BT, CT = relu[:, 0:2, :], relu[:, 2:4, :]
    w_B, w_C = BT.rearrange("p a t -> p (a t)"), CT.rearrange("p a t -> p (a t)")
    M = sb("M", [P, 2, TRI])
    yg = val
    hid = relu
    mix = cv[:, 0, :, :].rearrange("p s (t d) -> p (s t) d", d=D)

    xa = sb("xa", [P, TILES, D])
    x_res = sb("x_res", [P, TILES, D])
    bstat = sb("bstat", [P, TILES, 6])
    bmv = sb("bmv", [P, TILES, 2])
    bms = sb("bms", [P, TILES])
    brs = sb("brs", [P, TILES])
    ss_b = sb("ss_b", [P, TILES])
    ostat = sb("ostat", [P, TILES, 6])
    omv = sb("omv", [P, TILES, 2])
    oms = sb("oms", [P, TILES])
    ors = sb("ors", [P, TILES])
    x1 = sb("x1", [P, TILES, D])
    junk_b = junk_a
    bn = sb("bn", [P, TILES, D])
    bnT = sb("bnT", [P, TOK])
    qs = sb("qs", [P, 6, TILES * QK])
    qi = sb("qi", [P, TILES * QK], I32)
    yi = sb("yi", [P, TILES * QK], I32)
    qn = sb("qn", [P, TILES, QK, PA])
    ro = sb("ro", [P, TILES, QK, PA])
    r2 = sq
    Qs = sb("Qs", [P, TILES, G, HKV, 32])
    Ks = sb("Ks", [P, TILES, HKV, 32])
    QT = sb("QT", [P, G, TOK], F32R)
    KT = sb("KT", [P, TOK], F32R)
    Qb = sb("Qb", [P, TILES, G, HKV, 32], BF16)
    Kb = sb("Kb", [P, TILES, HKV, 32], BF16)
    QTb = sb("QTb", [P, G, TOK], BF16)
    KTb = sb("KTb", [P, TOK], BF16)
    Va = sb("Va", [P, TILES, HKV, 32])
    mneg = sb("mneg", [P, TILES, HA])
    PT = sb("PT", [P, 2, 512])
    yv = sl
    rden = sb("rden", [P, 2, 2, 4 * HKV])
    ytm = qn[:].rearrange("p t h c -> p (t h c)")[:, 0:TILES * D].rearrange("p (t h c) -> p t h c", t=TILES, c=PA)
    ya = bnT
    bhid = sb("bhid", [P, NBLK, TOK])
    hC = Qs[:].rearrange("p t g j c -> p t (g j c)")
    hD = bhid
    out_sb = sb("out_sb", [P, TILES, D])

    bank = [ctx.enter_context(nc.psum_tensor(f"bank{k}", [P, 512], F32)) for k in range(8)]
    FRONT = dict(banks=(0, 1), full="fr_full", evac=("fr_evac0", "fr_evac1"))
    BACK = dict(banks=(4, 5), full="bk_full", evac=("bk_evac0", "bk_evac1"))
    CB, YACC = bank[2], bank[3]
    B6, B7 = bank[6], bank[7]
    PV = (B6, B7)
    Q4 = Qs[:].rearrange("p t g j c -> p t (g j) c")
    Qb4 = Qb[:].rearrange("p t g j c -> p t (g j) c")

    def ring(r, n):
        return bank[r["banks"][n % 2]]

    def ring_bf(r, n):
        return ring(r, n)[:].bitcast(BF16)

    def evac(r, n):
        return S[r["evac"][n % 2]]

    def free_at(i, r, n):
        return at(i, r["evac"][n % 2], n // 2)

    def evac_at(i, r, n):
        return at(i, r["evac"][n % 2], n // 2 + 1)

    def full_at(i, r, n):
        return at(i, r["full"], n + 1)

    F_XM, F_N, F_V, F_G, F_XT, F_BC, F_O, F_N2, F_FC = 0, 1, 2, 4, 6, 8, 24, 25, 26
    K_N3, K_QKV, K_QB, K_KB, K_K, K_S, K_SOFT = 0, 1, 3, 5, 6, 7, 39
    K_Y, K_N4, K_FC, K_X2, K_W, K_H1, K_H2 = 71, 72, 73, 77, 78, 86, 90

    def K_TURN(k):
        return K_SOFT + (k // 2) * (2 + EXPS) + k % 2

    def K_EXP(e):
        return K_SOFT + 2 + e if e < EXPS else K_SOFT + 4 + e if e < EXPS + 2 else K_SOFT + 6 + e

    def K_YT(s, c):
        return K_SOFT + (6 + EXPS if s == 0 else 6 + 2 * EXPS) + c

    def diag(x, k, b):
        H8 = HS // 2
        whole = x[:, k, b * H8:(b + 1) * H8, :].rearrange("p h c -> p (h c)")
        return bass.AP(whole.tensor, whole.offset, [list(whole.ap[0]), [4 * PS, H8 // 2], [3 * PS, 2], [1, PS]])

    def tri(ap):
        return ap.rearrange("p (a b) -> p a b", b=P)[:, 0:3:2, :]

    decay_w = [(heads[:], t["heads"]), (diff, t["c_diff"])]
    first_w = [(ident[:], t["c_ident"]), (rows[:, 0:2, :], t["rows"][:, 0:2, :]), (cols[:], t["cols"]), (w_in[:], t["w_in"])]
    mixer_w = [(causal, t["c_causal"]), (w_B, t["w_B"]), (w_C, t["w_C"]), (rows[:, 2:9, :], t["rows"][:, 2:9, :]),
               (w_out[:], t["w_out"]), (w_mfc[:], t["w_mfc"]), (w_mpj[:], t["w_mpj"])]
    back_w = [(w_qkv[:], t["w_qkv"]), (mask_f, t["c_mask"]), (gain[:], t["gain"]), (cosT[:], t["c_cos"]),
              (sinT[:], t["c_sin"]), (w_o[:], t["w_o"]), (w_afc[:], t["w_afc"]), (w_apj[:], t["w_apj"]), (w_1[:], t["w_1"]),
              (w_2[:], t["w_2"]), (w_h1[:], t["w_h1"]), (w_h2[:], t["w_h2"]), (w_3[:], t["w_3"])]
    decay_in, first_in, mixer_in, back_in = sem("decay_in"), sem("first_in"), sem("mixer_in"), sem("back_in")
    prep_pool, prep_act, prep, prep_dve = sem("prep_pool"), sem("prep_act"), sem("prep"), sem("prep_dve")
    xt_v = t["x"].rearrange("(n p) d -> p n d", p=P)
    ot_v = out.rearrange("(n p) d -> p n d", p=P)
    block = ctx.enter_context(nc.Block())

    def run(engine, parts, i, whole, first={}):
        for name, ahead, k in BODY[engine]:
            if name in first and i + ahead == 0 and k == 0:
                first[name]()
            if name in parts and (whole or 0 <= i + ahead < PAIRS):
                parts[name](i + ahead, k)

    def pipeline(engine, eng, parts, first={}):
        depth = max(ahead for _, ahead, _ in BODY[engine])
        for i in range(-depth, 0):
            run(engine, parts, i, False, first)
        with eng.Fori(0, PAIRS - depth) as i:
            run(engine, parts, i, True)
        for i in range(PAIRS - depth, PAIRS):
            run(engine, parts, i, False)

    @block.sync
    def _(sp):
        def load_x(i):
            sp.wait_ge(S["xm"], at(i, "xm", 0))
            sp.dma_start(x_in[:], xt_v[:, bass.ds(i * TILES, TILES), :]).then_inc(S["x_in"], 16)

        def load_res(i, _):
            sp.wait_ge(S["x1"], at(i, "x1", 0))
            sp.dma_start(x_res[:], xt_v[:, bass.ds(i * TILES, TILES), :]).then_inc(S["x_res"], 16)

        def store(i, _):
            sp.wait_ge(S["out_ready"], at(i, "out_ready", 1))
            sp.dma_start(ot_v[:, bass.ds(i * TILES, TILES), :], out_sb[:]).then_inc(S["stored"], 16)

        for name in PER:
            sp.sem_inc(S[name], 1)
        for dst, src in decay_w:
            sp.dma_start(dst, src).then_inc(decay_in, 16)
        load_x(0)
        for dst, src in first_w:
            sp.dma_start(dst, src).then_inc(first_in, 16)
        for dst, src in mixer_w:
            sp.dma_start(dst, src).then_inc(mixer_in, 16)
        for dst, src in back_w:
            sp.dma_start(dst, src).then_inc(back_in, 16)

        def load_next(i, _):
            if not (isinstance(i, int) and i == 0):
                load_x(i)

        pipeline("SP", sp, dict(load_x=load_next, load_res=load_res, store=store))
        sp.wait_ge(S["stored"], at(PAIRS, "stored", 0))

    @block.gpsimd
    def _(pool):
        g = nc.gpsimd
        g.memset(half[:], -0.5)
        g.memset(eps_ln[:], EPS_LN)
        g.memset(eps_rms[:], D * EPS_RMS)
        g.memset(vpad[:], 0.0)
        g.memset(xpad[:], 0.0).then_inc(prep_pool, 1)
        g.memset(Qs[:], 0.0)
        g.memset(Ks[:, :, :, 0:24], 0.0)
        g.memset(Ks[:, :, :, 24:26], 1.0)
        g.memset(Ks[:, :, :, 26:32], 0.0)
        g.memset(Qb[:], 0.0)
        g.memset(Kb[:], 0.0)
        g.memset(Va[:, :, :, 0:PA], 0.0)
        g.memset(Va[:, :, :, PA + 1:32], 0.0)
        g.memset(Va[:, :, :, PA:PA + 1], 1.0).then_inc(prep_pool, 1)
        pool.wait_ge(prep_pool, 2)

        def rsqrt(i, c, name, src, dst, tmp, eps, ready, ready_c, used):
            pool.wait_ge(S[ready], at(i, ready, ready_c))
            pool.wait_ge(S[used], at(i, used, c))
            g.tensor_tensor(tmp[:], src, eps[:], ALU.add).then_inc(S[name + "_eps"], 1)
            pool.wait_ge(S[name + "_eps"], at(i, name + "_eps", c + 1))
            g.tensor_tensor(dst[:], tmp[:], half[:], ALU.pow).then_inc(S[name], 1)

        def square_hidden(i, r, n0, h, done):
            for j in range(NBLK):
                pool.wait_ge(evac(r, n0 + j), evac_at(i, r, n0 + j))
                g.tensor_tensor(h[:, j, :], h[:, j, :], h[:, j, :], ALU.mult).then_inc(S[done], 1)

        def norm_in(i, _):
            rsqrt(i, 0, "rs_f", mv[:, :, 1], rs, ms, eps_ln, "aggr_f", TILES, "nrm_f")

        def norm_in2(i, _):
            rsqrt(i, 1, "rs_f", ss_f[:], rs, ms, eps_rms, "ssq_f", TILES, "nrm_f")

        def m_out(i, _):
            rsqrt(i, 2, "rs_f", ss_f[:], rs, ms, eps_rms, "ssq_f", 2 * TILES, "nrm_f")

        def up(i, _):
            square_hidden(i, FRONT, F_FC, hid, "hid_f")

        def norm_a(i, _):
            rsqrt(i, 0, "rs_b", ss_b[:], brs, bms, eps_rms, "ssq_b", TILES, "nrm_b")

        def o_proj(i, _):
            rsqrt(i, 1, "rs_b", ss_b[:], brs, bms, eps_rms, "ssq_b", 2 * TILES, "nrm_b")

        def up_b(i, _):
            square_hidden(i, BACK, K_FC, bhid, "hid_b")

        def down_b(i, _):
            rsqrt(i, 2, "rs_b", bmv[:, :, 1], brs, bms, eps_ln, "aggr_b", TILES, "nrm_b")

        def ln_a(i, _):
            rsqrt(i, 3, "rs_b", bmv[:, :, 1], brs, bms, eps_ln, "aggr_b", 2 * TILES, "nrm_b")

        def ffn_out(i, _):
            rsqrt(i, 0, "rs_o", omv[:, :, 1], ors, oms, eps_ln, "aggr_o", TILES, "nrm_o")

        pipeline("Pool", pool, dict(norm_in=norm_in, norm_in2=norm_in2, ln_a=ln_a, m_out=m_out, up=up, norm_a=norm_a, o_proj=o_proj, up_b=up_b,
                            down_b=down_b, ffn_out=ffn_out))

    @block.scalar
    def _(act):
        a = nc.scalar
        act.wait_ge(prep, 1)
        a.activation(sc[:, 1, :], sc[:, 0, :], ACT.Exp).then_inc(prep_act, 1)
        a.activation(sc[:, 2, :], sc[:, 11, :], ACT.Exp).then_inc(prep_act, 1)
        act.wait_ge(decay_in, 16 * len(decay_w))
        act.wait_ge(prep, 2)
        for h in range(HS):
            a.activation(LM[:, h, :], diff, ACT.Exp, scale=sc[:, 3, h:h + 1]).then_inc(prep_act, 1)
        act.wait_ge(prep_pool, 1)

        def before_n3():
            act.wait_ge(prep_pool, 2)
            act.wait_ge(prep, 4)

        def squares(i, c, src, dst, junk, done):
            for k in range(TILES):
                last = a.activation(junk[:, k, :], src[:, k, :], ACT.Square, accum_out=dst[:, k:k + 1])
            last.then_inc(S[done], TILES)
            act.wait_ge(S[done], at(i, done, TILES * (c + 1)))

        def copy(i, r, n, dst, src=None):
            act.wait_ge(S[r["full"]], full_at(i, r, n))
            a.activation(dst, ring(r, n)[:] if src is None else src, ACT.Copy).then_inc(evac(r, n), 1)

        def norm_in2(i, _):
            act.wait_ge(S["xm"], at(i, "xm", 1))
            squares(i, 0, xm, ss_f, junk_a, "ssq_f")

        def in_turn(i, _):
            act.wait_ge(S["fr_full"], full_at(i, FRONT, F_XM))
            a.activation(xmT_hi[:], ring(FRONT, F_XM)[:], ACT.Copy).then_inc(S["xm_hi"], 1)
            copy(i, FRONT, F_N, nT[:])

        def gates(i, _):
            for b in range(2):
                n = F_V + b
                copy(i, FRONT, n, vpad[:, b, :, KC - 1:], ring(FRONT, n)[:].rearrange("p (s l) -> p s l", s=2))
            for b in range(2):
                n = F_G + b
                act.wait_ge(S["fr_full"], full_at(i, FRONT, n))
                a.activation(gate[:, b, :], ring(FRONT, n)[:], ACT.Silu).then_inc(evac(FRONT, n), 1)
            for b in range(2):
                act.wait_ge(S["conv"], at(i, "conv", KC * (b + 1)))
                a.activation(val[:, b, :], cv[:, b, :, :].rearrange("p s l -> p (s l)"), ACT.Silu).then_inc(S["val"], 1)

        def val_turn(i, _):
            for b in range(2):
                n = F_XT + b
                act.wait_ge(S["fr_full"], full_at(i, FRONT, n))
                for k in range(TILES):
                    src = ring(FRONT, n)[:, k * P:(k + 1) * P].rearrange("p (a b c) -> p a b c", b=2, c=PS)
                    last = a.activation(diag(xpad, k, b), src, ACT.Copy)
                last.then_inc(evac(FRONT, n), 1)

        def scan(i, u):
            if u % 4 == 2 and u // 4 + 1 < HS // 2:
                project_BC(i, u // 4 + 1)
            if u == 0:
                project_BC(i, 0)

        def project_BC(i, hp):
            if hp == 0:
                act.wait_ge(S["mlp_f"], at(i, "mlp_f", 0))
            for k, dst in enumerate((BT, CT)):
                if hp >= 2:
                    act.wait_ge(S["cb_full"], at(i, "cb_full", 4 * (hp - 1)))
                copy(i, FRONT, F_BC + 2 * hp + k, dst[:, hp % 2, :])

        def m_out(i, _):
            act.wait_ge(evac(FRONT, F_O), evac_at(i, FRONT, F_O))
            squares(i, 1, xm, ss_f, junk_a, "ssq_f")

        def n2_turn(i, _):
            copy(i, FRONT, F_N2, nT[:])

        def up(i, _):
            for j in range(NBLK):
                act.wait_ge(S["fr_full"], full_at(i, FRONT, F_FC + j))
                a.activation(relu[:, j, :], ring(FRONT, F_FC + j)[:], ACT.Relu).then_inc(evac(FRONT, F_FC + j), 1)

        def norm_a(i, _):
            act.wait_ge(S["xa"], at(i, "xa", 1))
            squares(i, 0, xa, ss_b, junk_b, "ssq_b")

        def n3_turn(i, _):
            copy(i, BACK, K_N3, bnT[:])

        def qkv(i, _):
            for tp in range(2):
                n = K_QKV + tp
                act.wait_ge(S["bk_full"], full_at(i, BACK, n))
                q3 = ring(BACK, n)[:, 0:2 * QKV].rearrange("p (t c) -> p t c", t=2)
                a.activation(sq[:, 2 * tp:2 * tp + 2, :, :].rearrange("p t h c -> p t (h c)"), q3[:, :, 0:QK * PA], ACT.Square)
                vv = q3[:, :, QK * PA:].rearrange("p t (h c) -> p t h c", c=PA)
                for k in range(2):
                    last = a.activation(Va[:, 2 * tp + k, :, 0:PA], vv[:, k, :, :], ACT.Copy)
                last.then_inc(S["sq"], 1)

        def q_evac(i, n, k):
            copy(i, BACK, n, QT[:, :, k * P:(k + 1) * P], ring(BACK, n)[:].rearrange("p (g c) -> p g c", g=G))

        def qk_turn(i, _):
            for c in range(2):
                n = K_QB + c
                act.wait_ge(S["bk_full"], full_at(i, BACK, n))
                for k in range(2):
                    src = ring_bf(BACK, n)[:, k * 4 * P:(k + 1) * 4 * P].rearrange("p (g c) -> p g c", g=G)
                    last = a.activation(QTb[:, :, (2 * c + k) * P:(2 * c + k + 1) * P], src, ACT.Copy)
                last.then_inc(evac(BACK, n), 1)
            copy(i, BACK, K_KB, KTb[:], ring_bf(BACK, K_KB)[:, 0:TOK])

        def split32(i, _):
            copy(i, BACK, K_K, KT[:])

        def q2_turn(i, s):
            for k in (2 * s, 2 * s + 1):
                q_evac(i, K_TURN(k), k)

        def attend(i, e):
            if e == EXPS or e == 2 * EXPS:
                s = e // EXPS - 1
                act.wait_ge(S["pv"], at(i, "pv", e))
                if s == 1:
                    act.wait_ge(S["bk_full"], full_at(i, BACK, K_YT(0, 1)))
                else:
                    act.wait_ge(S["bk_full"], at(i, "bk_full", 0))
                for c in range(2):
                    a.activation(yv[:, c, :], PV[c][:], ACT.Copy).then_inc(S["pv_evac"], 1)
            if e == 2 * EXPS:
                return
            n = K_EXP(e)
            act.wait_ge(S["bk_full"], full_at(i, BACK, n))
            act.wait_ge(S["pv"], at(i, "pv", e - 1 if e >= 2 else 0))
            a.activation(PT[:, e % 2, :], ring(BACK, n)[:], ACT.Exp).then_inc(evac(BACK, n), 1)

        def y_turn(i, _):
            copy(i, BACK, K_Y, ya[:])

        def o_proj(i, _):
            act.wait_ge(S["b7_free"], at(i, "b7_free", 1))
            squares(i, 1, xa, ss_b, junk_b, "ssq_b")

        def n4_turn(i, _):
            copy(i, BACK, K_N4, bnT[:])

        def up_b(i, _):
            for j in range(NBLK):
                act.wait_ge(S["bk_full"], full_at(i, BACK, K_FC + j))
                a.activation(bhid[:, j, :], ring(BACK, K_FC + j)[:], ACT.Relu).then_inc(evac(BACK, K_FC + j), 1)

        def x2_turn(i, _):
            copy(i, BACK, K_X2, bnT[:])

        def gated(i, j):
            n = K_W + 2 * j
            act.wait_ge(S["bk_full"], full_at(i, BACK, n))
            if j >= 2:
                act.wait_ge(evac(BACK, n - 3), evac_at(i, BACK, n - 3))
            a.activation(sl[:, j % 2, :], ring(BACK, n)[:], ACT.Silu,
                         scale=cols[:, C_W1 + j:C_W1 + j + 1]).then_inc(evac(BACK, n), 1)

        def gelu(i, n, dst, c):
            act.wait_ge(S["bk_full"], full_at(i, BACK, n))
            a.activation(dst, ring(BACK, n)[:], ACT.Gelu, scale=cols[:, c:c + 1]).then_inc(evac(BACK, n), 1)

        def hidden1(i, j):
            gelu(i, K_H1 + j, hC[:, j, :], C_H1 + j)

        def hidden2(i, j):
            gelu(i, K_H2 + j, bhid[:, j, :], C_H2 + j)

        pipeline("Activation", act, dict(norm_in2=norm_in2, in_turn=in_turn, gates=gates, val_turn=val_turn, scan=scan, m_out=m_out,
                           n2_turn=n2_turn, up=up, norm_a=norm_a, n3_turn=n3_turn, qkv=qkv, qk_turn=qk_turn, split32=split32, q2_turn=q2_turn, attend=attend,
                           y_turn=y_turn, o_proj=o_proj, n4_turn=n4_turn, up_b=up_b, x2_turn=x2_turn, gated=gated,
                           hidden1=hidden1, hidden2=hidden2), dict(n3_turn=before_n3))

    @block.vector
    def _(dve):
        v = nc.vector
        step = [0]

        def prep_link(ins):
            step[0] += 1
            ins.then_inc(prep_dve, 1)
            dve.wait_ge(prep_dve, step[0])

        dve.wait_ge(decay_in, 16 * len(decay_w))
        prep_link(v.tensor_scalar(sc[:, 4, :], heads[:, 0, :], -1.0, None, ALU.mult))
        prep_link(v.tensor_tensor(sc[:, 0, :], heads[:, 0, :], sc[:, 4, :], ALU.min))
        v.tensor_scalar(sc[:, 11, :], heads[:, 1, :], 80.0, None, ALU.min).then_inc(prep, 1)
        dve.wait_ge(prep_act, 2)
        prep_link(v.tensor_scalar(sc[:, 4, :], sc[:, 1, :], 2.0, None, ALU.add))
        prep_link(v.reciprocal(sc[:, 5, :], sc[:, 4, :]))
        prep_link(v.tensor_tensor(sc[:, 6, :], sc[:, 1, :], sc[:, 5, :], ALU.mult))
        prep_link(v.tensor_tensor(sc[:, 7, :], sc[:, 6, :], sc[:, 6, :], ALU.mult))
        prep_link(v.tensor_scalar(sc[:, 8, :], sc[:, 7, :], 2.0 / 17, 2.0 / 15, ALU.mult, ALU.add))
        for odd in (13, 11, 9, 7, 5, 3, 1):
            prep_link(v.tensor_tensor(sc[:, 9, :], sc[:, 8, :], sc[:, 7, :], ALU.mult))
            prep_link(v.tensor_scalar(sc[:, 8, :], sc[:, 9, :], 2.0 / odd, None, ALU.add))
        prep_link(v.tensor_tensor(sc[:, 9, :], sc[:, 8, :], sc[:, 6, :], ALU.mult))
        prep_link(v.tensor_scalar(sc[:, 4, :], heads[:, 0, :], 0.0, None, ALU.max))
        prep_link(v.tensor_tensor(sc[:, 10, :], sc[:, 4, :], sc[:, 9, :], ALU.add))
        prep_link(v.tensor_tensor(sc[:, 5, :], sc[:, 10, :], sc[:, 2, :], ALU.mult))
        v.tensor_scalar(sc[:, 3, :], sc[:, 5, :], -1.0, -1e4, ALU.mult, ALU.max).then_inc(prep, 1)
        dve.wait_ge(prep_pool, 1)
        dve.wait_ge(first_in, 16 * len(first_w))
        prep_link(v.tensor_tensor(rows[:, R_M0, :], rows[:, R_M0, :], rows[:, R_M1, :], ALU.add))

        def before_gates():
            dve.wait_ge(mixer_in, 16 * len(mixer_w))
            for w, r, nk in ((w_out, R_MS, 2), (w_mpj, R_MM, NBLK)):
                for k in range(nk):
                    v.tensor_tensor(w[:, k, :], w[:, k, :], rows[:, r, :], ALU.mult)
            for w, w_hi, w_lo in ((w_B, w_B_hi, w_B_lo), (w_C, w_C_hi, w_C_lo)):
                prep_link(v.tensor_copy(w_hi[:], w))
                v.tensor_tensor(w_lo[:], w, w_hi[:].bitcast(F32), ALU.subtract)
            dve.wait_ge(prep_act, 2 + HS)
            for h in range(HS):
                last = v.scalar_tensor_tensor(LM[:, h, :], LM[:, h, :], sc[:, 10, h:h + 1], causal, ALU.mult, ALU.mult)
            last.then_inc(prep, 1)
            dve.wait_ge(prep, 3)

        def before_n3():
            dve.wait_ge(back_in, 16 * len(back_w))
            for w, r, nk in ((w_apj, R_AM, NBLK), (w_3, R_W3, NBLK)):
                for k in range(nk):
                    v.tensor_tensor(w[:, k, :], w[:, k, :], rows[:, r, :], ALU.mult)
            v.tensor_tensor(w_o[:], w_o[:], rows[:, R_AS, :], ALU.mult)
            v.tensor_scalar(gain[:].rearrange("p (t h) -> p t h", t=TILES)[:, :, 0:HA],
                            gain[:].rearrange("p (t h) -> p t h", t=TILES)[:, :, 0:HA], 1.0 / float(np.sqrt(PA)), None, ALU.mult)
            v.tensor_copy(ident_bf[:], ident[:])
            v.tensor_copy(mask_bf[:], mask_f.unsqueeze(2).to_broadcast([P, 2, G, P])).then_inc(prep, 1)
            dve.wait_ge(prep, 4)
            dve.wait_ge(prep_pool, 2)

        def token_stats(i, c, src, st, m, side):
            for k in range(TILES):
                last = v.bn_stats(st[:, k, :], src[:, k, :])
            last.then_inc(S["bn_" + side], 1)
            dve.wait_ge(S["bn_" + side], at(i, "bn_" + side, c + 1))
            v.memset(waited[:], 0.0)
            for k in range(TILES):
                last = v.bn_aggr(m[:, k, :], st[:, k, :])
            last.then_inc(S["aggr_" + side], TILES)

        def layer_norm(i, c, src, dst, m, r, name):
            dve.wait_ge(S[name], at(i, name, c))
            for k in range(TILES):
                last = v.tensor_scalar(dst[:, k, :], src[:, k, :], m[:, k, 0:1], r[:, k:k + 1], ALU.subtract, ALU.mult)
            return last

        def rms_norm(i, c, src, dst, r, name):
            dve.wait_ge(S[name], at(i, name, c))
            for k in range(TILES):
                last = v.tensor_scalar(dst[:, k, :], src[:, k, :], r[:, k:k + 1], float(np.sqrt(D)), ALU.mult, ALU.mult)
            return last

        def flat(x3):
            return x3[:].rearrange("p t d -> p (t d)")

        def by_channel(r):
            return rows[:, r, :].unsqueeze(1).to_broadcast([P, TILES, D])

        def norm_in(i, _):
            dve.wait_ge(S["x_in"], at(i, "x_in", 16))
            token_stats(i, 0, x_in, stat, mv, "f")

        def norm_in2(i, _):
            layer_norm(i, 1, x_in, xh, mv, rs, "rs_f").then_inc(S["nrm_f"], 1)
            dve.wait_ge(S["nrm_f"], at(i, "nrm_f", 1))
            v.tensor_tensor(xm[:], xh[:], by_channel(R_M0), ALU.mult).then_inc(S["xm"], 1)

        def in_turn(i, _):
            rms_norm(i, 2, xm, nrm, rs, "rs_f").then_inc(S["nrm_f"], 1)
            dve.wait_ge(S["xm_hi"], at(i, "xm_hi", 1))
            v.tensor_tensor(xmT_lo[:], ring(FRONT, F_XM)[:], xmT_hi[:].bitcast(F32), ALU.subtract).then_inc(evac(FRONT, F_XM), 1)

        def gates(i, _):
            for b in range(2):
                w = lambda j: cols[:, C_CW + b * KC + j:C_CW + b * KC + j + 1]
                dve.wait_ge(evac(FRONT, F_V + b), evac_at(i, FRONT, F_V + b))
                v.tensor_scalar(cv[:, b, :, :], vpad[:, b, :, 0:L], w(0), cols[:, C_CB + b:C_CB + b + 1],
                                ALU.mult, ALU.add).then_inc(S["conv"], 1)
                for j in range(1, KC):
                    dve.wait_ge(S["conv"], at(i, "conv", KC * b + j))
                    v.scalar_tensor_tensor(cv[:, b, :, :], vpad[:, b, :, j:j + L], w(j), cv[:, b, :, :],
                                           ALU.mult, ALU.add).then_inc(S["conv"], 1)

        def scan(i, u):
            if u < UNITS:
                dve.wait_ge(S["cb_full"], at(i, "cb_full", u + 1))
                dve.wait_ge(S["y_mm"], at(i, "y_mm", u - 1 if u >= 2 else 0))
                v.tensor_tensor(M[:, u % 2, :], CB[:, 0:TRI], LM[:, u // 2, :], ALU.mult).then_inc(S["masked"], 1)
            if u in (HS + 1, UNITS):
                b = 0 if u == HS + 1 else 1
                dve.wait_ge(S["y_mm"], at(i, "y_mm", HS * (b + 1)))
                v.scalar_tensor_tensor(yg[:, b, :], val[:, b, :], cols[:, C_D + b:C_D + b + 1], YACC[:],
                                       ALU.mult, ALU.add).then_inc(S["yacc_free"], 1)
                dve.wait_ge(S["yacc_free"], at(i, "yacc_free", b + 1))
                v.tensor_tensor(yg[:, b, :], yg[:, b, :], gate[:, b, :], ALU.mult).then_inc(S["yg"], 1)

        def m_out(i, _):
            dve.wait_ge(S["fr_full"], full_at(i, FRONT, F_O))
            v.tensor_tensor(flat(xm), flat(xm), ring(FRONT, F_O)[:], ALU.add).then_inc(evac(FRONT, F_O), 1)

        def m_norm(i, _):
            rms_norm(i, 3, xm, nrm, rs, "rs_f").then_inc(S["nrm_f"], 1)
            dve.wait_ge(S["val"], at(i, "val", 2))
            v.tensor_tensor(mix, xh[:], by_channel(R_A1), ALU.mult).then_inc(S["mix"], 1)

        def down(i, _):
            dve.wait_ge(S["mlp_f"], at(i, "mlp_f", 1))
            v.tensor_tensor(flat(xm), flat(xm), YACC[:], ALU.add).then_inc(S["yacc_free"], 1)
            dve.wait_ge(S["yacc_free"], at(i, "yacc_free", 3))
            v.tensor_tensor(xm[:], xm[:], by_channel(R_A0), ALU.mult).then_inc(S["mix"], 1)
            dve.wait_ge(S["mix"], at(i, "mix", 2))
            dve.wait_ge(S["x1"], at(i, "x1", 0))
            v.tensor_tensor(xa[:], xm[:], mix, ALU.add).then_inc(S["xa"], 1)

        def n3_turn(i, _):
            rms_norm(i, 1, xa, bn, brs, "rs_b").then_inc(S["nrm_b"], 1)

        n_link = [0]

        def rope1(i, _):
            n_link[0] = 0
            rope_links(i, 0)

        def rope2(i, _):
            rope_links(i, 1)

        def rope3(i, _):
            rope_links(i, 2)

        def rope_links(i, part):

            def link(ins):
                n_link[0] += 1
                ins.then_inc(S["newton"], 1)
                dve.wait_ge(S["newton"], at(i, "newton", n_link[0]))

            W = lambda k: qs[:, k, :]
            if part == 0:
                dve.wait_ge(S["sq"], at(i, "sq", 2))
                link(v.reduce_sum(W(5), sq[:].rearrange("p t h c -> p (t h) c"), axis=AX.X))
                link(v.tensor_scalar(W(0), W(5), 1.0 / PA, EPS_RMS, ALU.mult, ALU.add))
                link(v.tensor_scalar(qi[:], W(0).bitcast(I32), 1, None, ALU.logical_shift_right))
                link(v.tensor_scalar(yi[:], qi[:], -1.0, float(0x5F3759DF), ALU.mult, ALU.add))
                link(v.tensor_tensor(W(1), yi[:].bitcast(F32), yi[:].bitcast(F32), ALU.mult))
                link(v.scalar_tensor_tensor(W(2), W(1), -0.5, W(0), ALU.mult, ALU.mult))
                link(v.scalar_tensor_tensor(W(3), W(2), 1.5, yi[:].bitcast(F32), ALU.add, ALU.mult))
                return
            if part == 1:
                for k in (3, 4):
                    link(v.tensor_tensor(W(1), W(k), W(k), ALU.mult))
                    link(v.scalar_tensor_tensor(W(2), W(1), -0.5, W(0), ALU.mult, ALU.mult))
                    link(v.scalar_tensor_tensor(W(7 - k), W(2), 1.5, W(k), ALU.add, ALU.mult))
                link(v.tensor_tensor(W(1), W(3), gain[:], ALU.mult))
                for tp in range(2):
                    n = K_QKV + tp
                    T = slice(2 * tp * QK, 2 * (tp + 1) * QK)
                    q3 = ring(BACK, n)[:, 0:2 * QKV].rearrange("p (t h c) -> p t h c", t=2, c=PA)[:, :, 0:QK, :]
                    scale = qs[:, 1, T].rearrange("p (t h) -> p t h", t=2).unsqueeze(3).to_broadcast([P, 2, QK, PA])
                    v.tensor_tensor(qn[:, 2 * tp:2 * tp + 2, :, :], q3, scale, ALU.mult).then_inc(evac(BACK, n), 1)
                return
            dve.wait_ge(evac(BACK, K_QKV), evac_at(i, BACK, K_QKV))
            dve.wait_ge(evac(BACK, K_QKV + 1), evac_at(i, BACK, K_QKV + 1))
            H2 = PA // 2
            for s in range(2):
                T = slice(2 * s, 2 * s + 2)
                fold = lambda z: z.rearrange("p t h c -> p (t h) c")
                v.tensor_tensor(ro[:, T], qn[:, T], cosT[:], ALU.mult)
                v.tensor_tensor(fold(r2[:, T])[:, :, 0:H2], fold(qn[:, T])[:, :, H2:], fold(sinT[:])[:, :, 0:H2], ALU.mult)
                last = v.tensor_tensor(fold(r2[:, T])[:, :, H2:], fold(qn[:, T])[:, :, 0:H2], fold(sinT[:])[:, :, H2:], ALU.mult)
            last.then_inc(S["rope"], 1)
            dve.wait_ge(S["rope"], at(i, "rope", 1))
            v.tensor_tensor(ro[:], ro[:], r2[:], ALU.add).then_inc(S["rope"], 1)
            dve.wait_ge(S["rope"], at(i, "rope", 2))
            qr, kr = ro[:, :, 0:HA, :], ro[:, :, HA:QK, :]
            v.tensor_copy(Qb4[:, :, :, 0:8], qr)
            v.tensor_copy(Kb[:, :, :, 0:8], kr)
            v.tensor_copy(Qb4[:, :, :, 8:16], qr)
            v.tensor_copy(Kb[:, :, :, 16:24], kr).then_inc(S["split_b"], 1)
            dve.wait_ge(S["split_b"], at(i, "split_b", 1))
            v.tensor_tensor(Qb4[:, :, :, 16:24], qr, Qb4[:, :, :, 0:8], ALU.subtract)
            v.tensor_tensor(Kb[:, :, :, 8:16], kr, Kb[:, :, :, 0:8], ALU.subtract).then_inc(S["split_b"], 1)

        def split32(i, _):
            qr, kr = ro[:, :, 0:HA, :], ro[:, :, HA:QK, :]
            v.tensor_copy(Ks[:, :, :, 0:8].bitcast(F32R), kr)
            v.tensor_copy(Ks[:, :, :, 16:24].bitcast(F32R), kr)
            v.tensor_copy(Q4[:, :, :, 0:8].bitcast(F32R), qr)
            v.tensor_copy(Q4[:, :, :, 8:16].bitcast(F32R), qr).then_inc(S["split"], 1)
            dve.wait_ge(S["split"], at(i, "split", 1))
            v.tensor_tensor(Ks[:, :, :, 8:16], kr, Ks[:, :, :, 0:8], ALU.subtract).then_inc(S["split"], 1)
            v.tensor_tensor(Q4[:, :, :, 16:24], qr, Q4[:, :, :, 0:8], ALU.subtract)

        def score(i, u):
            s, h = u // HA, u % HA
            n = K_S + u
            hq = (h % G) * HKV + h // G
            dve.wait_ge(S["bk_full"], full_at(i, BACK, n))
            v.reduce_max(mneg[:, 2 * s, hq:hq + 1], ring(BACK, n)[:, 0:P], axis=AX.X, negate=True)
            v.reduce_max(mneg[:, 2 * s + 1, hq:hq + 1], ring(BACK, n)[:, P:TRI], axis=AX.X, negate=True).then_inc(evac(BACK, n), 1)
            if h == HA - 1:
                T = slice(2 * s, 2 * s + 2)
                dve.wait_ge(evac(BACK, n), evac_at(i, BACK, n))
                v.tensor_copy(Q4[:, T, :, 24].bitcast(F32R), mneg[:, T, :]).then_inc(S["mrow"], 1)
                dve.wait_ge(S["mrow"], at(i, "mrow", 2 * s + 1))
                v.tensor_tensor(Q4[:, T, :, 25].bitcast(F32R), mneg[:, T, :], Q4[:, T, :, 24], ALU.subtract).then_inc(S["mrow"], 1)

        def y_rows(i, s):
            for c in range(2):
                n = K_YT(s, c)
                dve.wait_ge(S["bk_full"], full_at(i, BACK, n))
                rows_ = ring(BACK, n)[:].rearrange("p (g t j c) -> p g t j c", g=2, t=2, j=HKV)
                rd = rden[:, s, c, :].rearrange("p (g t j) -> p g t j", g=2, t=2)
                for g in range(2):
                    last = v.reciprocal(rd[:, g], rows_[:, g, :, :, PA])
                last.then_inc(S["rden"], 1)
                dve.wait_ge(S["rden"], at(i, "rden", 2 * s + c + 1))
                for g in range(2):
                    last = v.tensor_tensor(ytm[:, 2 * s:2 * s + 2, 2 * c + g:HA:G, :], rows_[:, g, :, :, 0:PA],
                                           rd[:, g].unsqueeze(3).to_broadcast([P, 2, HKV, PA]), ALU.mult)
                last.then_inc(evac(BACK, n), 1)

        def o_proj(i, _):
            dve.wait_ge(S["b7_full"], at(i, "b7_full", 1))
            v.tensor_tensor(flat(xa), flat(xa), B7[:], ALU.add).then_inc(S["b7_free"], 1)

        def n4_norm(i, _):
            rms_norm(i, 2, xa, bn, brs, "rs_b").then_inc(S["nrm_b"], 1)

        def down_b(i, _):
            dve.wait_ge(S["b7_full"], at(i, "b7_full", 2))
            v.tensor_tensor(flat(xa), flat(xa), B7[:], ALU.add).then_inc(S["b7_free"], 1)
            dve.wait_ge(S["b7_free"], at(i, "b7_free", 2))
            token_stats(i, 0, xa, bstat, bmv, "b")

        def ln_a(i, _):
            layer_norm(i, 3, xa, bn, bmv, brs, "rs_b").then_inc(S["nrm_b"], 1)
            dve.wait_ge(S["nrm_b"], at(i, "nrm_b", 3))
            dve.wait_ge(S["x_res"], at(i, "x_res", 16))
            dve.wait_ge(S["out_ready"], at(i, "out_ready", 0))
            v.tensor_tensor(x1[:], bn[:], x_res[:], ALU.add).then_inc(S["x1"], 1)
            dve.wait_ge(S["x1"], at(i, "x1", 1))
            token_stats(i, 1, x1, bstat, bmv, "b")

        def ln_b(i, _):
            layer_norm(i, 4, x1, bn, bmv, brs, "rs_b").then_inc(S["nrm_b"], 1)

        def gated(i, j):
            n = K_W + 2 * j + 1
            dve.wait_ge(S["bk_full"], full_at(i, BACK, n))
            dve.wait_ge(evac(BACK, n - 1), evac_at(i, BACK, n - 1))
            v.scalar_tensor_tensor(bhid[:, j, :], ring(BACK, n)[:], cols[:, C_W2 + j:C_W2 + j + 1], sl[:, j % 2, :],
                                   ALU.mult, ALU.mult).then_inc(evac(BACK, n), 1)

        def ffn_out(i, _):
            dve.wait_ge(S["b7_full"], at(i, "b7_full", 3))
            token_stats(i, 0, B7[:].rearrange("p (t d) -> p t d", t=TILES), ostat, omv, "o")

        def ffn_norm(i, _):
            dve.wait_ge(S["stored"], at(i, "stored", 0))
            layer_norm(i, 1, B7[:].rearrange("p (t d) -> p t d", t=TILES), out_sb, omv, ors, "rs_o").then_inc(S["nrm_o"], 1)
            dve.wait_ge(S["nrm_o"], at(i, "nrm_o", 1))
            v.tensor_tensor(out_sb[:], out_sb[:], x1[:], ALU.add).then_inc(S["out_ready"], 1)

        pipeline("DVE", dve, dict(norm_in=norm_in, norm_in2=norm_in2, in_turn=in_turn, gates=gates, scan=scan, m_out=m_out,
                           m_norm=m_norm, down=down, n3_turn=n3_turn, rope1=rope1, rope2=rope2, rope3=rope3, split32=split32,
                           score=score, y_rows=y_rows, o_proj=o_proj, n4_norm=n4_norm, down_b=down_b, ln_a=ln_a,
                           ln_b=ln_b, gated=gated, ffn_out=ffn_out, ffn_norm=ffn_norm),
                 dict(gates=before_gates, n3_turn=before_n3))

    @block.tensor
    def _(pe):
        p = nc.tensor
        pe.wait_ge(prep_pool, 1)
        pe.wait_ge(first_in, 16 * len(first_w))

        def before_scan():
            pe.wait_ge(prep, 3)

        def before_m_out():
            pe.wait_ge(mixer_in, 16 * len(mixer_w))

        def before_n3():
            pe.wait_ge(back_in, 16 * len(back_w))
            pe.wait_ge(prep, 4)
            pe.wait_ge(prep_pool, 2)

        def mm(o, lhsT, rhs, start):
            return p.matmul(o, lhsT, rhs, start=start, stop=True, skip_group_check=True)

        def split_product(o, w_hi, w_lo, x_hi, x_lo):
            mm(o, w_hi, x_hi, True)
            mm(o, w_hi, x_lo, False)
            return mm(o, w_lo, x_hi, False)

        def turn(o, src):
            for k in range(TILES):
                last = p.transpose(o[:, k * P:(k + 1) * P], src[:, k, :], ident[:])
            return last

        def to_tokens(o, hidden, w, j):
            for k in range(TILES):
                last = mm(o[:, k * P:(k + 1) * P], hidden[:, k * P:(k + 1) * P], w[:, j, :], start=(j == 0 and k == 0))
            return last

        def project(i, r, n, w, src):
            pe.wait_ge(evac(r, n), free_at(i, r, n))
            mm(ring(r, n)[:], w, src, True).then_inc(S[r["full"]], 1)

        def in_turn(i, _):
            pe.wait_ge(S["xm"], at(i, "xm", 1))
            pe.wait_ge(evac(FRONT, F_XM), free_at(i, FRONT, F_XM))
            turn(ring(FRONT, F_XM), xm).then_inc(S["fr_full"], 1)
            pe.wait_ge(S["nrm_f"], at(i, "nrm_f", 2))
            pe.wait_ge(evac(FRONT, F_N), free_at(i, FRONT, F_N))
            turn(ring(FRONT, F_N), nrm).then_inc(S["fr_full"], 1)

        def gates(i, _):
            pe.wait_ge(evac(FRONT, F_N), evac_at(i, FRONT, F_N))
            for j in range(4):
                project(i, FRONT, F_V + j, w_in[:, j * P:(j + 1) * P], nT[:])

        def val_turn(i, _):
            for b in range(2):
                n = F_XT + b
                pe.wait_ge(S["val"], at(i, "val", b + 1))
                pe.wait_ge(evac(FRONT, n), free_at(i, FRONT, n))
                for k in range(TILES):
                    last = p.transpose(ring(FRONT, n)[:, k * P:(k + 1) * P], val[:, b, k * P:(k + 1) * P], ident[:])
                last.then_inc(S["fr_full"], 1)

        def project_BC(i, hp):
            blk = slice(hp * P, (hp + 1) * P)
            for n, w_hi, w_lo in ((F_BC + 2 * hp, w_B_hi, w_B_lo), (F_BC + 2 * hp + 1, w_C_hi, w_C_lo)):
                pe.wait_ge(evac(FRONT, n), free_at(i, FRONT, n))
                split_product(ring(FRONT, n)[:], w_hi[:, blk], w_lo[:, blk], xmT_hi[:], xmT_lo[:]).then_inc(S["fr_full"], 1)

        def scores(i, u):
            h, s = u // 2, u % 2
            hp, r, q0 = h // 2, (h % 2) * NS, s * L
            if u % 4 == 0:
                for n in (F_BC + 2 * hp, F_BC + 2 * hp + 1):
                    pe.wait_ge(evac(FRONT, n), evac_at(i, FRONT, n))
            pe.wait_ge(S["masked"], at(i, "masked", u))
            B_, C_ = BT[r:r + NS, hp % 2, :], CT[r:r + NS, hp % 2, :]
            mm(CB[:, 0:L], B_[:, q0:q0 + P], C_[:, q0:q0 + L], True)
            mm(CB[:, L:TRI], B_[:, q0 + P:q0 + L], C_[:, q0 + P:q0 + L], False).then_inc(S["cb_full"], 1)

        def values(i, u):
            h, s = u // 2, u % 2
            q0 = s * L
            if u % HS == 0:
                pe.wait_ge(S["yacc_free"], at(i, "yacc_free", u // HS))
            if u == 0:
                for n in (F_XT, F_XT + 1):
                    pe.wait_ge(evac(FRONT, n), evac_at(i, FRONT, n))
            pe.wait_ge(S["masked"], at(i, "masked", u + 1))
            quad = slice(32 * (h // 2 % 4), 32 * (h // 2 % 4) + 32)
            mm(YACC[quad, q0:q0 + L], xpad[:, 2 * s, h, :], M[:, u % 2, 0:L], start=(u % 4 == 0))
            mm(YACC[quad, q0 + P:q0 + L], xpad[:, 2 * s + 1, h, :], M[:, u % 2, L:TRI], False).then_inc(S["y_mm"], 1)

        def scan(i, u):
            if u == 0:
                project_BC(i, 0)
            if u % 4 == 2 and u // 4 + 1 < HS // 2:
                project_BC(i, u // 4 + 1)
            if u < UNITS:
                scores(i, u)
            if u >= 1:
                values(i, u - 1)

        def m_out(i, _):
            pe.wait_ge(evac(FRONT, F_O), free_at(i, FRONT, F_O))
            for j in range(2):
                pe.wait_ge(S["yg"], at(i, "yg", j + 1))
                last = to_tokens(ring(FRONT, F_O), yg[:, j, :], w_out, j)
            last.then_inc(S["fr_full"], 1)

        def n2_turn(i, _):
            pe.wait_ge(S["nrm_f"], at(i, "nrm_f", 3))
            pe.wait_ge(evac(FRONT, F_N2), free_at(i, FRONT, F_N2))
            turn(ring(FRONT, F_N2), nrm).then_inc(S["fr_full"], 1)

        def up(i, _):
            pe.wait_ge(evac(FRONT, F_N2), evac_at(i, FRONT, F_N2))
            for j in range(NBLK):
                project(i, FRONT, F_FC + j, w_mfc[:, j * P:(j + 1) * P], nT[:])

        def down(i, _):
            pe.wait_ge(S["yacc_free"], at(i, "yacc_free", 2))
            for j in range(NBLK):
                pe.wait_ge(S["hid_f"], at(i, "hid_f", j + 1))
                last = to_tokens(YACC, hid[:, j, :], w_mpj, j)
            last.then_inc(S["mlp_f"], 1)

        def n3_turn(i, _):
            pe.wait_ge(S["nrm_b"], at(i, "nrm_b", 1))
            pe.wait_ge(evac(BACK, K_N3), free_at(i, BACK, K_N3))
            turn(ring(BACK, K_N3), bn).then_inc(S["bk_full"], 1)

        def qkv(i, _):
            pe.wait_ge(evac(BACK, K_N3), evac_at(i, BACK, K_N3))
            for tp in range(2):
                n = K_QKV + tp
                pe.wait_ge(evac(BACK, n), free_at(i, BACK, n))
                for k in range(2):
                    T = (2 * tp + k) * P
                    last = mm(ring(BACK, n)[:, k * QKV:(k + 1) * QKV], bnT[:, T:T + P], w_qkv[:], True)
                last.then_inc(S["bk_full"], 1)

        def q_turn(i, n, k):
            pe.wait_ge(evac(BACK, n), free_at(i, BACK, n))
            for g in range(G):
                last = p.transpose(ring(BACK, n)[:, g * P:(g + 1) * P], Qs[:, k, g, :, :].rearrange("p j c -> p (j c)"), ident[:])
            last.then_inc(S["bk_full"], 1)

        def qk_turn(i, _):
            pe.wait_ge(S["split_b"], at(i, "split_b", 2))
            for c in range(2):
                n = K_QB + c
                pe.wait_ge(evac(BACK, n), free_at(i, BACK, n))
                for k in range(2):
                    for g in range(G):
                        m = (k * G + g) * P
                        last = p.transpose(ring_bf(BACK, n)[:, m:m + P],
                                           Qb[:, 2 * c + k, g, :, :].rearrange("p j c -> p (j c)"), ident_bf[:])
                last.then_inc(S["bk_full"], 1)
            pe.wait_ge(evac(BACK, K_KB), free_at(i, BACK, K_KB))
            for k in range(TILES):
                last = p.transpose(ring_bf(BACK, K_KB)[:, k * P:(k + 1) * P],
                                   Kb[:, k, :, :].rearrange("p j c -> p (j c)"), ident_bf[:])
            last.then_inc(S["bk_full"], 1)

        def split32(i, _):
            pe.wait_ge(S["split"], at(i, "split", 2))
            pe.wait_ge(evac(BACK, K_K), free_at(i, BACK, K_K))
            turn(ring(BACK, K_K), Ks[:].rearrange("p t j c -> p t (j c)")).then_inc(S["bk_full"], 1)

        def score(i, u):
            s, h = u // HA, u % HA
            n, j, g, q0 = K_S + u, h // G, h % G, s * L
            rows_ = slice(32 * j, 32 * j + 24)
            o = ring(BACK, n)
            if u == 0:
                for m in (K_QB, K_QB + 1, K_KB):
                    pe.wait_ge(evac(BACK, m), evac_at(i, BACK, m))
            pe.wait_ge(evac(BACK, n), free_at(i, BACK, n))
            mm(o[:, 0:P], QTb[rows_, g, q0:q0 + P], KTb[rows_, q0:q0 + P], True)
            mm(o[:, P:TRI], QTb[rows_, g, q0 + P:q0 + L], KTb[rows_, q0:q0 + L], False)
            mm(tri(o[:, 0:TRI]), ident_bf[:], mask_bf[:, 0, 0:2, :], False).then_inc(S["bk_full"], 1)

        def q2_turn(i, s):
            pe.wait_ge(S["mrow"], at(i, "mrow", 2 * s + 2))
            for k in (2 * s, 2 * s + 1):
                n = K_TURN(k)
                pe.wait_ge(evac(BACK, n), free_at(i, BACK, n))
                for g in range(G):
                    last = p.transpose(ring(BACK, n)[:, g * P:(g + 1) * P], Qs[:, k, g, :, :].rearrange("p j c -> p (j c)"), ident[:])
                last.then_inc(S["bk_full"], 1)

        def weights_T(i, e):
            s, j, c = e // EXPS, e % EXPS // 3, e % 3
            n, q0, rows_ = K_EXP(e), s * L, slice(32 * j, 32 * j + 26)
            o = ring(BACK, n)[:]
            if e % EXPS == 0:
                for k in (2 * s, 2 * s + 1):
                    pe.wait_ge(evac(BACK, K_TURN(k)), evac_at(i, BACK, K_TURN(k)))
            if e == 0:
                pe.wait_ge(evac(BACK, K_K), evac_at(i, BACK, K_K))
            pe.wait_ge(evac(BACK, n), free_at(i, BACK, n))
            if c < 2:
                o3 = o.rearrange("p (g q) -> p g q", g=2)
                mm(o3, KT[rows_, q0:q0 + P], QT[rows_, 2 * c:2 * c + 2, q0:q0 + L], True)
                mm(o3[:, :, 0:P], ident_bf[:], mask_bf[:, 1, 0:2, :], False).then_inc(S["bk_full"], 1)
            else:
                o3 = o.rearrange("p (g q) -> p g q", g=G)
                mm(o3, KT[rows_, q0 + P:q0 + L], QT[rows_, :, q0 + P:q0 + L], True)
                mm(o3, ident_bf[:], mask_bf[:, 1, :, :], False).then_inc(S["bk_full"], 1)

        def weighted(i, e):
            s, j, c = e // EXPS, e % EXPS // 3, e % 3
            quad = slice(32 * j, 32 * j + 32)
            if e % EXPS == 0:
                pe.wait_ge(S["pv_evac"], at(i, "pv_evac", 2 * s))
                if s == 0:
                    pe.wait_ge(S["nrm_o"], at(i, "nrm_o", 0))
            pe.wait_ge(evac(BACK, K_EXP(e)), evac_at(i, BACK, K_EXP(e)))
            w = PT[:, e % 2, :]
            if c < 2:
                last = mm(PV[c][quad, :], Va[:, 2 * s, j, :], w, True)
            else:
                for b in range(2):
                    o3 = PV[b][quad, :].rearrange("p (g q) -> p g q", g=2)[:, :, P:L]
                    last = mm(o3, Va[:, 2 * s + 1, j, :], w[:, b * L:(b + 1) * L].rearrange("p (g q) -> p g q", g=2), False)
            last.then_inc(S["pv"], 1)

        def attend(i, e):
            if e < 2 * EXPS:
                weights_T(i, e)
            if e >= 1:
                weighted(i, e - 1)

        def y_rows(i, s):
            for c in range(2):
                n = K_YT(s, c)
                pe.wait_ge(S["pv_evac"], at(i, "pv_evac", 2 * s + c + 1))
                pe.wait_ge(evac(BACK, n), free_at(i, BACK, n))
                for m in range(4):
                    last = p.transpose(ring(BACK, n)[:, m * P:(m + 1) * P], yv[:, c, m * P:(m + 1) * P], ident[:])
                last.then_inc(S["bk_full"], 1)

        def y_turn(i, _):
            for c in range(2):
                pe.wait_ge(evac(BACK, K_YT(1, c)), evac_at(i, BACK, K_YT(1, c)))
            pe.wait_ge(evac(BACK, K_Y), free_at(i, BACK, K_Y))
            turn(ring(BACK, K_Y), ytm.rearrange("p t h c -> p t (h c)")).then_inc(S["bk_full"], 1)

        def o_proj(i, _):
            pe.wait_ge(evac(BACK, K_Y), evac_at(i, BACK, K_Y))
            for k in range(TILES):
                last = mm(B7[:, k * P:(k + 1) * P], ya[:, k * P:(k + 1) * P], w_o[:], start=(k == 0))
            last.then_inc(S["b7_full"], 1)

        def n4_turn(i, _):
            pe.wait_ge(S["nrm_b"], at(i, "nrm_b", 2))
            pe.wait_ge(evac(BACK, K_N4), free_at(i, BACK, K_N4))
            turn(ring(BACK, K_N4), bn).then_inc(S["bk_full"], 1)

        def up_b(i, _):
            pe.wait_ge(evac(BACK, K_N4), evac_at(i, BACK, K_N4))
            for j in range(NBLK):
                project(i, BACK, K_FC + j, w_afc[:, j * P:(j + 1) * P], bnT[:])

        def down_b(i, _):
            pe.wait_ge(S["b7_free"], at(i, "b7_free", 1))
            for j in range(NBLK):
                pe.wait_ge(S["hid_b"], at(i, "hid_b", j + 1))
                last = to_tokens(B7, bhid[:, j, :], w_apj, j)
            last.then_inc(S["b7_full"], 1)

        def x2_turn(i, _):
            pe.wait_ge(S["nrm_b"], at(i, "nrm_b", 4))
            pe.wait_ge(evac(BACK, K_X2), free_at(i, BACK, K_X2))
            turn(ring(BACK, K_X2), bn).then_inc(S["bk_full"], 1)

        def gated(i, j):
            if j == 0:
                pe.wait_ge(evac(BACK, K_X2), evac_at(i, BACK, K_X2))
            project(i, BACK, K_W + 2 * j, w_1[:, j * P:(j + 1) * P], bnT[:])
            project(i, BACK, K_W + 2 * j + 1, w_2[:, j * P:(j + 1) * P], bnT[:])

        def hidden(i, n, j, w, src, ready):
            pe.wait_ge(evac(BACK, n), free_at(i, BACK, n))
            for k in range(NBLK):
                if j == 0:
                    pe.wait_ge(evac(BACK, ready(k)), evac_at(i, BACK, ready(k)))
                last = mm(ring(BACK, n)[:], w[:, k, j * P:(j + 1) * P], src[:, k, :], start=(k == 0))
            last.then_inc(S["bk_full"], 1)

        def hidden1(i, j):
            hidden(i, K_H1 + j, j, w_h1, bhid, lambda k: K_W + 2 * k + 1)

        def hidden2(i, j):
            hidden(i, K_H2 + j, j, w_h2, hC, lambda k: K_H1 + k)

        def ffn_out(i, _):
            pe.wait_ge(S["b7_free"], at(i, "b7_free", 2))
            for j in range(NBLK):
                pe.wait_ge(evac(BACK, K_H2 + j), evac_at(i, BACK, K_H2 + j))
                last = to_tokens(B7, bhid[:, j, :], w_3, j)
            last.then_inc(S["b7_full"], 1)

        pipeline("PE", pe, dict(in_turn=in_turn, gates=gates, val_turn=val_turn, scan=scan, m_out=m_out, n2_turn=n2_turn,
                          up=up, down=down, n3_turn=n3_turn, qkv=qkv, qk_turn=qk_turn, split32=split32, score=score, q2_turn=q2_turn, attend=attend, y_rows=y_rows,
                          y_turn=y_turn,
                          o_proj=o_proj, n4_turn=n4_turn, up_b=up_b, down_b=down_b, x2_turn=x2_turn, gated=gated,
                          hidden1=hidden1, hidden2=hidden2, ffn_out=ffn_out),
                 dict(scan=before_scan, m_out=before_m_out, n3_turn=before_n3))

    ctx.close()



def kernel(**inputs):
    import numpy as _np
    import concourse.bacc as _bacc
    from concourse import mybir as _mybir
    from concourse.bass_utils import run_bass_kernel_spmd as _run

    A = {k.replace("L0_attn_", "").replace("L0_ffn_", ""): _np.asarray(v) for k, v in inputs.items()}
    rep = lambda v: _np.broadcast_to(v, (P,) + v.shape)
    blocks = lambda w: w.reshape(-1, P, w.shape[-1]).transpose(1, 0, 2)
    col = lambda v: v.reshape(-1, P).T
    order = _np.arange(HA).reshape(HKV, G).T.reshape(-1)
    q_w = A["q_w"].reshape(D, HA, PA)[:, order, :].reshape(D, D)
    conv = A["conv_w"].reshape(2, P, KC).transpose(1, 0, 2).reshape(P, 2 * KC)
    tens = {
        "x": A["x"].reshape(BATCH * L, D),
        "w_in": A["in_proj_w"], "w_B": A["B_proj_w"], "w_C": A["C_proj_w"], "w_out": blocks(A["out_proj_w"]),
        "w_mfc": A["m_fc_w"], "w_mpj": blocks(A["m_proj_w"]),
        "w_qkv": _np.concatenate([q_w, A["k_w"], A["v_w"]], axis=1), "w_o": A["o_w"],
        "w_afc": A["a_fc_w"], "w_apj": blocks(A["a_proj_w"]),
        "w_1": A["w1_w"].T, "w_2": A["w2_w"].T, "w_h1": blocks(A["h1_w"].T), "w_h2": blocks(A["h2_w"].T),
        "w_3": blocks(A["w3_w"].T),
        "rows": rep(_np.stack([A["resid_mix_m"][0], A["resid_mix_m"][1], A["resid_mix_a"][0], A["resid_mix_a"][1],
                               A["mamba_scale"], A["m_mlp_scale"], A["attn_scale"], A["a_mlp_scale"], A["w3_s"]])),
        "cols": _np.concatenate([conv, col(A["conv_b"]), col(_np.repeat(A["D_param"], PS)), col(A["w1_s"]),
                                 col(A["w2_s"]), col(A["h1_s"]), col(A["h2_s"]), _np.zeros((P, 12), _np.float32)], axis=1),
        "heads": rep(_np.stack([A["dt_bias"], A["A_log"], A["A_log"]])),
        "gain": rep(_np.tile(_np.concatenate([A["q_gain"][order], _np.ones(HKV, _np.float32)]), TILES)),
    }
    r, c = _np.arange(P)[:, None], _np.arange(P)[None, :]
    later = _np.where(c >= r, c - r, 0)
    tens["c_ident"] = _np.eye(P)
    tens["c_diff"] = _np.concatenate([later, c - r + P, later], axis=1)
    tens["c_causal"] = _np.concatenate([c >= r, _np.ones((P, P)), c >= r], axis=1)
    tens["c_mask"] = _np.stack([_np.where(c > r, -1e30, 0.0), _np.where(r > c, -1e30, 0.0)], 1)
    inv = 1.0 / _np.float32(10000.0) ** (_np.arange(0, PA, 2, dtype=_np.float32) / PA)
    ang = _np.outer(_np.arange(L, dtype=_np.float32), inv).reshape(2, P, PA // 2).transpose(1, 0, 2)[:, :, None, :]
    ang = _np.broadcast_to(ang, (P, 2, QK, PA // 2))
    tens["c_cos"] = _np.concatenate([_np.cos(ang), _np.cos(ang)], axis=3)
    tens["c_sin"] = _np.concatenate([_np.sin(ang), -_np.sin(ang)], axis=3)

    nc = _bacc.Bacc("TRN2", target_bir_lowering=False, num_devices=1)
    t, arrays = {}, {}
    for name, a in tens.items():
        a = _np.ascontiguousarray(a, dtype=_np.float32)
        arrays["in_" + name] = a
        t[name] = nc.dram_tensor("in_" + name, a.shape, _mybir.dt.float32, kind="ExternalInput").ap()
    out = nc.dram_tensor("out_0", (BATCH * L, D), _mybir.dt.float32, kind="ExternalOutput").ap()
    program(nc, t, out)
    r = _run(nc, [arrays], core_ids=[0])
    return r.results[0]["out_0"].reshape(BATCH, L, D)
```
